# Optimizing a Trainium2 kernel written in Bass

```python
import numpy as np
import jax
import jax.numpy as jnp

def _softmax(x, axis=-1):
    return jax.nn.softmax(x, axis=axis)

def _gelu(x):
    return jax.nn.gelu(x, approximate=True)

def _silu(x):
    return jax.nn.silu(x)

def _sigmoid(x):
    return jax.nn.sigmoid(x)

def _layernorm(x, axis=-1, eps=1e-05):
    m = jnp.mean(x, axis=axis, keepdims=True)
    v = jnp.var(x, axis=axis, keepdims=True)
    return (x - m) / jnp.sqrt(v + eps)

def _scatter_add(tgt, idx, src, axis=0):
    return tgt.at[idx].add(src)

def _segment_sum(src, seg, n):
    return jax.ops.segment_sum(src, seg, n)
kernel_name = 'mk_adj_preln_d4_adj_r2_816b52'

def setup_inputs(seed: int=0):
    np.random.seed(seed)
    _w = jnp.asarray

    def _rec_inputs():
        import jax
        import jax.numpy as jnp
        _gk = jax.random.key(seed)
        x = -0.0003929 + 0.9999 * jax.random.normal(jax.random.fold_in(_gk, 1), (128, 64, 128), jnp.float32)
        _a = jax.random.bernoulli(jax.random.fold_in(_gk, 2), 0.0625, (64, 64))
        _a = jnp.logical_or(_a, jnp.swapaxes(_a, -1, -2))
        _a = jnp.logical_or(_a, jnp.eye(64, dtype=bool))
        _af = _a.astype(jnp.float32)
        _af = _af * jax.random.uniform(jax.random.fold_in(_gk, 3), (64, 64), jnp.float32, 0.05, 1)
        adj = _af
        return (x, adj)
    x, adj = _rec_inputs()

    def _L0_gnn_setup():
        import jax, jax.numpy as jnp
        import numpy as np
        EPS = 1e-05

        def _batchnorm(x, gamma, beta):
            mu = jnp.mean(x, axis=0)
            var = jnp.var(x, axis=0)
            return (x - mu) * jax.lax.rsqrt(var + EPS) * gamma + beta
        key = jax.random.key(seed)
        ks = jax.random.split(key, 4)
        b, n, d, h, o = (32, 1024, 128, 256, 128)
        features = jax.random.normal(ks[0], (b, n, d), dtype=jnp.float32)
        A = jax.random.uniform(ks[1], (n, n), dtype=jnp.float32)
        lim1 = float(np.sqrt(6.0 / (d + h)))
        W1 = jax.random.uniform(ks[2], (h, d), minval=-lim1, maxval=lim1, dtype=jnp.float32)
        b1 = jnp.zeros((h,), jnp.float32)
        lim2 = float(np.sqrt(6.0 / (h + o)))
        W2 = jax.random.uniform(ks[3], (o, h), minval=-lim2, maxval=lim2, dtype=jnp.float32)
        b2 = jnp.zeros((o,), jnp.float32)
        g1 = jnp.ones((h,), jnp.float32)
        be1 = jnp.zeros((h,), jnp.float32)
        g2 = jnp.ones((o,), jnp.float32)
        be2 = jnp.zeros((o,), jnp.float32)
        return {'features': features, 'A': A, 'W1': W1, 'b1': b1, 'g1': g1, 'be1': be1, 'W2': W2, 'b2': b2, 'g2': g2, 'be2': be2}
    _L0_gnn_all = _L0_gnn_setup()
    _L0_gnn_in = {k: v for k, v in _L0_gnn_all.items() if k in ('W1', 'b1', 'g1', 'be1', 'W2', 'b2', 'g2', 'be2')}
    del _L0_gnn_all

    def _L1_gnn_setup():
        import jax, jax.numpy as jnp
        import numpy as np
        B, T, D, H = (64, 1024, 128, 128)
        MAX_SKIP = 4

        def _lstm_last(Wih, Whh, bih, bhh, xs):
            N, _, Hd = xs.shape
            bias = bih + bhh

            def step(carry, x_t):
                h, c = carry
                g = x_t @ Wih.T + h @ Whh.T + bias
                i, f, gg, o = jnp.split(g, 4, axis=-1)
                c = jax.nn.sigmoid(f) * c + jax.nn.sigmoid(i) * jnp.tanh(gg)
                h = jax.nn.sigmoid(o) * jnp.tanh(c)
                return ((h, c), None)
            init = (jnp.zeros((N, Hd), xs.dtype), jnp.zeros((N, Hd), xs.dtype))
            (h_last, _), _ = jax.lax.scan(step, init, jnp.swapaxes(xs, 0, 1))
            return h_last
        key = jax.random.key(seed)
        ks = jax.random.split(key, 8)
        s = 0.05
        x = jax.random.normal(ks[0], (B, T, D), jnp.float32)
        adj = jax.random.uniform(ks[1], (T, T), jnp.float32) / T
        Wg0 = jax.random.normal(ks[2], (D, H), jnp.float32) * s
        bg0 = jnp.zeros((H,), jnp.float32)
        Wg1 = jax.random.normal(ks[3], (H, H), jnp.float32) * s
        bg1 = jnp.zeros((H,), jnp.float32)
        Wih = jax.random.normal(ks[4], (MAX_SKIP, 4 * H, H), jnp.float32) * s
        Whh = jax.random.normal(ks[5], (MAX_SKIP, 4 * H, H), jnp.float32) * s
        bih = jax.random.normal(ks[6], (MAX_SKIP, 4 * H), jnp.float32) * s
        bhh = jax.random.normal(ks[7], (MAX_SKIP, 4 * H), jnp.float32) * s
        return dict(x=x, adj=adj, Wg0=Wg0, bg0=bg0, Wg1=Wg1, bg1=bg1, Wih=Wih, Whh=Whh, bih=bih, bhh=bhh)
    _L1_gnn_all = _L1_gnn_setup()
    _L1_gnn_in = {k: v for k, v in _L1_gnn_all.items() if k in ('Wg0', 'bg0', 'Wg1', 'bg1', 'Wih', 'Whh', 'bih', 'bhh')}
    del _L1_gnn_all

    def _L2_gnn_setup():
        import jax, jax.numpy as jnp
        import numpy as np
        B, N, D_IN, HID, D_OUT = (64, 512, 128, 128, 128)
        key = jax.random.key(seed)
        kf, ka, kw1, kw2 = jax.random.split(key, 4)
        features = jax.random.normal(kf, (B, N, D_IN), dtype=jnp.float32)
        A = jax.random.uniform(ka, (N, N), dtype=jnp.float32)
        A = 0.5 * (A + A.T)
        lim1 = float(np.sqrt(6.0 / (D_IN + HID)))
        lim2 = float(np.sqrt(6.0 / (HID + D_OUT)))
        W1 = jax.random.uniform(kw1, (D_IN, HID), minval=-lim1, maxval=lim1, dtype=jnp.float32)
        b1 = jnp.zeros((HID,), jnp.float32)
        W2 = jax.random.uniform(kw2, (HID, D_OUT), minval=-lim2, maxval=lim2, dtype=jnp.float32)
        b2 = jnp.zeros((D_OUT,), jnp.float32)
        return {'features': features, 'A': A, 'W1': W1, 'b1': b1, 'W2': W2, 'b2': b2}
    _L2_gnn_all = _L2_gnn_setup()
    _L2_gnn_in = {k: v for k, v in _L2_gnn_all.items() if k in ('W1', 'b1', 'W2', 'b2')}
    del _L2_gnn_all

    def _L3_gnn_setup():
        import jax, jax.numpy as jnp
        import numpy as np
        N = 2048
        NFEAT, NHID, NCLASS = (128, 256, 128)
        B = 4

        def _slconv(x, adj, S, W):
            support = jnp.einsum('bnf,fh->bnh', x, W)
            weighting = adj * S
            return jnp.einsum('nm,bmh->bnh', weighting, support)
        key = jax.random.key(seed)
        ks = jax.random.split(key, 6)
        x = jax.random.normal(ks[0], (B, N, NFEAT), dtype=jnp.float32)
        adj = jax.random.uniform(ks[1], (N, N), dtype=jnp.float32)
        S = jnp.ones((N, N), dtype=jnp.float32)
        W1 = jax.random.normal(ks[2], (NFEAT, NHID), dtype=jnp.float32) / np.sqrt(NFEAT)
        W2 = jax.random.normal(ks[3], (NHID, 2 * NHID), dtype=jnp.float32) / np.sqrt(NHID)
        W3 = jax.random.normal(ks[4], (2 * NHID, NCLASS), dtype=jnp.float32) / np.sqrt(2 * NHID)
        return {'x': x, 'adj': adj, 'S': S, 'W1': W1, 'W2': W2, 'W3': W3}
    _L3_gnn_all = _L3_gnn_setup()
    _L3_gnn_in = {k: v for k, v in _L3_gnn_all.items() if k in ('W1', 'W2', 'W3')}
    del _L3_gnn_all
    return {'x': x, 'adj': adj, 'L0_gnn_W1': _L0_gnn_in['W1'], 'L0_gnn_b1': _L0_gnn_in['b1'], 'L0_gnn_g1': _L0_gnn_in['g1'], 'L0_gnn_be1': _L0_gnn_in['be1'], 'L0_gnn_W2': _L0_gnn_in['W2'], 'L0_gnn_b2': _L0_gnn_in['b2'], 'L0_gnn_g2': _L0_gnn_in['g2'], 'L0_gnn_be2': _L0_gnn_in['be2'], 'L1_gnn_Wg0': _L1_gnn_in['Wg0'], 'L1_gnn_bg0': _L1_gnn_in['bg0'], 'L1_gnn_Wg1': _L1_gnn_in['Wg1'], 'L1_gnn_bg1': _L1_gnn_in['bg1'], 'L1_gnn_Wih': _L1_gnn_in['Wih'], 'L1_gnn_Whh': _L1_gnn_in['Whh'], 'L1_gnn_bih': _L1_gnn_in['bih'], 'L1_gnn_bhh': _L1_gnn_in['bhh'], 'L2_gnn_W1': _L2_gnn_in['W1'], 'L2_gnn_b1': _L2_gnn_in['b1'], 'L2_gnn_W2': _L2_gnn_in['W2'], 'L2_gnn_b2': _L2_gnn_in['b2'], 'L3_gnn_W1': _L3_gnn_in['W1'], 'L3_gnn_W2': _L3_gnn_in['W2'], 'L3_gnn_W3': _L3_gnn_in['W3']}

def reference(x, adj, L0_gnn_W1, L0_gnn_b1, L0_gnn_g1, L0_gnn_be1, L0_gnn_W2, L0_gnn_b2, L0_gnn_g2, L0_gnn_be2, L1_gnn_Wg0, L1_gnn_bg0, L1_gnn_Wg1, L1_gnn_bg1, L1_gnn_Wih, L1_gnn_Whh, L1_gnn_bih, L1_gnn_bhh, L2_gnn_W1, L2_gnn_b1, L2_gnn_W2, L2_gnn_b2, L3_gnn_W1, L3_gnn_W2, L3_gnn_W3):
    import jax
    import jax.numpy as jnp

    def _L0_gnn_ref(features, A, W1, b1, g1, be1, W2, b2, g2, be2):
        import jax, jax.numpy as jnp
        import numpy as np
        EPS = 1e-05

        def _batchnorm(x, gamma, beta):
            mu = jnp.mean(x, axis=0)
            var = jnp.var(x, axis=0)
            return (x - mu) * jax.lax.rsqrt(var + EPS) * gamma + beta
        b, n, d = features.shape
        A_norm = A + jnp.eye(n, dtype=A.dtype)
        deg = jnp.sum(A_norm, axis=0) + jnp.sum(A_norm, axis=1) - jnp.diagonal(A_norm)
        dinv = jax.lax.rsqrt(deg)
        A_hat = A_norm * dinv[:, None] * dinv[None, :]
        agg = jnp.einsum('nm,bmd->bnd', A_hat, features)
        x = agg.reshape(-1, d)
        h = jax.nn.relu(_batchnorm(x @ W1.T + b1, g1, be1))
        out = h @ W2.T + b2
        out = _batchnorm(out, g2, be2)
        return out.reshape(b, n, -1)

    def _L1_gnn_ref(x, adj, Wg0, bg0, Wg1, bg1, Wih, Whh, bih, bhh):
        import jax, jax.numpy as jnp
        import numpy as np
        B, T, D, H = (64, 1024, 128, 128)
        MAX_SKIP = 4

        def _lstm_last(Wih, Whh, bih, bhh, xs):
            N, _, Hd = xs.shape
            bias = bih + bhh

            def step(carry, x_t):
                h, c = carry
                g = x_t @ Wih.T + h @ Whh.T + bias
                i, f, gg, o = jnp.split(g, 4, axis=-1)
                c = jax.nn.sigmoid(f) * c + jax.nn.sigmoid(i) * jnp.tanh(gg)
                h = jax.nn.sigmoid(o) * jnp.tanh(c)
                return ((h, c), None)
            init = (jnp.zeros((N, Hd), xs.dtype), jnp.zeros((N, Hd), xs.dtype))
            (h_last, _), _ = jax.lax.scan(step, init, jnp.swapaxes(xs, 0, 1))
            return h_last
        h = jax.nn.relu(jnp.einsum('ts,bsh->bth', adj, x @ Wg0 + bg0))
        h = jax.nn.relu(jnp.einsum('ts,bsh->bth', adj, h @ Wg1 + bg1))
        Bv, Tv, Hd = h.shape
        for p in range(1, MAX_SKIP + 1):
            nw = Tv // p
            wins = h[:, :nw * p, :].reshape(Bv * nw, p, Hd)
            last = _lstm_last(Wih[p - 1], Whh[p - 1], bih[p - 1], bhh[p - 1], wins)
            idx = jnp.arange(nw) * p + (p - 1)
            h = h.at[:, idx, :].set(last.reshape(Bv, nw, Hd))
        return h

    def _L2_gnn_ref(features, A, W1, b1, W2, b2):
        import jax, jax.numpy as jnp
        import numpy as np
        B, N, D_IN, HID, D_OUT = (64, 512, 128, 128, 128)
        deg = jnp.sum(A, axis=0) + jnp.sum(A, axis=1) - jnp.diagonal(A)
        d_inv_sqrt = jnp.where(deg > 0, jax.lax.rsqrt(deg), 0.0)
        L = jnp.diag(deg) - A
        L_norm = d_inv_sqrt[:, None] * L * d_inv_sqrt[None, :]
        _, U = jnp.linalg.eigh(L_norm)
        agg = jnp.einsum('mn,bnd->bmd', U.T, features)
        h = jax.nn.relu(agg @ W1 + b1)
        out = h @ W2 + b2
        return jnp.einsum('nm,bmd->bnd', U, out)

    def _L3_gnn_ref(x, adj, S, W1, W2, W3):
        import jax, jax.numpy as jnp
        import numpy as np
        N = 2048
        NFEAT, NHID, NCLASS = (128, 256, 128)
        B = 4

        def _slconv(x, adj, S, W):
            support = jnp.einsum('bnf,fh->bnh', x, W)
            weighting = adj * S
            return jnp.einsum('nm,bmh->bnh', weighting, support)
        h = jax.nn.relu(_slconv(x, adj, S, W1))
        h = jax.nn.relu(_slconv(h, adj, S, W2))
        return _slconv(h, adj, S, W3)
    h = jnp.maximum(_layernorm(x, axis=-1), 0.0)
    x = x + _L0_gnn_ref(h, adj, L0_gnn_W1, L0_gnn_b1, L0_gnn_g1, L0_gnn_be1, L0_gnn_W2, L0_gnn_b2, L0_gnn_g2, L0_gnn_be2)
    h = jnp.maximum(_layernorm(x, axis=-1), 0.0)
    x = x + _L1_gnn_ref(h, adj, L1_gnn_Wg0, L1_gnn_bg0, L1_gnn_Wg1, L1_gnn_bg1, L1_gnn_Wih, L1_gnn_Whh, L1_gnn_bih, L1_gnn_bhh)
    h = jnp.maximum(_layernorm(x, axis=-1), 0.0)
    x = x + _L2_gnn_ref(h, adj, L2_gnn_W1, L2_gnn_b1, L2_gnn_W2, L2_gnn_b2)
    h = jnp.maximum(_layernorm(x, axis=-1), 0.0)
    x = x + _L3_gnn_ref(h, adj, adj, L3_gnn_W1, L3_gnn_W2, L3_gnn_W3)
    return x

_drawn_inputs = setup_inputs


def setup_inputs(seed=0):
    import zlib

    import numpy as np

    out = dict(_drawn_inputs(seed))
    spreads = {'L0_gnn_b1': (0.0, 0.8),
     'L0_gnn_g1': (1.0, 0.2),
     'L0_gnn_be1': (0.0, 0.347),
     'L0_gnn_b2': (0.0, 0.8),
     'L0_gnn_g2': (1.0, 0.2),
     'L0_gnn_be2': (0.0, 0.1),
     'L1_gnn_bg0': (0.0, 0.542),
     'L1_gnn_bg1': (0.0, 0.729),
     'L2_gnn_b1': (0.0, 0.555),
     'L2_gnn_b2': (0.0, 0.4)}
    factors = {'L1_gnn_Whh': 8.0, 'L1_gnn_bih': 7.466, 'L1_gnn_bhh': 8.0}
    for name, (base, spread) in spreads.items():
        noise = np.random.default_rng([zlib.crc32(name.encode()), seed]).standard_normal(out[name].shape)
        drawn = base * np.exp(spread * noise) if base else spread * noise
        out[name] = jnp.asarray(drawn.astype(out[name].dtype))
    for name, factor in factors.items():
        out[name] = (out[name] * factor).astype(out[name].dtype)
    return out
```

```python
from contextlib import ExitStack

import numpy as np

import concourse.bass as bass
from concourse import mybir

F32 = mybir.dt.float32
ALU = mybir.AluOpType
ACT = mybir.ActivationFunctionType
AX = mybir.AxisListType.X

P = 128
GRAPHS, NODES, D = 128, 64, 128
TOKENS = GRAPHS * NODES
TILES = TOKENS // P
CH = 512
TPC = CH // P
NK = 4
SG = NK * CH
ITER = TOKENS // SG
NCHUNK = TOKENS // CH
EPS = 1e-5
MAX_SKIP = 4
SET = SG // 2
SGR = SET // NODES
TINY = 1e-30
HALF = NODES // 2
M = 32
ROUNDS = 3
REFLECTIONS = NODES - 2


def constants():
    p = np.arange(P)[:, None]
    c = np.arange(P)[None, :]
    n = np.arange(NODES)[None, :]
    t = {}
    t["ident"] = (p == c)
    t["blocks"] = (p // NODES == c // NODES)
    t["fold"] = (p % NODES == c % NODES)
    t["ones"] = np.ones((P, P))
    t["step"] = np.broadcast_to(c >= NODES, (P, P))
    t["delta"] = np.broadcast_to(c == NODES, (P, P))
    t["below"] = (p > n) & (p < NODES)
    t["next"] = (p == n + 1)
    t["sub"] = (p == n + 1)
    t["grid"] = np.arange(M)[None, :] + 1 + M * (p // NODES)
    t["lane"] = p % NODES
    t["minus_half"] = np.full((P, 4), -0.5)
    t["half"] = np.full((P, 1), 0.5)
    return {k: np.asarray(v, np.float32) for k, v in t.items()}


CONST_W = {k: v.shape[1] for k, v in constants().items()}
WEIGHT_W = {
    "w1T": 256, "w2T": 256, "wg0": 128, "wg1": 128, "wihT": 4 * 512, "whhT": 4 * 512, "l2w1": 128, "l2w2": 128,
    "l3w1": 256, "l3w2": 1024, "l3w3": 512,
    "b1": 2, "g1": 2, "be1": 2, "b2": 1, "g2": 1, "be2": 1, "bg1": 1, "bih": 16, "bhh": 16, "l2b1": 1,
    "bg0row": 128, "l2b2row": 128,
}


def offsets(widths):
    at, out = 0, {}
    for k, w in widths.items():
        out[k] = (at, at + w)
        at += w
    return out, at


class Steps:

    def __init__(self, before, names):
        self.before, self.names = before, names

    def at(self, i, name):
        return i * len(self.names) + (self.before + self.names.index(name) + 1)

    def start(self, i):
        return i * len(self.names) + self.before

    @property
    def end(self):
        return self.before + ITER * len(self.names)


BEGUN = 1

LN = ["stats", "aggr", "shift"]
LNP = ["var", "rstd"]
A_PE = Steps(BEGUN, ["agg", "w1"])
A_ACT = Steps(BEGUN, ["norm", "aggT", "y_lo"])
A_DVE = Steps(BEGUN, LN + ["y_hi", "bn_stats"])
B_PE = Steps(A_PE.end, ["w2"])
B_ACT = Steps(A_ACT.end, ["bn_relu"])
B_DVE = Steps(A_DVE.end, ["y", "bn_stats"])
C_PE = Steps(B_PE.end, ["turn", "agg", "g0", "agg2", "g1", "turn_h"])
C_ACT = Steps(B_ACT.end, ["bn", "norm", "aggT", "relu0", "aggT2", "h"])
C_DVE = Steps(B_DVE.end, ["add"] + LN + ["bias0", "bias1", "add_h"])
D_PE = Steps(C_PE.end, ["agg", "w1", "w2", "back", "mix1", "s1", "mix2", "s2a", "s2b", "s3", "mix3"])
D_ACT = Steps(C_ACT.end, ["norm", "aggT", "hid", "norm3", "mix1T", "relu1", "mix2T", "relu2a", "relu2b", "s3"])
D_DVE = Steps(C_DVE.end, LN + ["o", "add"] + [s + "3" for s in LN] + ["add3"])

A_POOL = Steps(BEGUN, LNP)
C_POOL = Steps(A_POOL.end, LNP)
D_POOL = Steps(C_POOL.end, LNP + [s + "3" for s in LNP])

LSTM = [(1, 0, 0), (1, 0, 1)] + [(p, s, 0) for p in range(2, MAX_SKIP + 1) for s in range(p)]
GATE = {"i": 0, "f": 1, "g": 2, "o": 3}


def gates(s):
    return "igo" if s == 0 else "igfo"


def lstm_names():
    pe, act, dve = [], [], []
    for r, (p, s, _) in enumerate(LSTM):
        pe += [f"{g}{r}" for g in gates(s)]
        act += [f"{g}{r}" for g in gates(s)] + [f"tanh{r}"]
        dve += [f"ig{r}"] + ([f"fc{r}"] if s else []) + ([f"c{r}"] if s else []) + [f"h{r}"]
    return Steps(BEGUN, pe), Steps(BEGUN, act), Steps(BEGUN, dve)


R_PE, R_ACT, R_DVE = lstm_names()


def build(nc, x_in, cst_in, w_in, adj_in, out):
    ctx = ExitStack()
    with ctx:
        def sb(name, shape):
            return ctx.enter_context(nc.sbuf_tensor(name, shape, F32))

        def sem(name):
            return ctx.enter_context(nc.semaphore(name))

        def sems(name, n):
            return [sem(f"{name}{k}") for k in range(n)]

        coff, cw = offsets(CONST_W)
        woff, ww = offsets(WEIGHT_W)
        cst = sb("cst", [P, cw])
        wts = sb("wts", [P, ww])

        def C(name):
            return cst[:, coff[name][0]:coff[name][1]]

        def W(name):
            return wts[:, woff[name][0]:woff[name][1]]

        X = sb("X", [P, TILES * D])
        BIG = sb("BIG", [P, 2 * TOKENS])
        Y1 = BIG[:, :].rearrange("p (c t) -> p c t", c=2)
        Y2 = Y1[:, 0, :]
        PS = ctx.enter_context(nc.psum_tensor("PS", [P, 8, 512], F32))

        def bank(k):
            return PS[:, 2 * k, :]

        def banks(k):
            return PS[:, 2 * k:2 * k + 2, :]

        AA = sb("AA", [P, NODES])
        BDA = sb("BDA", [P, P])
        BDAT = sb("BDAT", [P, P])
        BDHT = sb("BDHT", [P, P])
        BDST = sb("BDST", [P, P])
        BDU = sb("BDU", [P, P])
        BDUT = sb("BDUT", [P, P])
        RB0 = sb("RB0", [P, P])
        RB1 = sb("RB1", [P, P])
        lbias = sb("lbias", [P, 16])
        col = sb("col", [P, 16])
        tmp = sb("tmp", [P, P])
        tmp2 = sb("tmp2", [P, P])

        LS = sb("LS", [NODES, NODES])
        S = sb("S", [P, NODES])
        xcol = sb("xcol", [P, 1])
        vcol = sb("vcol", [P, 1])
        wcol = sb("wcol", [P, 1])
        xrow = sb("xrow", [P, NODES])
        vrow = sb("vrow", [P, NODES])
        wrow = sb("wrow", [P, NODES])
        rest = sb("rest", [P, NODES])
        junk = sb("junk", [P, NODES])
        sc = sb("sc", [P, 40])
        Trow = sb("Trow", [P, 6, NODES])
        Qh = sb("Qh", [P, NODES, M])
        xg = sb("xg", [P, M])
        rq = sb("rq", [P, M])
        cnt = sb("cnt", [P, M])
        Fq = sb("Fq", [P, 8, NODES])
        EV = sb("EV", [NODES, 12, P])

        stats = sb("stats", [P, NK, TPC, 6])
        mv = sb("mv", [P, NK, TPC, 2])
        rstd = sb("rstd", [P, NK, TPC])
        shift = sb("shift", [P, NK, TPC])
        T0 = sb("T0", [P, NK, CH])
        T1 = sb("T1", [P, NK, 2 * CH])
        ST1 = sb("ST1", [P, 2, NCHUNK, 6])
        ST2 = sb("ST2", [P, NCHUNK, 6])
        bn = sb("bn", [P, 16])
        LAT = BIG[:, TOKENS:2 * TOKENS]
        LB = LAT[:, 0:2 * 4 * 512].rearrange("p (s b n) -> p s b n", s=2, b=4)
        LX = LAT[:, 4096:4096 + 2 * 512].rearrange("p (s n) -> p s n", s=2)
        H = LAT[:, 5120:5120 + SG]
        R1 = BIG[:, 0:4096].rearrange("p (k n) -> p k n", k=NK)
        A2 = BIG[:, 4096:8192].rearrange("p (k n) -> p k n", k=NK)
        R2 = BIG[:, 8192:16384].rearrange("p (k n) -> p k n", k=NK)

        ld_cst, ld_w, ld_adj, ld_x, st_out = sem("ld_cst"), sem("ld_w"), sem("ld_adj"), sem("ld_x"), sem("st_out")
        prep_dve, prep_pe = sem("prep_dve"), sem("prep_pe")
        hh_x, hh_row, hh_v, hh_av = sem("hh_x"), sem("hh_row"), sem("hh_v"), sem("hh_av")
        hh_ops, grid_ops, twist_ops = sem("hh_ops"), sem("grid_ops"), sem("twist_ops")
        grid_cnt, grid_sum = sem("grid_cnt"), sem("grid_sum")
        bn1_ready, bn2_ready = sem("bn1_ready"), sem("bn2_ready")
        bn_ops = sem("bn_ops")
        pe_done, act_done, dve_done = sems("pe_done", NK), sems("act_done", NK), sems("dve_done", NK)
        pool_done = sems("pool_done", NK)
        degree, degree_root, norm2, norm_root, hh_norm2, hh_norm = (
            sem(n) for n in ("degree", "degree_root", "norm2", "norm_root", "hh_norm2", "hh_norm"))
        passed = sem("passed")
        bn_var, bn_root = sem("bn_var"), sem("bn_root")
        pe_set, act_set, dve_set = sems("pe_set", 2), sems("act_set", 2), sems("dve_set", 2)

        block = ctx.enter_context(nc.Block())

        def chunk_cols(i, k, n=CH):
            return bass.ds(i * (NK * n) + k * n, n)

        def wT(name, p, g):
            a = woff[name][0] + (p - 1) * 512 + GATE[g] * P
            return wts[:, a:a + P]

        def lstm_in(buf, q, p, s, part):
            if p == 1:
                return buf[:, q * SET + part * 512:q * SET + (part + 1) * 512], 512
            nw = NODES // p
            v = buf[:, q * SET:(q + 1) * SET].rearrange("p (b n) -> p b n", n=NODES)
            return v[:, :, s:s + p * (nw - 1) + 1:p], SGR * nw

        def alone(eng):
            eng.sem_inc(passed, 1)

        def begin(eng, *groups):
            for group in groups:
                for one in group:
                    eng.sem_inc(one, BEGUN)

        @block.sync
        def _(sp):
            sp.dma_start(AA[0:NODES, :], adj_in).then_inc(ld_adj, 16)
            sp.dma_start(AA[NODES:P, :], adj_in).then_inc(ld_adj, 16)
            sp.dma_start(cst[:, :], cst_in).then_inc(ld_cst, 16)
            sp.dma_start(X[:, :], x_in).then_inc(ld_x, 16)
            sp.dma_start(wts[:, :], w_in).then_inc(ld_w, 16)
            with sp.Fori(0, ITER) as i:
                for k in range(NK):
                    sp.wait_ge(dve_done[k], D_DVE.at(i, "add3"))
                    sp.dma_start(out[:, chunk_cols(i, k)], X[:, chunk_cols(i, k)]).then_inc(st_out, 16)
            sp.wait_ge(st_out, 16 * NCHUNK)

        @block.tensor
        def _(pe):
            begin(pe, pe_done, pe_set)

            def mm(o, l, r, start=True, stop=True):
                return nc.tensor.matmul(o, l, r, start=start, stop=stop)

            ident = C("ident")
            ones = C("ones")
            n_prep = [0]

            def prep(ins):
                n_prep[0] += 1
                ins.then_inc(prep_pe, 1)

            pe.wait_ge(ld_cst, 16)
            pe.wait_ge(prep_dve, PREP["BDA"])
            prep(nc.tensor.transpose(PS[:, 0, 0:P], BDA[:, :], ident))
            pe.wait_ge(prep_dve, PREP["BDAT"])
            prep(mm(PS[:, 1, 0:P], ones, BDAT[:, :]))
            pe.wait_ge(prep_dve, PREP["hat_rows"])
            prep(nc.tensor.transpose(PS[:, 2, 0:P], tmp[:, :], ident))
            pe.wait_ge(prep_dve, PREP["lap_rows"])
            prep(nc.tensor.transpose(PS[0:NODES, 3, 0:NODES], tmp2[0:NODES, 0:NODES], ident[0:NODES, 0:NODES]))

            pe.wait_ge(prep_dve, PREP["S"])
            with pe.Fori(0, REFLECTIONS) as k:
                pe.wait_ge(hh_x, k + 1)
                mm(PS[:, 0, 0:NODES], xcol[0:NODES, 0:1].broadcast_to((NODES, P)), ident[0:NODES, 0:NODES]).then_inc(hh_row, 1)
                pe.wait_ge(hh_v, k + 1)
                mm(PS[:, 1, 0:NODES], vcol[0:NODES, 0:1].broadcast_to((NODES, P)), S[0:NODES, :]).then_inc(hh_av, 1)
            pe.wait_ge(prep_dve, PREP["diagonals"])
            mm(PS[:, 2, 0:NODES], ones[0:NODES, :], EV[:, 0, 0:NODES])
            prep(mm(PS[:, 2, NODES:P], ones[0:NODES, :], EV[:, 1, 0:NODES]))
            with pe.Fori(0, ROUNDS) as r:
                pe.wait_ge(grid_cnt, r + 1)
                mm(PS[:, 0, 0:1], C("fold"), sc[:, 3:4]).then_inc(grid_sum, 1)
            pe.wait_ge(prep_dve, PREP["V"])
            nc.tensor.transpose(PS[0:NODES, 0, 0:NODES], Fq[0:NODES, 6, :], ident[0:NODES, 0:NODES])
            prep(nc.tensor.transpose(PS[0:NODES, 1, 0:NODES], S[NODES:P, :], ident[NODES:P, NODES:P]))
            pe.wait_ge(prep_dve, PREP["VT"])
            VT, QT = EV[:, 2, 0:NODES], EV[:, 3, 0:NODES]
            mm(PS[0:NODES, 0, 0:NODES], QT, VT)
            prep(mm(PS[0:NODES, 1, 0:P], VT, EV[:, 3, :]))
            pe.wait_ge(prep_dve, PREP["U"])
            U = EV[:, 4, 0:NODES]
            mm(PS[0:NODES, 2, 0:NODES], LS[:, :], U)
            prep(mm(PS[0:NODES, 3, 0:NODES], U, U))
            pe.wait_ge(prep_dve, PREP["AU"])
            prep(mm(PS[0:NODES, 0, 0:NODES], U, EV[:, 6, 0:NODES]))
            pe.wait_ge(prep_dve, PREP["ritz"])
            prep(mm(PS[0:NODES, 1, 0:NODES], ones[0:NODES, 0:NODES], EV[:, 9, 0:NODES]))
            pe.wait_ge(prep_dve, PREP["I+E"])
            mm(PS[:, 2, 0:NODES], EV[:, 5, :], EV[:, 8, 0:NODES])
            prep(mm(PS[:, 3, 0:NODES], EV[:, 8, :], EV[:, 5, 0:NODES]))

            pe.wait_ge(ld_w, 16)
            pe.wait_ge(prep_dve, PREP["all"])
            with pe.Fori(0, ITER) as i:
                for k in range(NK):
                    pe.wait_ge(act_done[k], A_ACT.at(i, "norm"))
                    for t in range(TPC):
                        j = mm(bank(k)[:, t * P:(t + 1) * P], T0[:, k, t * P:(t + 1) * P], BDHT[:, :])
                    j.then_inc(pe_done[k], 1)
                for k in range(NK):
                    pe.wait_ge(act_done[k], A_ACT.at(i, "aggT"))
                    for c in range(2):
                        j = mm(banks(k)[:, c, :], W("w1T")[:, c * P:(c + 1) * P], T1[:, k, 0:CH])
                    j.then_inc(pe_done[k], 1)
            with pe.Fori(0, ITER) as i:
                for k in range(NK):
                    pe.wait_ge(act_done[k], B_ACT.at(i, "bn_relu"))
                    pe.wait_ge(dve_done[k], B_DVE.start(i))
                    for c in range(2):
                        j = mm(bank(k), W("w2T")[:, c * P:(c + 1) * P], T1[:, k, c * CH:(c + 1) * CH],
                               start=(c == 0), stop=(c == 1))
                    j.then_inc(pe_done[k], 1)

            def tiles(k, lhs, rhs, n=1):
                for t in range(TPC):
                    j = mm(bank(k)[:, t * P:(t + 1) * P], lhs[:, t * P:(t + 1) * P], rhs)
                j.then_inc(pe_done[k], 1)

            with pe.Fori(0, ITER) as i:
                for k in range(NK):
                    pe.wait_ge(act_done[k], C_ACT.at(i, "bn"))
                    pe.wait_ge(dve_done[k], C_DVE.start(i))
                    for t in range(TPC):
                        j = nc.tensor.transpose(bank(k)[:, t * P:(t + 1) * P], T1[:, k, t * P:(t + 1) * P], ident)
                    j.then_inc(pe_done[k], 1)
                for k in range(NK):
                    pe.wait_ge(act_done[k], C_ACT.at(i, "norm"))
                    tiles(k, T0[:, k, :], BDAT[:, :])
                for k in range(NK):
                    pe.wait_ge(act_done[k], C_ACT.at(i, "aggT"))
                    tiles(k, T1[:, k, :], W("wg0"))
                for k in range(NK):
                    pe.wait_ge(act_done[k], C_ACT.at(i, "relu0"))
                    tiles(k, T0[:, k, :], BDAT[:, :])
                for k in range(NK):
                    pe.wait_ge(act_done[k], C_ACT.at(i, "aggT2"))
                    mm(bank(k), W("wg1"), T1[:, k, 0:CH]).then_inc(pe_done[k], 1)
                for r, (p, s, part) in enumerate(LSTM):
                    for q in range(2):
                        x, n = lstm_in(H, q, p, s, part)
                        G = PS[:, 4 * q:4 * q + 4, 0:n]
                        if r == 0:
                            for k in (2 * q, 2 * q + 1):
                                pe.wait_ge(act_done[k], C_ACT.at(i, "h"))
                        for g in gates(s):
                            if r:
                                last = {"i": "h", "g": "h", "f": "h", "o": "h"}[g]
                                if g == "i":
                                    pe.wait_ge(dve_set[q], R_DVE.at(i, f"{last}{r - 1}"))
                            j = mm(G[:, GATE[g], :], wT("wihT", p, g), x, stop=(s == 0))
                            if s == 0:
                                j.then_inc(pe_set[q], 1)
                        if s:
                            for g in gates(s):
                                mm(G[:, GATE[g], :], wT("whhT", p, g), LB[:, q, 3, 0:n], start=False)\
                                    .then_inc(pe_set[q], 1)
                for k in range(NK):
                    pe.wait_ge(dve_set[k // 2], R_DVE.start(i + 1))
                    for t in range(TPC):
                        j = nc.tensor.transpose(bank(k)[:, t * P:(t + 1) * P],
                                                H[:, k * CH + t * P:k * CH + (t + 1) * P], ident)
                    j.then_inc(pe_done[k], 1)

            with pe.Fori(0, ITER) as i:
                for k in range(NK):
                    pe.wait_ge(act_done[k], D_ACT.at(i, "norm"))
                    tiles(k, T0[:, k, :], BDU[:, :])
                for k in range(NK):
                    pe.wait_ge(act_done[k], D_ACT.at(i, "aggT"))
                    mm(bank(k), W("l2w1"), T1[:, k, 0:CH]).then_inc(pe_done[k], 1)
                for k in range(NK):
                    pe.wait_ge(act_done[k], D_ACT.at(i, "hid"))
                    tiles(k, T0[:, k, :], W("l2w2"))
                for k in range(NK):
                    pe.wait_ge(dve_done[k], D_DVE.at(i, "o"))
                    mm(bank(k), BDUT[:, :], T1[:, k, 0:CH]).then_inc(pe_done[k], 1)
                for k in range(NK):
                    pe.wait_ge(act_done[k], D_ACT.at(i, "norm3"))
                    tiles(k, T0[:, k, :], BDST[:, :])
                for k in range(NK):
                    pe.wait_ge(act_done[k], D_ACT.at(i, "mix1T"))
                    for t in range(TPC):
                        j = mm(banks(k)[:, t // 2, (t % 2) * 256:(t % 2 + 1) * 256],
                               T1[:, k, t * P:(t + 1) * P], W("l3w1"))
                    j.then_inc(pe_done[k], 1)
                for k in range(NK):
                    pe.wait_ge(act_done[k], D_ACT.at(i, "relu1"))
                    for t in range(TPC):
                        for c in range(2):
                            j = mm(banks(k)[:, c, t * P:(t + 1) * P],
                                   R1[:, k, t * 256 + c * P:t * 256 + (c + 1) * P], BDST[:, :])
                    j.then_inc(pe_done[k], 1)
                for half, before in ((0, "mix2T"), (1, "relu2a")):
                    for k in range(NK):
                        pe.wait_ge(act_done[k], D_ACT.at(i, before))
                        for o in range(2):
                            for c in range(2):
                                j = mm(banks(k)[:, o, :],
                                       W("l3w2")[:, c * 512 + (2 * half + o) * P:c * 512 + (2 * half + o + 1) * P],
                                       A2[:, k, c * CH:(c + 1) * CH], start=(c == 0), stop=(c == 1))
                        j.then_inc(pe_done[k], 1)
                for k in range(NK):
                    pe.wait_ge(act_done[k], D_ACT.at(i, "relu2b"))
                    for t in range(TPC):
                        for c in range(4):
                            j = mm(bank(k)[:, t * P:(t + 1) * P], R2[:, k, c * CH + t * P:c * CH + (t + 1) * P],
                                   W("l3w3")[:, c * P:(c + 1) * P], start=(c == 0), stop=(c == 3))
                    j.then_inc(pe_done[k], 1)
                for k in range(NK):
                    pe.wait_ge(act_done[k], D_ACT.at(i, "s3"))
                    mm(bank(k), BDST[:, :], T1[:, k, 0:CH]).then_inc(pe_done[k], 1)

        @block.scalar
        def _(act):
            begin(act, act_done, act_set)

            def normed(k, sem_steps, i, name, before):
                act.wait_ge(dve_done[k], before)
                alone(act)
                for t in range(TPC):
                    j = nc.scalar.activation(T0[:, k, t * P:(t + 1) * P], X[:, bass.ds(i * SG + k * CH + t * P, P)],
                                             ACT.Relu, bias=shift[:, k, t:t + 1], scale=rstd[:, k, t:t + 1])
                j.then_inc(act_done[k], 1)

            def evac(k, dst, src, before, fn=ACT.Copy, **kw):
                act.wait_ge(pe_done[k], before)
                alone(act)
                nc.scalar.activation(dst, src, fn, **kw).then_inc(act_done[k], 1)

            act.wait_ge(ld_w, 16)
            with act.Fori(0, ITER) as i:
                for k in range(NK):
                    act.wait_ge(pe_done[k], A_PE.start(i))
                    normed(k, A_ACT, i, "norm", A_DVE.at(i, "shift"))
                for k in range(NK):
                    evac(k, T1[:, k, 0:CH], bank(k), A_PE.at(i, "agg"))
                for k in range(NK):
                    evac(k, Y1[:, 0, chunk_cols(i, k)], banks(k)[:, 0, :], A_PE.at(i, "w1"),
                         ACT.Identity, bias=W("b1")[:, 0:1])
            act.wait_ge(bn1_ready, 1)
            with act.Fori(0, ITER) as i:
                for k in range(NK):
                    act.wait_ge(pe_done[k], B_PE.start(i))
                    alone(act)
                    for c in range(2):
                        j = nc.scalar.activation(T1[:, k, c * CH:(c + 1) * CH], Y1[:, c, chunk_cols(i, k)], ACT.Relu,
                                                 bias=bn[:, 6 + c:7 + c], scale=bn[:, 4 + c:5 + c])
                    j.then_inc(act_done[k], 1)
            act.wait_ge(bn2_ready, 1)
            with act.Fori(0, ITER) as i:
                for k in range(NK):
                    act.wait_ge(pe_done[k], C_PE.start(i))
                    alone(act)
                    nc.scalar.activation(T1[:, k, 0:CH], Y2[:, chunk_cols(i, k)], ACT.Identity,
                                         bias=bn[:, 13:14], scale=bn[:, 12:13]).then_inc(act_done[k], 1)
                for k in range(NK):
                    normed(k, C_ACT, i, "norm", C_DVE.at(i, "shift"))
                for k in range(NK):
                    evac(k, T1[:, k, 0:CH], bank(k), C_PE.at(i, "agg"))
                for k in range(NK):
                    act.wait_ge(dve_done[k], C_DVE.at(i, "bias0"))
                    nc.scalar.activation(T0[:, k, :], T1[:, k, CH:2 * CH], ACT.Relu).then_inc(act_done[k], 1)
                for k in range(NK):
                    evac(k, T1[:, k, 0:CH], bank(k), C_PE.at(i, "agg2"))
                for k in range(NK):
                    act.wait_ge(dve_done[k], C_DVE.at(i, "bias1"))
                    nc.scalar.activation(H[:, k * CH:(k + 1) * CH], T1[:, k, CH:2 * CH], ACT.Relu)\
                        .then_inc(act_done[k], 1)
                for r, (p, s, part) in enumerate(LSTM):
                    for q in range(2):
                        _, n = lstm_in(H, q, p, s, part)
                        for g in gates(s):
                            act.wait_ge(pe_set[q], R_PE.at(i, f"{g}{r}"))
                            src = PS[:, 4 * q + GATE[g], 0:n]
                            dst = LB[:, q, 0, 0:n] if g == "g" else src
                            nc.scalar.activation(dst, src, ACT.Tanh if g == "g" else ACT.Sigmoid,
                                                 bias=lbias[:, (p - 1) * 4 + GATE[g]:(p - 1) * 4 + GATE[g] + 1])\
                                .then_inc(act_set[q], 1)
                        act.wait_ge(dve_set[q], R_DVE.at(i, f"c{r}" if s else f"ig{r}"))
                        nc.scalar.activation(LB[:, q, 2, 0:n], LB[:, q, 1, 0:n], ACT.Tanh).then_inc(act_set[q], 1)
            with act.Fori(0, ITER) as i:
                for k in range(NK):
                    act.wait_ge(pe_done[k], D_PE.start(i))
                    normed(k, D_ACT, i, "norm", D_DVE.at(i, "shift"))
                for k in range(NK):
                    evac(k, T1[:, k, 0:CH], bank(k), D_PE.at(i, "agg"))
                for k in range(NK):
                    evac(k, T0[:, k, :], bank(k), D_PE.at(i, "w1"), ACT.Relu, bias=W("l2b1"))
                for k in range(NK):
                    normed(k, D_ACT, i, "norm3", D_DVE.at(i, "shift3"))
                for k in range(NK):
                    evac(k, T1[:, k, 0:CH], bank(k), D_PE.at(i, "mix1"))
                for k in range(NK):
                    evac(k, R1[:, k, :], banks(k).rearrange("p b n -> p (b n)"), D_PE.at(i, "s1"), ACT.Relu)
                for k in range(NK):
                    evac(k, A2[:, k, :], banks(k).rearrange("p b n -> p (b n)"), D_PE.at(i, "mix2"))
                for h in range(2):
                    for k in range(NK):
                        evac(k, R2[:, k, h * 1024:(h + 1) * 1024], banks(k).rearrange("p b n -> p (b n)"),
                             D_PE.at(i, "s2a" if h == 0 else "s2b"), ACT.Relu)
                for k in range(NK):
                    evac(k, T1[:, k, 0:CH], bank(k), D_PE.at(i, "s3"))

        @block.gpsimd
        def _(pool):
            begin(pool, pool_done)
            mh = C("minus_half")

            def root(ap, out=None, e=None):
                o = ap if out is None else out
                return nc.gpsimd.tensor_tensor(o, ap, mh[:, 0:1] if e is None else e, ALU.pow)

            pool.wait_ge(ld_cst, 16)
            pool.wait_ge(degree, 1)
            nc.gpsimd.tensor_tensor(col[:, 4:6], col[:, 4:6], mh[:, 0:2], ALU.pow).then_inc(degree_root, 1)
            with pool.Fori(0, REFLECTIONS) as k:
                pool.wait_ge(hh_norm2, k + 1)
                root(sc[:, 2:3], sc[:, 3:4], C("half")).then_inc(hh_norm, 1)
            pool.wait_ge(norm2, 1)
            root(sc[:, 16:17], sc[:, 29:30]).then_inc(norm_root, 1)

            def layer_norm_roots(i, k, st, dst, sfx=""):
                pool.wait_ge(dve_done[k], dst.at(i, "aggr" + sfx))
                alone(pool)
                nc.gpsimd.tensor_scalar(rstd[:, k, :], mv[:, k, :, 1], EPS, None, ALU.add).then_inc(pool_done[k], 1)
                pool.wait_ge(pool_done[k], st.at(i, "var" + sfx))
                nc.gpsimd.tensor_tensor(rstd[:, k, :], rstd[:, k, :], mh[:, 0:TPC], ALU.pow).then_inc(pool_done[k], 1)

            with pool.Fori(0, ITER) as i:
                for k in range(NK):
                    layer_norm_roots(i, k, A_POOL, A_DVE)
            for n, c in enumerate((4, 5, 12)):
                pool.wait_ge(bn_var, n + 1)
                root(bn[:, c:c + 1]).then_inc(bn_root, 1)
            with pool.Fori(0, ITER) as i:
                for k in range(NK):
                    layer_norm_roots(i, k, C_POOL, C_DVE)
            with pool.Fori(0, ITER) as i:
                for sfx in ("", "3"):
                    for k in range(NK):
                        layer_norm_roots(i, k, D_POOL, D_DVE, sfx)

        @block.vector
        def _(dve):
            begin(dve, dve_done, dve_set)
            v = nc.vector
            done = [0]

            def step(ins, name=None):
                done[0] += 1
                ins.then_inc(prep_dve, 1)
                dve.wait_ge(prep_dve, done[0])
                if name:
                    assert PREP[name] == done[0], (name, done[0])

            def c1(n):
                return col[:, n:n + 1]

            def s1(n):
                return sc[:, n:n + 1]

            ident, blocks = C("ident"), C("blocks")
            pair = [P, 2, NODES]

            dve.wait_ge(ld_adj, 32)
            dve.wait_ge(ld_cst, 16)
            step(v.tensor_tensor(BDA[:, :].rearrange("p (b n) -> p b n", b=2),
                                 AA[:, :].unsqueeze(1).broadcast_to(pair),
                                 blocks.rearrange("p (b n) -> p b n", b=2), ALU.mult), "BDA")
            dve.wait_ge(prep_pe, 1)
            step(v.tensor_copy(BDAT[:, :], PS[:, 0, 0:P]), "BDAT")
            step(v.tensor_tensor(BDST[:, :], BDAT[:, :], BDAT[:, :], ALU.mult))
            step(v.tensor_reduce(c1(0), BDA[:, :], AX, ALU.add))
            step(v.tensor_reduce(c1(1), BDAT[:, :], AX, ALU.add))
            step(v.tensor_tensor_reduce(tmp[:, :], BDA[:, :], ident, 1.0, 0.0, ALU.mult, ALU.add, c1(2)))
            step(v.scalar_tensor_tensor(c1(3), c1(0), c1(1), c1(2), ALU.add, ALU.subtract))
            step(v.tensor_scalar(c1(4), c1(3), 1.0, None, ALU.add))
            step(v.tensor_scalar(c1(5), c1(3), TINY, None, ALU.max))
            v.sem_inc(degree, 1)
            dve.wait_ge(degree_root, 1)
            step(v.tensor_tensor(tmp[:, :], BDA[:, :], ident, ALU.add))
            step(v.tensor_scalar(tmp[:, :], tmp[:, :], c1(4), None, ALU.mult), "hat_rows")
            dve.wait_ge(prep_pe, 3)
            step(v.tensor_scalar(BDHT[:, :], PS[:, 2, 0:P], c1(4), None, ALU.mult))
            step(v.tensor_scalar(c1(6), c1(3), 0.0, None, ALU.is_gt))
            step(v.tensor_tensor(c1(5), c1(5), c1(6), ALU.mult))
            n64 = slice(0, NODES)
            step(v.tensor_scalar(tmp2[n64, 0:NODES], ident[n64, n64], col[n64, 3:4], 2.0, ALU.mult, ALU.mult))
            step(v.tensor_tensor(tmp2[n64, 0:NODES], tmp2[n64, 0:NODES], BDA[n64, n64], ALU.subtract))
            step(v.tensor_tensor(tmp2[n64, 0:NODES], tmp2[n64, 0:NODES], BDAT[n64, n64], ALU.subtract))
            step(v.tensor_scalar(tmp2[n64, 0:NODES], tmp2[n64, 0:NODES], col[n64, 5:6], None, ALU.mult), "lap_rows")
            dve.wait_ge(prep_pe, 4)
            step(v.tensor_scalar(LS[:, :], PS[n64, 3, n64], col[n64, 5:6], 0.5, ALU.mult, ALU.mult))
            step(v.memset(vcol[:, :], 0.0))
            step(v.tensor_copy(S[n64, :], LS[:, :]))
            step(v.tensor_copy(S[NODES:P, :], ident[NODES:P, NODES:P]), "S")
            dve.wait_ge(ld_w, 16)
            step(v.tensor_scalar(RB0[:, :], W("bg0row"), c1(0), None, ALU.mult))
            step(v.tensor_scalar(RB1[:, :], PS[:, 1, 0:P], W("bg1"), None, ALU.mult))
            step(v.tensor_tensor(lbias[:, :], W("bih"), W("bhh"), ALU.add))

            NOPS = 22
            with dve.Fori(0, REFLECTIONS) as k:
                n = [0]

                def op(ins):
                    n[0] += 1
                    ins.then_inc(hh_ops, 1)

                def sync():
                    dve.wait_ge(hh_ops, k * NOPS + n[0])

                v.tensor_tensor(xcol[n64, :], S[n64, bass.ds(k, 1)], C("below")[n64, bass.ds(k, 1)], ALU.mult)\
                    .then_inc(hh_x, 1)
                dve.wait_ge(hh_row, k + 1)
                op(v.tensor_copy(xrow[:, :], PS[:, 0, 0:NODES]))
                sync()
                alone(dve)
                op(v.tensor_tensor(rest[:, :], xrow[:, :], C("step")[:, bass.ds(NODES - 2 - k, NODES)], ALU.mult))
                op(v.tensor_copy(s1(0), xrow[:, bass.ds(k + 1, 1)]))
                sync()
                op(v.tensor_tensor_reduce(junk[:, :], rest[:, :], rest[:, :], 1.0, 0.0, ALU.mult, ALU.add, s1(1)))
                op(v.tensor_scalar(s1(4), s1(0), 0.0, 2.0, ALU.is_ge, ALU.mult))
                sync()
                v.scalar_tensor_tensor(s1(2), s1(0), s1(0), s1(1), ALU.mult, ALU.add)\
                    .then_inc(hh_norm2, 1)
                op(v.tensor_scalar(s1(5), s1(1), 0.0, -2.0, ALU.is_gt, ALU.mult))
                sync()
                dve.wait_ge(hh_norm, k + 1)
                op(v.scalar_tensor_tensor(s1(6), s1(4), -1.0, s1(3), ALU.add, ALU.mult))
                sync()
                op(v.scalar_tensor_tensor(s1(7), s1(5), 1.0, s1(6), ALU.add, ALU.mult))
                sync()
                op(v.scalar_tensor_tensor(s1(8), s1(0), s1(7), s1(7), ALU.subtract, ALU.mult))
                op(v.scalar_tensor_tensor(vrow[:, :], C("delta")[:, bass.ds(NODES - 1 - k, NODES)], s1(7),
                                          xrow[:, :], ALU.mult, ALU.subtract))
                v.scalar_tensor_tensor(vcol[n64, :], C("next")[n64, bass.ds(k, 1)], sc[n64, 7:8], xcol[n64, :],
                                       ALU.mult, ALU.subtract).then_inc(hh_v, 1)
                sync()
                op(v.tensor_scalar(s1(8), s1(8), -TINY, None, ALU.min))
                op(v.tensor_tensor_reduce(junk[:, :], S[:, :], vrow[:, :], 1.0, 0.0, ALU.mult, ALU.add, s1(10)))
                sync()
                op(v.reciprocal(s1(9), s1(8)))
                dve.wait_ge(hh_av, k + 1)
                op(v.tensor_tensor_reduce(rest[:, :], vrow[:, :], PS[:, 1, 0:NODES], 1.0, 0.0, ALU.mult, ALU.add,
                                          s1(11)))
                sync()
                op(v.tensor_scalar(s1(12), s1(11), s1(9), s1(9), ALU.mult, ALU.mult))
                op(v.tensor_scalar(s1(13), s1(10), s1(9), None, ALU.mult))
                sync()
                op(v.tensor_scalar(s1(12), s1(12), 0.5, None, ALU.mult))
                sync()
                op(v.tensor_scalar(wrow[:, :], vrow[:, :], s1(12), None, ALU.mult))
                op(v.scalar_tensor_tensor(wcol[:, :], vcol[:, :], s1(12), s1(13), ALU.mult, ALU.add))
                sync()
                op(v.scalar_tensor_tensor(wrow[:, :], PS[:, 1, 0:NODES], s1(9), wrow[:, :], ALU.mult, ALU.add))
                op(v.scalar_tensor_tensor(S[:, :], vrow[:, :], wcol[:, :], S[:, :], ALU.mult, ALU.add))
                sync()
                op(v.scalar_tensor_tensor(S[:, :], wrow[:, :], vcol[:, :], S[:, :], ALU.mult, ALU.add))
                sync()
                alone(dve)
                assert n[0] == NOPS, n[0]

            step(v.tensor_tensor(EV[:, 0, 0:NODES], S[n64, :], ident[n64, n64], ALU.mult))
            step(v.tensor_tensor(EV[:, 1, 0:NODES], S[n64, :], C("sub")[n64, :], ALU.mult), "diagonals")
            dve.wait_ge(prep_pe, 5)
            d, e, ne2, ne, t4, t5 = (Trow[:, n, :] for n in range(6))
            step(v.tensor_copy(Trow[:, 0:2, :], PS[:, 2, 0:P].rearrange("p (a n) -> p a n", a=2)))
            step(v.tensor_scalar(ne, e, -1.0, None, ALU.mult))
            step(v.tensor_tensor(ne2, ne, e, ALU.mult))
            step(v.tensor_scalar(ne2, ne2, -TINY, None, ALU.min))
            step(v.tensor_tensor(t4, ne, e, ALU.max))
            step(v.tensor_scalar(t5, d, -1.0, None, ALU.mult))
            step(v.tensor_tensor(t5, t5, d, ALU.max))
            step(v.tensor_reduce(s1(20), t5, AX, ALU.max))
            step(v.tensor_tensor(t5, t5, t4, ALU.add))
            step(v.tensor_tensor(t5[:, 1:NODES], t5[:, 1:NODES], t4[:, 0:NODES - 1], ALU.add))
            step(v.tensor_reduce(s1(0), t5, AX, ALU.max))
            step(v.tensor_scalar(s1(1), s1(0), -1.0001, -TINY, ALU.mult, ALU.add))
            step(v.tensor_scalar(s1(2), s1(1), -2.0 / (2 * M + 1), None, ALU.mult), "bound")

            GOPS, PER = 6, 2
            UN = 9
            with dve.Fori(0, ROUNDS) as r:
                g0 = r * GOPS

                def gop(ins, m):
                    ins.then_inc(grid_ops, 1)
                    dve.wait_ge(grid_ops, g0 + m)

                gop(v.tensor_scalar(xg[:, :], C("grid"), s1(2), s1(1), ALU.mult, ALU.add), 1)
                gop(v.tensor_tensor(Qh[:, :, :], d.unsqueeze(2).broadcast_to([P, NODES, M]),
                                    xg[:, :].unsqueeze(1).broadcast_to([P, NODES, M]), ALU.subtract), 2)
                alone(dve)
                with dve.Fori(0, (NODES - 1) // UN) as b:
                    for u in range(UN):
                        base = r * (PER * (NODES - 1)) + b * (PER * UN) + PER * u
                        v.reciprocal(rq[:, :], Qh[:, bass.ds(b * UN + u, 1), :].squeeze(1)).then_inc(twist_ops, 1)
                        dve.wait_ge(twist_ops, base + 1)
                        v.scalar_tensor_tensor(Qh[:, bass.ds(b * UN + u + 1, 1), :].squeeze(1), rq[:, :],
                                               ne2[:, bass.ds(b * UN + u, 1)],
                                               Qh[:, bass.ds(b * UN + u + 1, 1), :].squeeze(1), ALU.mult, ALU.add)\
                            .then_inc(twist_ops, 1)
                        dve.wait_ge(twist_ops, base + 2)
                        alone(dve)
                alone(dve)
                gop(v.tensor_scalar(Qh[:, :, :], Qh[:, :, :], 0.0, None, ALU.is_lt), 3)
                gop(v.tensor_reduce(cnt[:, :], Qh[:, :, :].rearrange("p i m -> p m i"), AX, ALU.add), 4)
                v.tensor_scalar(xg[:, :], cnt[:, :], C("lane"), None, ALU.is_le, ALU.add, accum_out=s1(3))\
                    .then_inc(grid_cnt, 1)
                dve.wait_ge(grid_sum, r + 1)
                gop(v.scalar_tensor_tensor(s1(1), PS[:, 0, 0:1], s1(2), s1(1), ALU.mult, ALU.add), 5)
                gop(v.tensor_scalar(s1(2), s1(2), 1.0 / (2 * M + 1), None, ALU.mult), 6)
                alone(dve)
            step(v.tensor_scalar(s1(2), s1(2), (2 * M + 1) / 2.0, None, ALU.mult))
            step(v.tensor_tensor(s1(1), s1(1), s1(2), ALU.add))

            top, bot, a, gam, hot, zt, zb, mul = (Fq[:, n, :] for n in range(8))
            step(v.tensor_scalar(a, d, s1(1), None, ALU.subtract))
            step(v.tensor_copy(top, a))
            step(v.tensor_copy(bot, a))
            t0 = ROUNDS * PER * (NODES - 1)
            alone(dve)
            with dve.Fori(0, NODES - 1) as b:
                v.reciprocal(s1(14), top[:, bass.ds(b, 1)]).then_inc(twist_ops, 1)
                v.reciprocal(s1(15), bot[:, bass.ds(NODES - 1 - b, 1)]).then_inc(twist_ops, 1)
                dve.wait_ge(twist_ops, b * 4 + (t0 + 2))
                v.scalar_tensor_tensor(top[:, bass.ds(b + 1, 1)], s1(14), ne2[:, bass.ds(b, 1)],
                                       top[:, bass.ds(b + 1, 1)], ALU.mult, ALU.add).then_inc(twist_ops, 1)
                v.scalar_tensor_tensor(bot[:, bass.ds(NODES - 2 - b, 1)], s1(15), ne2[:, bass.ds(NODES - 2 - b, 1)],
                                       bot[:, bass.ds(NODES - 2 - b, 1)], ALU.mult, ALU.add).then_inc(twist_ops, 1)
                dve.wait_ge(twist_ops, b * 4 + (t0 + 4))
                alone(dve)
            step(v.tensor_tensor(gam, top, bot, ALU.add))
            step(v.tensor_tensor(gam, gam, a, ALU.subtract))
            step(v.tensor_tensor(gam, gam, gam, ALU.mult))
            step(v.tensor_reduce(s1(14), gam, AX, ALU.min))
            step(v.tensor_scalar(hot, gam, s1(14), None, ALU.is_equal))
            step(v.reciprocal(mul, top))
            step(v.tensor_tensor(mul, mul, ne, ALU.mult))
            step(v.tensor_scalar(mul, mul, 1e18, -1e18, ALU.min, ALU.max))
            step(v.tensor_tensor_scan(zt[:, ::-1], mul[:, ::-1], hot[:, ::-1], 0.0, ALU.mult, ALU.add))
            step(v.reciprocal(mul, bot))
            step(v.tensor_tensor(mul[:, 1:NODES], mul[:, 1:NODES], ne[:, 0:NODES - 1], ALU.mult))
            step(v.tensor_scalar(mul, mul, 1e18, -1e18, ALU.min, ALU.max))
            step(v.tensor_tensor_scan(zb, mul, hot, 0.0, ALU.mult, ALU.add))
            step(v.tensor_tensor(zb, zb, zt, ALU.add))
            step(v.tensor_tensor(zb, zb, hot, ALU.subtract))
            step(v.tensor_tensor_reduce(junk[:, :], zb, zb, 1.0, 0.0, ALU.mult, ALU.add, s1(16)))
            step(v.tensor_tensor_reduce(junk[:, 0:HALF], zb[:, 0:HALF], zb[:, 0:HALF], 1.0, 0.0, ALU.mult, ALU.add,
                                        s1(17)))
            for n, cut in ((21, HALF), (22, HALF // 2), (23, HALF + HALF // 2)):
                step(v.tensor_scalar(s1(24), e[:, cut - 1:cut], 0.0, 2.0, ALU.is_ge, ALU.mult))
                step(v.tensor_scalar(s1(24), s1(24), -1.0, None, ALU.add))
                step(v.scalar_tensor_tensor(s1(n), zb[:, cut:cut + 1], s1(24), zb[:, cut - 1:cut], ALU.mult, ALU.add))
            step(v.tensor_scalar(s1(18), s1(16), 0.5, None, ALU.mult))
            step(v.tensor_tensor(s1(18), s1(17), s1(18), ALU.is_gt))
            step(v.tensor_tensor(s1(25), s1(22), s1(23), ALU.subtract))
            step(v.scalar_tensor_tensor(s1(25), s1(25), s1(18), s1(23), ALU.mult, ALU.add))
            step(v.tensor_scalar(s1(26), s1(20), 8 * 2.0 ** -24 / 1.8, None, ALU.mult))
            step(v.tensor_scalar(s1(26), s1(26), s1(26), s1(16), ALU.mult, ALU.mult))
            step(v.tensor_scalar(s1(27), s1(21), e[:, HALF - 1:HALF], None, ALU.mult))
            step(v.tensor_tensor(s1(27), s1(27), s1(27), ALU.mult))
            step(v.tensor_tensor(s1(27), s1(27), s1(26), ALU.is_gt))
            step(v.tensor_tensor(s1(28), s1(21), s1(25), ALU.subtract))
            step(v.scalar_tensor_tensor(s1(28), s1(28), s1(27), s1(25), ALU.mult, ALU.add))
            step(v.tensor_scalar(s1(28), s1(28), 0.0, 2.0, ALU.is_le, ALU.mult))
            v.sem_inc(norm2, 1)
            dve.wait_ge(norm_root, 1)
            step(v.scalar_tensor_tensor(s1(29), s1(28), -1.0, s1(29), ALU.add, ALU.mult))
            step(v.tensor_scalar(zb, zb, s1(29), None, ALU.mult), "V")

            def ev(n, m=NODES):
                return EV[:, n, 0:m]

            def dup(n):
                return EV[:, n, :].rearrange("p (b n) -> p b n", b=2)

            def twice(ap):
                return ap.unsqueeze(1).broadcast_to([NODES, 2, NODES])

            dve.wait_ge(prep_pe, 6)
            step(v.tensor_copy(ev(2), PS[n64, 0, n64]))
            step(v.tensor_copy(dup(3), twice(PS[n64, 1, n64])), "VT")
            dve.wait_ge(prep_pe, 7)
            step(v.tensor_copy(ev(4), PS[n64, 0, n64]))
            step(v.tensor_copy(ev(5, P), PS[n64, 1, 0:P]), "U")
            dve.wait_ge(prep_pe, 8)
            step(v.tensor_copy(ev(6), PS[n64, 2, n64]), "AU")
            step(v.tensor_tensor_reduce(ev(9), PS[n64, 3, n64], ident[n64, n64], 1.0, 0.0, ALU.mult, ALU.add,
                                        sc[n64, 30:31]))
            step(v.tensor_tensor(ev(7), ident[n64, n64], PS[n64, 3, n64], ALU.subtract))
            dve.wait_ge(prep_pe, 9)
            step(v.tensor_copy(ev(8), PS[n64, 0, n64]))
            step(v.tensor_tensor_reduce(ev(9), ev(8), ident[n64, n64], 1.0, 0.0, ALU.mult, ALU.add, sc[n64, 31:32]))
            step(v.reciprocal(sc[n64, 30:31], sc[n64, 30:31]))
            step(v.tensor_tensor(sc[n64, 31:32], sc[n64, 31:32], sc[n64, 30:31], ALU.mult))
            step(v.tensor_scalar(ev(9), ident[n64, n64], sc[n64, 31:32], None, ALU.mult), "ritz")
            dve.wait_ge(prep_pe, 10)
            lam = PS[n64, 1, n64]
            step(v.tensor_tensor(ev(10), ev(7), lam, ALU.mult))
            step(v.tensor_tensor(ev(10), ev(10), ev(8), ALU.add))
            step(v.tensor_scalar(ev(11), lam, sc[n64, 31:32], None, ALU.subtract))
            step(v.tensor_tensor(ev(8), ev(11), ev(11), ALU.mult))
            step(v.tensor_scalar(ev(8), ev(8), 1e-9, None, ALU.is_gt))
            step(v.scalar_tensor_tensor(ev(11), ev(11), 1.0, ev(8), ALU.add, ALU.subtract))
            step(v.reciprocal(ev(11), ev(11)))
            step(v.tensor_tensor(ev(10), ev(10), ev(11), ALU.mult))
            step(v.tensor_scalar(ev(7), ev(7), 0.5, None, ALU.mult))
            step(v.tensor_tensor(ev(10), ev(10), ev(7), ALU.subtract))
            step(v.tensor_tensor(ev(10), ev(10), ev(8), ALU.mult))
            step(v.tensor_tensor(ev(10), ev(10), ev(7), ALU.add))
            step(v.tensor_tensor(dup(8), twice(ev(10)), twice(ident[n64, n64]), ALU.add), "I+E")
            step(v.memset(BDU[:, :], 0.0))
            step(v.memset(BDUT[:, :], 0.0))
            dve.wait_ge(prep_pe, 11)
            for b in range(2):
                h = slice(b * NODES, (b + 1) * NODES)
                step(v.tensor_copy(BDU[h, h], PS[h, 2, n64]))
                step(v.tensor_copy(BDUT[h, h], PS[h, 3, n64]), "all" if b else None)

            def layer_norm(k, i, st, pst, sfx=""):
                alone(dve)
                for t in range(TPC):
                    j = v.bn_stats(stats[:, k, t, :], X[:, bass.ds(i * SG + k * CH + t * P, P)])
                j.then_inc(dve_done[k], 1)
                dve.wait_ge(dve_done[k], st.at(i, "stats" + sfx))
                alone(dve)
                for t in range(TPC):
                    j = v.bn_aggr(mv[:, k, t, :], stats[:, k, t, :])
                j.then_inc(dve_done[k], 1)
                dve.wait_ge(dve_done[k], st.at(i, "aggr" + sfx))
                dve.wait_ge(pool_done[k], pst.at(i, "rstd" + sfx))
                v.scalar_tensor_tensor(shift[:, k, :], mv[:, k, :, 0], -1.0, rstd[:, k, :], ALU.mult, ALU.mult)\
                    .then_inc(dve_done[k], 1)

            def chunk_no(i, k):
                return bass.ds(i * NK + k, 1)

            dve.wait_ge(ld_x, 16)
            with dve.Fori(0, ITER) as i:
                for k in range(NK):
                    dve.wait_ge(act_done[k], A_ACT.start(i))
                    layer_norm(k, i, A_DVE, A_POOL)
                for k in range(NK):
                    dve.wait_ge(pe_done[k], A_PE.at(i, "w1"))
                    v.tensor_scalar(Y1[:, 1, chunk_cols(i, k)], banks(k)[:, 1, :], W("b1")[:, 1:2], None, ALU.add)\
                        .then_inc(dve_done[k], 1)
                for k in range(NK):
                    dve.wait_ge(dve_done[k], A_DVE.at(i, "y_hi"))
                    dve.wait_ge(act_done[k], A_ACT.at(i, "y_lo"))
                    alone(dve)
                    for c in range(2):
                        j = v.bn_stats(ST1[:, c, chunk_no(i, k), :].squeeze(1), Y1[:, c, chunk_cols(i, k)])
                    j.then_inc(dve_done[k], 1)

            def b1(n, m=1):
                return bn[:, n:n + m]

            nb = [0]

            def bstep(ins):
                nb[0] += 1
                ins.then_inc(bn_ops, 1)
                dve.wait_ge(bn_ops, nb[0])

            for k in range(NK):
                dve.wait_ge(dve_done[k], A_DVE.end)
            for c in range(2):
                bstep(v.bn_aggr(b1(2 * c, 2), ST1[:, c, :, :].rearrange("p n s -> p (n s)")))
                bstep(v.tensor_scalar(b1(4 + c), b1(2 * c + 1), EPS, None, ALU.add))
                v.sem_inc(bn_var, 1)
                dve.wait_ge(bn_root, 1 + c)
                bstep(v.tensor_tensor(b1(4 + c), b1(4 + c), W("g1")[:, c:c + 1], ALU.mult))
                bstep(v.tensor_tensor(b1(6 + c), b1(2 * c), b1(4 + c), ALU.mult))
                bstep(v.tensor_tensor(b1(6 + c), W("be1")[:, c:c + 1], b1(6 + c), ALU.subtract))
            v.sem_inc(bn1_ready, 1)
            with dve.Fori(0, ITER) as i:
                for k in range(NK):
                    dve.wait_ge(pe_done[k], B_PE.at(i, "w2"))
                    v.tensor_scalar(Y2[:, chunk_cols(i, k)], bank(k), W("b2"), None, ALU.add).then_inc(dve_done[k], 1)
                for k in range(NK):
                    dve.wait_ge(dve_done[k], B_DVE.at(i, "y"))
                    alone(dve)
                    v.bn_stats(ST2[:, chunk_no(i, k), :].squeeze(1), Y2[:, chunk_cols(i, k)]).then_inc(dve_done[k], 1)
            for k in range(NK):
                dve.wait_ge(dve_done[k], B_DVE.end)
            bstep(v.bn_aggr(b1(8, 2), ST2[:, :, :].rearrange("p n s -> p (n s)")))
            bstep(v.tensor_scalar(b1(12), b1(9), EPS, None, ALU.add))
            v.sem_inc(bn_var, 1)
            dve.wait_ge(bn_root, 3)
            bstep(v.tensor_tensor(b1(12), b1(12), W("g2"), ALU.mult))
            bstep(v.tensor_tensor(b1(13), b1(8), b1(12), ALU.mult))
            bstep(v.tensor_tensor(b1(13), W("be2"), b1(13), ALU.subtract))
            v.sem_inc(bn2_ready, 1)

            four = [P, TPC, P]

            def by_tile(ap):
                return ap.rearrange("p (t n) -> p t n", t=TPC)

            def add_to_state(k, i, before):
                dve.wait_ge(pe_done[k], before)
                v.tensor_tensor(X[:, chunk_cols(i, k)], X[:, chunk_cols(i, k)], bank(k), ALU.add)\
                    .then_inc(dve_done[k], 1)

            with dve.Fori(0, ITER) as i:
                for k in range(NK):
                    add_to_state(k, i, C_PE.at(i, "turn"))
                    dve.wait_ge(dve_done[k], C_DVE.at(i, "add"))
                    layer_norm(k, i, C_DVE, C_POOL)
                for k in range(NK):
                    dve.wait_ge(pe_done[k], C_PE.at(i, "g0"))
                    v.tensor_tensor(by_tile(T1[:, k, CH:2 * CH]), by_tile(bank(k)),
                                    RB0[:, :].unsqueeze(1).broadcast_to(four), ALU.add).then_inc(dve_done[k], 1)
                for k in range(NK):
                    dve.wait_ge(pe_done[k], C_PE.at(i, "g1"))
                    v.tensor_tensor(by_tile(T1[:, k, CH:2 * CH]), by_tile(bank(k)),
                                    RB1[:, :].unsqueeze(1).broadcast_to(four), ALU.add).then_inc(dve_done[k], 1)
                for r, (p, s, part) in enumerate(LSTM):
                    for q in range(2):
                        src, n = lstm_in(H, q, p, s, part)
                        G = PS[:, 4 * q:4 * q + 4, 0:n]
                        g_, cell, tcell, h_ = (LB[:, q, b, 0:n] for b in range(4))
                        dve.wait_ge(act_set[q], R_ACT.at(i, f"g{r}"))
                        v.tensor_tensor(LX[:, q, 0:n] if s else cell, g_, G[:, GATE["i"], :], ALU.mult)\
                            .then_inc(dve_set[q], 1)
                        if s:
                            dve.wait_ge(act_set[q], R_ACT.at(i, f"f{r}"))
                            v.tensor_tensor(cell, cell, G[:, GATE["f"], :], ALU.mult).then_inc(dve_set[q], 1)
                            dve.wait_ge(dve_set[q], R_DVE.at(i, f"fc{r}"))
                            v.tensor_tensor(cell, cell, LX[:, q, 0:n], ALU.add).then_inc(dve_set[q], 1)
                        dve.wait_ge(act_set[q], R_ACT.at(i, f"tanh{r}"))
                        if s == p - 1:
                            o, a1, a2 = src, tcell, G[:, GATE["o"], :]
                            if p > 1:
                                a1 = a1.rearrange("p (b w) -> p b w", b=SGR)
                                a2 = a2.rearrange("p (b w) -> p b w", b=SGR)
                        else:
                            o, a1, a2 = h_, tcell, G[:, GATE["o"], :]
                        v.tensor_tensor(o, a1, a2, ALU.mult).then_inc(dve_set[q], 1)
                for k in range(NK):
                    add_to_state(k, i, C_PE.at(i, "turn_h"))

            with dve.Fori(0, ITER) as i:
                for k in range(NK):
                    dve.wait_ge(dve_done[k], D_DVE.start(i))
                    layer_norm(k, i, D_DVE, D_POOL)
                for k in range(NK):
                    dve.wait_ge(pe_done[k], D_PE.at(i, "w2"))
                    v.tensor_tensor(by_tile(T1[:, k, 0:CH]), by_tile(bank(k)),
                                    W("l2b2row").unsqueeze(1).broadcast_to(four), ALU.add).then_inc(dve_done[k], 1)
                for k in range(NK):
                    add_to_state(k, i, D_PE.at(i, "back"))
                    dve.wait_ge(dve_done[k], D_DVE.at(i, "add"))
                    layer_norm(k, i, D_DVE, D_POOL, "3")
                for k in range(NK):
                    add_to_state(k, i, D_PE.at(i, "mix3"))


PREP = {"BDA": 1, "BDAT": 2, "hat_rows": 11, "lap_rows": 18, "S": 22, "diagonals": 27, "bound": 40, "V": 85,
        "VT": 87, "U": 89, "AU": 90, "ritz": 97, "I+E": 110, "all": 116}


def kernel(x, adj, **w):
    import concourse.bacc as bacc
    from concourse.bass_utils import run_bass_kernel_spmd

    f = {k: np.asarray(a) for k, a in w.items()}

    def cols(a):
        return np.ascontiguousarray(a.reshape(-1, P).T)

    def kchunks(a):
        return np.ascontiguousarray(a.reshape(-1, P, a.shape[1]).transpose(1, 0, 2).reshape(P, -1))

    def gate_major(a):
        return np.ascontiguousarray(a.transpose(2, 0, 1).reshape(P, -1))

    parts = {
        "w1T": f["L0_gnn_W1"].T, "w2T": kchunks(np.ascontiguousarray(f["L0_gnn_W2"].T)),
        "wg0": f["L1_gnn_Wg0"], "wg1": f["L1_gnn_Wg1"],
        "wihT": gate_major(f["L1_gnn_Wih"]), "whhT": gate_major(f["L1_gnn_Whh"]),
        "l2w1": f["L2_gnn_W1"], "l2w2": f["L2_gnn_W2"],
        "l3w1": f["L3_gnn_W1"], "l3w2": kchunks(f["L3_gnn_W2"]), "l3w3": kchunks(f["L3_gnn_W3"]),
        "b1": cols(f["L0_gnn_b1"]), "g1": cols(f["L0_gnn_g1"]), "be1": cols(f["L0_gnn_be1"]),
        "b2": cols(f["L0_gnn_b2"]), "g2": cols(f["L0_gnn_g2"]), "be2": cols(f["L0_gnn_be2"]),
        "bg1": cols(f["L1_gnn_bg1"]), "bih": cols(f["L1_gnn_bih"].reshape(-1)),
        "bhh": cols(f["L1_gnn_bhh"].reshape(-1)), "l2b1": cols(f["L2_gnn_b1"]),
        "bg0row": np.broadcast_to(f["L1_gnn_bg0"][None, :], (P, P)),
        "l2b2row": np.broadcast_to(f["L2_gnn_b2"][None, :], (P, P)),
    }
    arrays = {
        "x_in": np.ascontiguousarray(np.asarray(x).reshape(TILES, P, D).transpose(1, 0, 2).reshape(P, TILES * D)),
        "cst_in": np.ascontiguousarray(np.concatenate(list(constants().values()), axis=1)),
        "w_in": np.ascontiguousarray(np.concatenate([parts[k] for k in WEIGHT_W], axis=1)),
        "adj_in": np.ascontiguousarray(np.asarray(adj)),
    }
    nc = bacc.Bacc("TRN2", target_bir_lowering=False, num_devices=1)
    args = [nc.dram_tensor(n, a.shape, F32, kind="ExternalInput").ap() for n, a in arrays.items()]
    args.append(nc.dram_tensor("out", (P, TILES * D), F32, kind="ExternalOutput").ap())
    build(nc, *args)
    r = run_bass_kernel_spmd(nc, [arrays], core_ids=[0])
    got = r.results[0]["out"]
    return np.ascontiguousarray(got.reshape(P, TILES, D).transpose(1, 0, 2)).reshape(GRAPHS, NODES, D)
```

```python
from contextlib import ExitStack

import numpy as np

import concourse.bass as bass
from concourse import mybir

F32 = mybir.dt.float32
ALU = mybir.AluOpType
ACT = mybir.ActivationFunctionType
AX = mybir.AxisListType.X

P = 128
GRAPHS, NODES, D = 128, 64, 128
TOKENS = GRAPHS * NODES
TILES = TOKENS // P
CH = 512
TPC = CH // P
NK = 4
SG = NK * CH
ITER = TOKENS // SG
NCHUNK = TOKENS // CH
EPS = 1e-5
MAX_SKIP = 4
SET = SG // 2
SGR = SET // NODES
TINY = 1e-30
HALF = NODES // 2
M = 32
ROUNDS = 3
REFLECTIONS = NODES - 2


def constants():
    p = np.arange(P)[:, None]
    c = np.arange(P)[None, :]
    n = np.arange(NODES)[None, :]
    t = {}
    t["ident"] = (p == c)
    t["blocks"] = (p // NODES == c // NODES)
    t["fold"] = (p % NODES == c % NODES)
    t["ones"] = np.ones((P, P))
    t["below"] = (p > n) & (p < NODES)
    t["next"] = (p == n + 1)
    t["super"] = (n == p + 1)
    t["grid"] = np.arange(M)[None, :] + 1 + M * (p // NODES)
    t["lane"] = p % NODES
    t["minus_half"] = np.full((P, 4), -0.5)
    t["half"] = np.full((P, 1), 0.5)
    return {k: np.asarray(v, np.float32) for k, v in t.items()}


CONST_W = {k: v.shape[1] for k, v in constants().items()}
WEIGHT_W = {
    "w1T": 256, "w2T": 256, "wg0": 128, "wg1": 128, "wihT": 4 * 512, "whhT": 4 * 512, "l2w1": 128, "l2w2": 128,
    "l3w1": 256, "l3w2": 1024, "l3w3": 512,
    "b1": 2, "g1": 2, "be1": 2, "b2": 1, "g2": 1, "be2": 1, "bg1": 1, "bih": 16, "bhh": 16, "l2b1": 1,
    "bg0row": 128, "l2b2row": 128,
}


def offsets(widths):
    at, out = 0, {}
    for k, w in widths.items():
        out[k] = (at, at + w)
        at += w
    return out, at


class Steps:

    def __init__(self, before, names):
        self.before, self.names = before, names

    def at(self, i, name):
        return i * len(self.names) + (self.before + self.names.index(name) + 1)

    def start(self, i):
        return i * len(self.names) + self.before

    @property
    def end(self):
        return self.before + ITER * len(self.names)


BEGUN = 1

LN = ["stats", "aggr", "shift"]
LNP = ["var", "rstd"]
A_PE = Steps(BEGUN, ["agg", "w1"])
A_ACT = Steps(BEGUN, ["norm", "aggT", "y_lo"])
A_DVE = Steps(BEGUN, LN + ["y_hi", "bn_stats"])
B_PE = Steps(A_PE.end, ["w2"])
B_ACT = Steps(A_ACT.end, ["bn_relu"])
B_DVE = Steps(A_DVE.end, ["y", "bn_stats"])


class Order:

    def __init__(self, before, steps):
        self.before, self.steps = before, steps

    def at(self, i, name):
        return self.before + self.steps.index((i, name)) + 1

    @property
    def end(self):
        return self.before + len(self.steps)


def l1_order(before, first, inner, last):
    steps = [(0, n) for n in first]
    for i in range(ITER):
        steps += [(i, n) for n in inner] + [(i + 1, n) for n in first if i + 1 < ITER] + [(i, n) for n in last]
    return Order(before, steps)


C_PE = l1_order(B_PE.end, ["turn"], ["agg", "g0", "agg2", "g1"], ["turn_h"])
C_ACT = l1_order(B_ACT.end, ["bn", "norm"], ["aggT", "relu0", "aggT2", "h"], [])
C_DVE = l1_order(B_DVE.end, ["add"], ["bias0", "bias1"], ["add_h"])


def d_order(before, front, middle, rest, ahead=()):
    steps = [(0, n) for n in ahead]
    for i in range(ITER):
        steps += [(i, n) for n in front] + [(i - 1, n) for n in middle if i] + [(i, n) for n in rest]
        steps += [(i + 1, n) for n in ahead if i + 1 < ITER]
    return Order(before, steps + [(ITER - 1, n) for n in middle])


D_PE = d_order(C_PE.end, ["agg", "w1", "w2", "back"], ["s3", "mix3"], ["mix1", "s1", "mix2", "s2a", "s2b"])
D_ACT = d_order(C_ACT.end, ["aggT", "hid"], ["s3"], ["norm3", "mix1T", "relu1", "mix2T", "relu2a", "relu2b"],
                ["norm"])
D_DVE = d_order(C_DVE.end, ["o", "add"] + [s + "3" for s in LN], ["add3"], [], LN)
A_POOL = Steps(BEGUN, LNP)
D_POOL = d_order(A_POOL.end, [s + "3" for s in LNP], [], [], LNP)

LSTM = [(1, 0, 0), (1, 0, 1)] + [(p, s, 0) for p in range(2, MAX_SKIP + 1) for s in range(p)]
GATE = {"i": 0, "f": 1, "g": 2, "o": 3}


def gates(s):
    return "igo" if s == 0 else "igfo"


def lstm_steps():
    pe, act, pool = [], [], []
    for r, (p, s, _) in enumerate(LSTM):
        pe += [f"{g}{r}" for g in gates(s)]
        act += [f"{g}{r}" for g in gates(s)] + [f"tanh{r}"]
        pool += [f"ig{r}"] + ([f"fc{r}", f"c{r}"] if s else []) + [f"h{r}"]
    return Steps(BEGUN, pe), Steps(BEGUN, act), Steps(BEGUN, pool)


R_PE, R_ACT, R_POOL = lstm_steps()

REFLECTED = [26, 38, 50, 62, 62]
PACE = 2.9
PACE_GRID = 36.0


def build(nc, x_in, cst_in, w_in, adj_in, out):
    ctx = ExitStack()
    with ctx:
        def sb(name, shape):
            return ctx.enter_context(nc.sbuf_tensor(name, shape, F32))

        def sem(name):
            return ctx.enter_context(nc.semaphore(name))

        def sems(name, n):
            return [sem(f"{name}{k}") for k in range(n)]

        coff, cw = offsets(CONST_W)
        woff, ww = offsets(WEIGHT_W)
        cst = sb("cst", [P, cw])
        wts = sb("wts", [P, ww])

        def C(name):
            return cst[:, coff[name][0]:coff[name][1]]

        def W(name):
            return wts[:, woff[name][0]:woff[name][1]]

        X = sb("X", [P, TILES * D])
        BIG = sb("BIG", [P, 2 * TOKENS])
        Y1 = BIG[:, :].rearrange("p (c t) -> p c t", c=2)
        Y2 = Y1[:, 0, :]
        PS = ctx.enter_context(nc.psum_tensor("PS", [P, 8, 512], F32))

        def bank(k):
            return PS[:, 2 * k, :]

        def banks(k):
            return PS[:, 2 * k:2 * k + 2, :]

        AA = sb("AA", [P, NODES])
        BDA = sb("BDA", [P, P])
        BDAT = sb("BDAT", [P, P])
        BDHT = sb("BDHT", [P, P])
        BDST = sb("BDST", [P, P])
        BDU = sb("BDU", [P, P])
        BDUT = sb("BDUT", [P, P])
        RB0 = sb("RB0", [P, P])
        RB1 = sb("RB1", [P, P])
        lbias = sb("lbias", [P, 16])
        col = sb("col", [P, 16])
        tmp = sb("tmp", [P, P])
        tmp2 = sb("tmp2", [P, P])

        LS = sb("LS", [NODES, NODES])
        S = sb("S", [P, 2, NODES + 1])
        REC = sb("REC", [P, NODES])
        vcol = sb("vcol", [P, 1])
        wcol = sb("wcol", [P, 1])
        xrow = sb("xrow", [P, NODES])
        vrow = sb("vrow", [P, NODES])
        prow = sb("prow", [P, NODES])
        junk = sb("junk", [P, NODES])
        sc = sb("sc", [P, 40])
        Trow = sb("Trow", [P, 6, NODES])
        Qh = sb("Qh", [P, NODES, M])
        xg = sb("xg", [P, M])
        rq = sb("rq", [P, 2, M])
        cnt = sb("cnt", [P, M])
        Fq = sb("Fq", [P, 8, NODES])
        EV = sb("EV", [NODES, 12, P])

        lnv = sb("lnv", [P, 3, NK * TPC])
        stats = sb("stats", [P, NK, TPC, 6])
        mv = sb("mv", [P, NK, TPC, 2])
        rstd = sb("rstd", [P, NK, TPC])
        shift = sb("shift", [P, NK, TPC])
        T0 = sb("T0", [P, NK, CH])
        T1 = sb("T1", [P, NK, 2 * CH])
        ST1 = sb("ST1", [P, 2, NCHUNK, 6])
        ST2 = sb("ST2", [P, NCHUNK, 6])
        bnv = sb("bnv", [P, 16])
        LAT = BIG[:, TOKENS:2 * TOKENS]
        LB = LAT[:, 0:2 * 6 * 512].rearrange("p (s b n) -> p s b n", s=2, b=6)
        I_, G_, F_, O_, CELL, HP = range(6)
        H = LAT[:, 6144:6144 + SG]
        R1 = BIG[:, 0:4096].rearrange("p (k n) -> p k n", k=NK)
        A2 = BIG[:, 4096:8192].rearrange("p (k n) -> p k n", k=NK)
        R2 = BIG[:, 8192:16384].rearrange("p (k n) -> p k n", k=NK)

        ld_cst, ld_w, ld_adj, ld_x, st_out = sem("ld_cst"), sem("ld_w"), sem("ld_adj"), sem("ld_x"), sem("st_out")
        prep_dve, prep_pe = sem("prep_dve"), sem("prep_pe")
        hh_S, hh_row, hh_v, hh_av = sem("hh_S"), sem("hh_row"), sem("hh_v"), sem("hh_av")
        hh_upd = sem("hh_upd")
        hh_ops, grid_ops, twist_ops = sem("hh_ops"), sem("grid_ops"), sem("twist_ops")
        grid_cnt, grid_sum = sem("grid_cnt"), sem("grid_sum")
        bn1_ready, bn2_ready = sem("bn1_ready"), sem("bn2_ready")
        bn_ops = sem("bn_ops")
        pe_done, act_done, dve_done = sems("pe_done", NK), sems("act_done", NK), sems("dve_done", NK)
        pool_done = sems("pool_done", NK)
        degree, degree_root, norm2, norm_root, hh_norm2, hh_norm, hh_rec = (
            sem(n) for n in ("degree", "degree_root", "norm2", "norm_root", "hh_norm2", "hh_norm", "hh_rec"))
        passed = sem("passed")
        bn_var, bn_root = sem("bn_var"), sem("bn_root")
        pe_set, act_set, pool_set = sems("pe_set", 2), sems("act_set", 2), sems("pool_set", 2)
        ln_ops, ln_ready = sem("ln_ops"), sem("ln_ready")

        block = ctx.enter_context(nc.Block())

        def chunk_cols(i, k, n=CH):
            return bass.ds(i * (NK * n) + k * n, n)

        def wT(name, p, g):
            a = woff[name][0] + (p - 1) * 512 + GATE[g] * P
            return wts[:, a:a + P]

        def lstm_in(buf, q, p, s, part):
            if p == 1:
                return buf[:, q * SET + part * 512:q * SET + (part + 1) * 512], 512
            nw = NODES // p
            v = buf[:, q * SET:(q + 1) * SET].rearrange("p (b n) -> p b n", n=NODES)
            return v[:, :, s:s + p * (nw - 1) + 1:p], SGR * nw

        def alone(eng):
            eng.sem_inc(passed, 1)

        def eb(n):
            return PS[:, 6 + n // 2, (n % 2) * 256:(n % 2) * 256 + 256]

        def turn_bank(k):
            return PS[:, 6 + k % 2, :]

        def begin(eng, *groups):
            for group in groups:
                for one in group:
                    eng.sem_inc(one, BEGUN)

        @block.sync
        def _(sp):
            sp.dma_start(AA[0:NODES, :], adj_in).then_inc(ld_adj, 16)
            sp.dma_start(AA[NODES:P, :], adj_in).then_inc(ld_adj, 16)
            sp.dma_start(cst[:, :], cst_in).then_inc(ld_cst, 16)
            sp.dma_start(X[:, :], x_in).then_inc(ld_x, 16)
            sp.dma_start(wts[:, :], w_in).then_inc(ld_w, 16)
            for i in range(ITER):
                for k in range(NK):
                    sp.wait_ge(dve_done[k], D_DVE.at(i, "add3"))
                    a = i * SG + k * CH
                    sp.dma_start(out[:, a:a + CH], X[:, a:a + CH]).then_inc(st_out, 16)
            sp.wait_ge(st_out, 16 * NCHUNK)

        @block.tensor
        def _(pe):
            begin(pe, pe_done, pe_set)

            def mm(o, l, r, start=True, stop=True):
                return nc.tensor.matmul(o, l, r, start=start, stop=stop)

            ident = C("ident")
            ones = C("ones")
            n_prep = [0]

            def prep(ins):
                n_prep[0] += 1
                ins.then_inc(prep_pe, 1)

            pe.wait_ge(ld_cst, 16)
            pe.wait_ge(prep_dve, PREP["BDA"])
            prep(nc.tensor.transpose(PS[:, 0, 0:P], BDA[:, :], ident))
            pe.wait_ge(prep_dve, PREP["BDAT"])
            prep(mm(PS[:, 1, 0:P], ones, BDAT[:, :]))
            pe.wait_ge(prep_dve, PREP["hat_rows"])
            prep(nc.tensor.transpose(PS[:, 2, 0:P], tmp[:, :], ident))
            pe.wait_ge(prep_dve, PREP["lap_rows"])
            prep(nc.tensor.transpose(PS[0:NODES, 3, 0:NODES], tmp2[0:NODES, 0:NODES], ident[0:NODES, 0:NODES]))

            def eigen_products(lo, hi, tail):
                for k in range(lo, hi):
                    A = S[:, k % 2, :]
                    yield PACE
                    pe.wait_ge(hh_S, k + 1)
                    mm(eb(0)[:, 0:NODES + 1], A[0:NODES, 0:1].broadcast_to((NODES, P)),
                       ident[0:NODES, k:k + NODES + 1] if k + NODES + 1 <= P else None).then_inc(hh_row, 1)
                    yield PACE
                    pe.wait_ge(hh_v, k + 1)
                    mm(eb(2)[:, 0:NODES], vcol[0:NODES, 0:1].broadcast_to((NODES, P)), A[0:NODES, 1:NODES + 1])\
                        .then_inc(hh_av, 1)
                if not tail:
                    return
                yield PACE
                pe.wait_ge(prep_dve, PREP["diagonals"])
                mm(eb(0)[:, 0:NODES], ones[0:NODES, :], EV[:, 0, 0:NODES])
                prep(mm(eb(0)[:, NODES:P], ones[0:NODES, :], EV[:, 1, 1:NODES + 1]))
                for n in range(ROUNDS):
                    yield PACE_GRID
                    pe.wait_ge(grid_cnt, n + 1)
                    mm(eb(2)[:, 0:1], C("fold"), sc[:, 3:4]).then_inc(grid_sum, 1)
                yield PACE_GRID
                pe.wait_ge(prep_dve, PREP["V"])
                nc.tensor.transpose(eb(0)[0:NODES, 0:NODES], Fq[0:NODES, 6, :], ident[0:NODES, 0:NODES])
                prep(nc.tensor.transpose(eb(2)[0:NODES, 0:NODES], REC[NODES:P, :], ident[NODES:P, NODES:P]))
                yield PACE
                pe.wait_ge(prep_dve, PREP["VT"])
                VT, QT = EV[:, 2, 0:NODES], EV[:, 3, 0:NODES]
                mm(eb(0)[0:NODES, 0:NODES], QT, VT)
                prep(mm(eb(1)[0:NODES, 0:P], VT, EV[:, 3, :]))
                yield PACE
                pe.wait_ge(prep_dve, PREP["U"])
                U = EV[:, 4, 0:NODES]
                mm(eb(2)[0:NODES, 0:NODES], LS[:, :], U)
                prep(mm(eb(3)[0:NODES, 0:NODES], U, U))
                yield PACE
                pe.wait_ge(prep_dve, PREP["AU"])
                prep(mm(eb(0)[0:NODES, 0:NODES], U, EV[:, 6, 0:NODES]))
                yield PACE
                pe.wait_ge(prep_dve, PREP["ritz"])
                prep(mm(eb(1)[0:NODES, 0:NODES], ones[0:NODES, 0:NODES], EV[:, 9, 0:NODES]))
                yield PACE
                pe.wait_ge(prep_dve, PREP["I+E"])
                mm(eb(2)[:, 0:NODES], EV[:, 5, :], EV[:, 8, 0:NODES])
                prep(mm(eb(3)[:, 0:NODES], EV[:, 8, :], EV[:, 5, 0:NODES]))
                yield PACE

            pe.wait_ge(prep_dve, PREP["S"])
            for _ in eigen_products(0, REFLECTED[0], False):
                pass

            pe.wait_ge(ld_w, 16)
            with pe.Fori(0, ITER) as i:
                for k in range(NK):
                    pe.wait_ge(act_done[k], A_ACT.at(i, "norm"))
                    for t in range(TPC):
                        j = mm(bank(k)[:, t * P:(t + 1) * P], T0[:, k, t * P:(t + 1) * P], BDHT[:, :])
                    j.then_inc(pe_done[k], 1)
                for k in range(NK):
                    pe.wait_ge(act_done[k], A_ACT.at(i, "aggT"))
                    for c in range(2):
                        j = mm(banks(k)[:, c, :], W("w1T")[:, c * P:(c + 1) * P], T1[:, k, 0:CH])
                    j.then_inc(pe_done[k], 1)
            with pe.Fori(0, ITER) as i:
                for k in range(NK):
                    pe.wait_ge(act_done[k], B_ACT.at(i, "bn_relu"))
                    pe.wait_ge(dve_done[k], B_DVE.start(i))
                    for c in range(2):
                        j = mm(bank(k), W("w2T")[:, c * P:(c + 1) * P], T1[:, k, c * CH:(c + 1) * CH],
                               start=(c == 0), stop=(c == 1))
                    j.then_inc(pe_done[k], 1)

            def tiles(k, lhs, rhs, n=1):
                for t in range(TPC):
                    j = mm(bank(k)[:, t * P:(t + 1) * P], lhs[:, t * P:(t + 1) * P], rhs)
                j.then_inc(pe_done[k], 1)

            def turn(i, k):
                pe.wait_ge(act_done[k], C_ACT.at(i, "bn"))
                if k >= 2:
                    pe.wait_ge(dve_done[k - 2], C_DVE.at(i, "add"))
                for t in range(TPC):
                    j = nc.tensor.transpose(turn_bank(k)[:, t * P:(t + 1) * P], T1[:, k, t * P:(t + 1) * P], ident)
                j.then_inc(pe_done[k], 1)

            def lstm(i, small):
                since, since_turn = 0.0, False
                pace = next(small)
                rank = [[], []]
                for r, (p, s, part) in enumerate(LSTM):
                    for q in range(2):
                        x, n = lstm_in(H, q, p, s, part)
                        if r == 0:
                            for k in (2 * q, 2 * q + 1):
                                pe.wait_ge(act_done[k], C_ACT.at(i, "h"))
                        elif p > 1:
                            pe.wait_ge(pool_set[q], R_POOL.at(i, f"h{r - 1}"))
                        for g in gates(s):
                            m = len(rank[q])
                            rank[q].append(f"{g}{r}")
                            if m >= 3:
                                pe.wait_ge(act_set[q], R_ACT.at(i, rank[q][m - 3]))
                            G = PS[:, 3 * q + m % 3, 0:n]
                            j = mm(G, wT("wihT", p, g), x, stop=(s == 0))
                            if s:
                                j = mm(G, wT("whhT", p, g), LB[:, q, HP, 0:n], start=False)
                            j.then_inc(pe_set[q], 1)
                            since += n * 4 * (1 + (s > 0)) / 2400
                            if r == 2 and not since_turn:
                                since_turn = True
                                if i + 1 < ITER:
                                    for k in (2, 3):
                                        pe.wait_ge(dve_done[k], C_DVE.at(i + 1, "add"))
                            if r >= 2 and pace is not None and since >= pace:
                                pace, since = next(small, None), 0.0
                        if r == 1 and i + 1 < ITER:
                            for k in (2 * q, 2 * q + 1):
                                turn(i + 1, k)
                if pace is not None:
                    for _ in small:
                        pass

            for k in range(NK):
                turn(0, k)
            for i in range(ITER):
                for k in range(NK):
                    pe.wait_ge(act_done[k], C_ACT.at(i, "norm"))
                    if i:
                        pe.wait_ge(dve_done[k], C_DVE.at(i - 1, "add_h"))
                    tiles(k, T0[:, k, :], BDAT[:, :])
                for k in range(NK):
                    pe.wait_ge(act_done[k], C_ACT.at(i, "aggT"))
                    tiles(k, T1[:, k, :], W("wg0"))
                for k in range(NK):
                    pe.wait_ge(act_done[k], C_ACT.at(i, "relu0"))
                    tiles(k, T0[:, k, :], BDAT[:, :])
                for k in range(NK):
                    pe.wait_ge(act_done[k], C_ACT.at(i, "aggT2"))
                    mm(bank(k), W("wg1"), T1[:, k, 0:CH]).then_inc(pe_done[k], 1)
                lstm(i, eigen_products(REFLECTED[i], REFLECTED[i + 1], i == ITER - 1))
                for k in range(NK):
                    pe.wait_ge(pool_set[k // 2], R_POOL.start(i + 1))
                    if k == 2:
                        pe.wait_ge(pool_set[0], R_POOL.start(i + 1))
                    for t in range(TPC):
                        j = nc.tensor.transpose(bank(k)[:, t * P:(t + 1) * P],
                                                H[:, k * CH + t * P:k * CH + (t + 1) * P], ident)
                    j.then_inc(pe_done[k], 1)

            pe.wait_ge(prep_dve, PREP["all"])

            def last_products(i):
                for k in range(NK):
                    pe.wait_ge(act_done[k], D_ACT.at(i, "relu2b"))
                    for t in range(TPC):
                        for c in range(4):
                            j = mm(banks(k)[:, 1, t * P:(t + 1) * P], R2[:, k, c * CH + t * P:c * CH + (t + 1) * P],
                                   W("l3w3")[:, c * P:(c + 1) * P], start=(c == 0), stop=(c == 3))
                    j.then_inc(pe_done[k], 1)
                for k in range(NK):
                    pe.wait_ge(act_done[k], D_ACT.at(i, "s3"))
                    mm(banks(k)[:, 1, :], BDST[:, :], T1[:, k, CH:2 * CH]).then_inc(pe_done[k], 1)

            for i in range(ITER):
                for k in range(NK):
                    pe.wait_ge(act_done[k], D_ACT.at(i, "norm"))
                    if i:
                        pe.wait_ge(act_done[k], D_ACT.at(i - 1, "relu2b"))
                    else:
                        pe.wait_ge(dve_done[k], C_DVE.end)
                    tiles(k, T0[:, k, :], BDU[:, :])
                for k in range(NK):
                    pe.wait_ge(act_done[k], D_ACT.at(i, "aggT"))
                    mm(bank(k), W("l2w1"), T1[:, k, 0:CH]).then_inc(pe_done[k], 1)
                for k in range(NK):
                    pe.wait_ge(act_done[k], D_ACT.at(i, "hid"))
                    tiles(k, T0[:, k, :], W("l2w2"))
                for k in range(NK):
                    pe.wait_ge(dve_done[k], D_DVE.at(i, "o"))
                    mm(bank(k), BDUT[:, :], T1[:, k, 0:CH]).then_inc(pe_done[k], 1)
                if i:
                    last_products(i - 1)
                for k in range(NK):
                    pe.wait_ge(act_done[k], D_ACT.at(i, "norm3"))
                    tiles(k, T0[:, k, :], BDST[:, :])
                for k in range(NK):
                    pe.wait_ge(act_done[k], D_ACT.at(i, "mix1T"))
                    if i:
                        pe.wait_ge(dve_done[k], D_DVE.at(i - 1, "add3"))
                    for t in range(TPC):
                        j = mm(banks(k)[:, t // 2, (t % 2) * 256:(t % 2 + 1) * 256],
                               T1[:, k, t * P:(t + 1) * P], W("l3w1"))
                    j.then_inc(pe_done[k], 1)
                for k in range(NK):
                    pe.wait_ge(act_done[k], D_ACT.at(i, "relu1"))
                    for t in range(TPC):
                        for c in range(2):
                            j = mm(banks(k)[:, c, t * P:(t + 1) * P],
                                   R1[:, k, t * 256 + c * P:t * 256 + (c + 1) * P], BDST[:, :])
                    j.then_inc(pe_done[k], 1)
                for half, before in ((0, "mix2T"), (1, "relu2a")):
                    for k in range(NK):
                        pe.wait_ge(act_done[k], D_ACT.at(i, before))
                        for o in range(2):
                            for c in range(2):
                                j = mm(banks(k)[:, o, :],
                                       W("l3w2")[:, c * 512 + (2 * half + o) * P:c * 512 + (2 * half + o + 1) * P],
                                       A2[:, k, c * CH:(c + 1) * CH], start=(c == 0), stop=(c == 1))
                        j.then_inc(pe_done[k], 1)
            last_products(ITER - 1)

        @block.scalar
        def _(act):
            begin(act, act_done, act_set)

            def normed(k, sem_steps, i, name, before):
                act.wait_ge(dve_done[k], before)
                alone(act)
                for t in range(TPC):
                    j = nc.scalar.activation(T0[:, k, t * P:(t + 1) * P], X[:, bass.ds(i * SG + k * CH + t * P, P)],
                                             ACT.Relu, bias=shift[:, k, t:t + 1], scale=rstd[:, k, t:t + 1])
                j.then_inc(act_done[k], 1)

            def evac(k, dst, src, before, fn=ACT.Copy, **kw):
                act.wait_ge(pe_done[k], before)
                alone(act)
                nc.scalar.activation(dst, src, fn, **kw).then_inc(act_done[k], 1)

            act.wait_ge(ld_w, 16)
            with act.Fori(0, ITER) as i:
                for k in range(NK):
                    act.wait_ge(pe_done[k], A_PE.start(i))
                    normed(k, A_ACT, i, "norm", A_DVE.at(i, "shift"))
                for k in range(NK):
                    evac(k, T1[:, k, 0:CH], bank(k), A_PE.at(i, "agg"))
                for k in range(NK):
                    evac(k, Y1[:, 0, chunk_cols(i, k)], banks(k)[:, 0, :], A_PE.at(i, "w1"),
                         ACT.Identity, bias=W("b1")[:, 0:1])
            act.wait_ge(bn1_ready, 1)
            with act.Fori(0, ITER) as i:
                for k in range(NK):
                    act.wait_ge(pe_done[k], B_PE.start(i))
                    alone(act)
                    for c in range(2):
                        j = nc.scalar.activation(T1[:, k, c * CH:(c + 1) * CH], Y1[:, c, chunk_cols(i, k)], ACT.Relu,
                                                 bias=bnv[:, 6 + c:7 + c], scale=bnv[:, 4 + c:5 + c])
                    j.then_inc(act_done[k], 1)
            act.wait_ge(bn2_ready, 1)

            def bn(i):
                for k in range(NK):
                    act.wait_ge(pe_done[k], B_PE.end if i == 0 else C_PE.at(i - 1, "g1"))
                    nc.scalar.activation(T1[:, k, 0:CH], Y2[:, i * SG + k * CH:i * SG + (k + 1) * CH], ACT.Identity,
                                         bias=bnv[:, 13:14], scale=bnv[:, 12:13]).then_inc(act_done[k], 1)

            def norm(i):
                act.wait_ge(ln_ready, i + 1)
                for k in range(NK):
                    if i:
                        act.wait_ge(pe_done[k], C_PE.at(i - 1, "agg2"))
                    for t in range(TPC):
                        a = i * SG + k * CH + t * P
                        j = nc.scalar.activation(T0[:, k, t * P:(t + 1) * P], X[:, a:a + P], ACT.Relu,
                                                 bias=shift[:, k, t:t + 1], scale=rstd[:, k, t:t + 1])
                    j.then_inc(act_done[k], 1)

            bn(0)
            norm(0)
            for i in range(ITER):
                for k in range(NK):
                    evac(k, T1[:, k, 0:CH], bank(k), C_PE.at(i, "agg"))
                for k in range(NK):
                    act.wait_ge(dve_done[k], C_DVE.at(i, "bias0"))
                    nc.scalar.activation(T0[:, k, :], T1[:, k, CH:2 * CH], ACT.Relu).then_inc(act_done[k], 1)
                for k in range(NK):
                    evac(k, T1[:, k, 0:CH], bank(k), C_PE.at(i, "agg2"))
                for k in range(NK):
                    act.wait_ge(dve_done[k], C_DVE.at(i, "bias1"))
                    nc.scalar.activation(H[:, k * CH:(k + 1) * CH], T1[:, k, CH:2 * CH], ACT.Relu)\
                        .then_inc(act_done[k], 1)
                if i + 1 < ITER:
                    bn(i + 1)
                rank = [0, 0]
                for r, (p, s, part) in enumerate(LSTM):
                    if r == 4 and i + 1 < ITER:
                        norm(i + 1)
                    for q in range(2):
                        _, n = lstm_in(H, q, p, s, part)
                        act.wait_ge(pool_set[q], R_POOL.at(i, f"h{r - 1}") if r else R_POOL.start(i))
                        for g in gates(s):
                            act.wait_ge(pe_set[q], R_PE.at(i, f"{g}{r}"))
                            nc.scalar.activation(LB[:, q, {"i": I_, "g": G_, "f": F_, "o": O_}[g], 0:n],
                                                 PS[:, 3 * q + rank[q] % 3, 0:n],
                                                 ACT.Tanh if g == "g" else ACT.Sigmoid,
                                                 bias=lbias[:, (p - 1) * 4 + GATE[g]:(p - 1) * 4 + GATE[g] + 1])\
                                .then_inc(act_set[q], 1)
                            rank[q] += 1
                        act.wait_ge(pool_set[q], R_POOL.at(i, f"c{r}" if s else f"ig{r}"))
                        nc.scalar.activation(LB[:, q, I_, 0:n], LB[:, q, CELL, 0:n], ACT.Tanh).then_inc(act_set[q], 1)

            def copy(k, dst, src, before, fn=ACT.Copy, **kw):
                act.wait_ge(pe_done[k], before)
                nc.scalar.activation(dst, src, fn, **kw).then_inc(act_done[k], 1)

            def norm_tiles(i, k, name, before, free):
                act.wait_ge(dve_done[k], before)
                act.wait_ge(pe_done[k], free)
                for t in range(TPC):
                    a = i * SG + k * CH + t * P
                    j = nc.scalar.activation(T0[:, k, t * P:(t + 1) * P], X[:, a:a + P], ACT.Relu,
                                             bias=shift[:, k, t:t + 1], scale=rstd[:, k, t:t + 1])
                j.then_inc(act_done[k], 1)

            def both(k):
                return banks(k).rearrange("p b n -> p (b n)")

            for k in range(NK):
                norm_tiles(0, k, "norm", D_DVE.at(0, "shift"), C_PE.end)
            for i in range(ITER):
                for k in range(NK):
                    copy(k, T1[:, k, 0:CH], bank(k), D_PE.at(i, "agg"))
                for k in range(NK):
                    copy(k, T0[:, k, :], bank(k), D_PE.at(i, "w1"), ACT.Relu, bias=W("l2b1"))
                for k in range(NK):
                    if i:
                        copy(k, T1[:, k, CH:2 * CH], banks(k)[:, 1, :], D_PE.at(i - 1, "s3"))
                    norm_tiles(i, k, "norm3", D_DVE.at(i, "shift3"), D_PE.at(i, "w2"))
                for k in range(NK):
                    copy(k, T1[:, k, 0:CH], bank(k), D_PE.at(i, "mix1"))
                for k in range(NK):
                    copy(k, R1[:, k, :], both(k), D_PE.at(i, "s1"), ACT.Relu)
                for k in range(NK):
                    copy(k, A2[:, k, :], both(k), D_PE.at(i, "mix2"))
                for k in range(NK):
                    copy(k, R2[:, k, 0:1024], both(k), D_PE.at(i, "s2a"), ACT.Relu)
                for k in range(NK):
                    copy(k, R2[:, k, 1024:2048], both(k), D_PE.at(i, "s2b"), ACT.Relu)
                    if i + 1 < ITER:
                        norm_tiles(i + 1, k, "norm", D_DVE.at(i + 1, "shift"), D_PE.at(i, "mix1"))
            for k in range(NK):
                copy(k, T1[:, k, CH:2 * CH], banks(k)[:, 1, :], D_PE.at(ITER - 1, "s3"))

        @block.gpsimd
        def _(pool):
            begin(pool, pool_done, pool_set)
            mh = C("minus_half")

            def root(ap, out=None, e=None):
                o = ap if out is None else out
                return nc.gpsimd.tensor_tensor(o, ap, mh[:, 0:1] if e is None else e, ALU.pow)

            pool.wait_ge(ld_cst, 16)
            pool.wait_ge(degree, 1)
            nc.gpsimd.tensor_tensor(col[:, 4:6], col[:, 4:6], mh[:, 0:2], ALU.pow).then_inc(degree_root, 1)
            for k in range(REFLECTED[0]):
                pool.wait_ge(hh_norm2, k + 1)
                root(sc[:, 2:3], sc[:, 3:4], C("half")).then_inc(hh_norm, 1)

            def layer_norm_roots(i, k, st, dst, sfx=""):
                pool.wait_ge(dve_done[k], dst.at(i, "aggr" + sfx))
                if st is A_POOL:
                    alone(pool)
                nc.gpsimd.tensor_scalar(rstd[:, k, :], mv[:, k, :, 1], EPS, None, ALU.add).then_inc(pool_done[k], 1)
                pool.wait_ge(pool_done[k], st.at(i, "var" + sfx))
                nc.gpsimd.tensor_tensor(rstd[:, k, :], rstd[:, k, :], mh[:, 0:TPC], ALU.pow).then_inc(pool_done[k], 1)

            with pool.Fori(0, ITER) as i:
                for k in range(NK):
                    layer_norm_roots(i, k, A_POOL, A_DVE)
            for n, c in enumerate((4, 5, 12)):
                pool.wait_ge(bn_var, n + 1)
                root(bnv[:, c:c + 1]).then_inc(bn_root, 1)
            def product(q, name, out, a, b, op=ALU.mult):
                nc.gpsimd.tensor_tensor(out, a, b, op).then_inc(pool_set[q], 1)

            for i in range(ITER):
                for r, (p, s, part) in enumerate(LSTM):
                    for q in range(2):
                        place, n = lstm_in(H, q, p, s, part)
                        ig, gg, ff, oo, cell, hp = (LB[:, q, b, 0:n] for b in (I_, G_, F_, O_, CELL, HP))
                        pool.wait_ge(act_set[q], R_ACT.at(i, f"g{r}"))
                        product(q, "ig", gg if s else cell, ig, gg)
                        if s:
                            pool.wait_ge(act_set[q], R_ACT.at(i, f"f{r}"))
                            product(q, "fc", cell, cell, ff)
                            pool.wait_ge(pool_set[q], R_POOL.at(i, f"fc{r}"))
                            product(q, "c", cell, cell, gg, ALU.add)
                        pool.wait_ge(act_set[q], R_ACT.at(i, f"tanh{r}"))
                        if s < p - 1:
                            product(q, "h", hp, ig, oo)
                        elif p == 1:
                            product(q, "h", place, ig, oo)
                        else:
                            product(q, "h", place, ig.rearrange("p (b w) -> p b w", b=SGR),
                                    oo.rearrange("p (b w) -> p b w", b=SGR))
            for i in range(ITER + 1):
                for k in range(NK):
                    if i:
                        layer_norm_roots(i - 1, k, D_POOL, D_DVE, "3")
                for k in range(NK):
                    if i < ITER:
                        layer_norm_roots(i, k, D_POOL, D_DVE)

        @block.vector
        def _(dve):
            begin(dve, dve_done)
            v = nc.vector
            done = [0]

            def step(ins, name=None):
                done[0] += 1
                ins.then_inc(prep_dve, 1)
                dve.wait_ge(prep_dve, done[0])
                if name:
                    assert PREP[name] == done[0], (name, done[0])

            def c1(n):
                return col[:, n:n + 1]

            def s1(n):
                return sc[:, n:n + 1]

            ident, blocks = C("ident"), C("blocks")
            pair = [P, 2, NODES]

            dve.wait_ge(ld_adj, 32)
            dve.wait_ge(ld_cst, 16)
            step(v.tensor_tensor(BDA[:, :].rearrange("p (b n) -> p b n", b=2),
                                 AA[:, :].unsqueeze(1).broadcast_to(pair),
                                 blocks.rearrange("p (b n) -> p b n", b=2), ALU.mult), "BDA")
            dve.wait_ge(prep_pe, 1)
            step(v.tensor_copy(BDAT[:, :], PS[:, 0, 0:P]), "BDAT")
            step(v.tensor_tensor(BDST[:, :], BDAT[:, :], BDAT[:, :], ALU.mult))
            step(v.tensor_reduce(c1(0), BDA[:, :], AX, ALU.add))
            step(v.tensor_reduce(c1(1), BDAT[:, :], AX, ALU.add))
            step(v.tensor_tensor_reduce(tmp[:, :], BDA[:, :], ident, 1.0, 0.0, ALU.mult, ALU.add, c1(2)))
            step(v.scalar_tensor_tensor(c1(3), c1(0), c1(1), c1(2), ALU.add, ALU.subtract))
            step(v.tensor_scalar(c1(4), c1(3), 1.0, None, ALU.add))
            step(v.tensor_scalar(c1(5), c1(3), TINY, None, ALU.max))
            v.sem_inc(degree, 1)
            dve.wait_ge(degree_root, 1)
            step(v.tensor_tensor(tmp[:, :], BDA[:, :], ident, ALU.add))
            step(v.tensor_scalar(tmp[:, :], tmp[:, :], c1(4), None, ALU.mult), "hat_rows")
            dve.wait_ge(prep_pe, 3)
            step(v.tensor_scalar(BDHT[:, :], PS[:, 2, 0:P], c1(4), None, ALU.mult))
            step(v.tensor_scalar(c1(6), c1(3), 0.0, None, ALU.is_gt))
            step(v.tensor_tensor(c1(5), c1(5), c1(6), ALU.mult))
            n64 = slice(0, NODES)
            step(v.tensor_scalar(tmp2[n64, 0:NODES], ident[n64, n64], col[n64, 3:4], 2.0, ALU.mult, ALU.mult))
            step(v.tensor_tensor(tmp2[n64, 0:NODES], tmp2[n64, 0:NODES], BDA[n64, n64], ALU.subtract))
            step(v.tensor_tensor(tmp2[n64, 0:NODES], tmp2[n64, 0:NODES], BDAT[n64, n64], ALU.subtract))
            step(v.tensor_scalar(tmp2[n64, 0:NODES], tmp2[n64, 0:NODES], col[n64, 5:6], None, ALU.mult), "lap_rows")
            dve.wait_ge(prep_pe, 4)
            step(v.tensor_scalar(LS[:, :], PS[n64, 3, n64], col[n64, 5:6], 0.5, ALU.mult, ALU.mult))
            step(v.memset(S[:, :, :], 0.0))
            step(v.memset(EV[:, 1, NODES:NODES + 1], 0.0))
            step(v.tensor_copy(S[n64, 0, 0:NODES], LS[:, :]))
            step(v.tensor_copy(S[NODES:P, 0, 0:NODES], ident[NODES:P, NODES:P]), "S")
            v.sem_inc(hh_S, 1)
            dve.wait_ge(ld_w, 16)
            step(v.tensor_scalar(RB0[:, :], W("bg0row"), c1(0), None, ALU.mult))
            step(v.tensor_scalar(RB1[:, :], PS[:, 1, 0:P], W("bg1"), None, ALU.mult))
            step(v.tensor_tensor(lbias[:, :], W("bih"), W("bhh"), ALU.add))

            alpha, r2, n2, norm = xrow[:, 0:1], s1(1), s1(2), s1(3)
            sg, xm, esg, hd, nc_, guard, t_, m_, nc2, pc, y_ = (s1(n) for n in range(4, 15))
            hh = [0]

            def op(ins):
                hh[0] += 1
                ins.then_inc(hh_ops, 1)

            def sync(back=0):
                dve.wait_ge(hh_ops, hh[0] - back)

            I32 = mybir.dt.int32

            def inverse_root(x, y, do, wait):
                do(v.tensor_scalar(y.bitcast(I32), x.bitcast(I32), 1, None, ALU.logical_shift_right))
                wait()
                do(v.tensor_scalar(y.bitcast(I32), y.bitcast(I32), -1.0, float(0x5F3759DF), ALU.mult, ALU.add))
                wait()
                return (3.0, 12.0, 768.0)

            def reflection(k, by_pool):
                A, B = S[:, k % 2, :], S[:, 1 - k % 2, :]
                dve.wait_ge(hh_row, k + 1)
                op(v.tensor_copy(xrow[:, :], eb(0)[:, 1:NODES + 1]))
                op(v.tensor_tensor(xm, A[:, 0:1], C("below")[:, k:k + 1], ALU.mult))
                sync(1)
                op(v.tensor_tensor_reduce(junk[:, 1:NODES], xrow[:, 1:NODES], xrow[:, 1:NODES], 1.0, 0.0,
                                          ALU.mult, ALU.add, r2))
                op(v.tensor_scalar(sg, alpha, 0.0, 2.0, ALU.is_lt, ALU.mult))
                op(v.tensor_copy(REC[:, k:k + 1], A[:, 0:1]))
                sync(2)
                op(v.scalar_tensor_tensor(n2, alpha, alpha, r2, ALU.mult, ALU.add))
                if by_pool:
                    sync()
                    v.sem_inc(hh_norm2, 1)
                else:
                    sync(2)
                op(v.tensor_scalar(sg, sg, -1.0, None, ALU.add))
                op(v.tensor_scalar(vrow[:, 1:NODES], xrow[:, 1:NODES], -1.0, None, ALU.mult))
                op(v.tensor_scalar(guard, r2, 0.0, -1e30, ALU.is_le, ALU.mult))
                sync(2)
                op(v.tensor_scalar(esg, C("next")[:, k:k + 1], sg, None, ALU.mult))
                sync(1)
                op(v.tensor_scalar(guard, guard, -1.0, None, ALU.add))
                if by_pool:
                    dve.wait_ge(hh_norm, k + 1)
                else:
                    for c in inverse_root(n2, y_, op, sync):
                        op(v.scalar_tensor_tensor(m_, y_, y_, n2, ALU.mult, ALU.mult))
                        sync()
                        op(v.scalar_tensor_tensor(y_, m_, -c, y_, ALU.add, ALU.mult))
                        sync()
                    op(v.tensor_scalar(norm, y_, n2, -1.0 / 8192, ALU.mult, ALU.mult))
                sync()
                v.scalar_tensor_tensor(vcol[:, :], esg, norm, xm, ALU.mult, ALU.subtract).then_inc(hh_v, 1)
                op(v.scalar_tensor_tensor(vrow[:, 0:1], norm, sg, alpha, ALU.mult, ALU.subtract))
                sync()
                op(v.scalar_tensor_tensor(hd, norm, sg, vrow[:, 0:1], ALU.mult, ALU.mult))
                op(v.tensor_tensor_reduce(junk[:, :], A[:, 1:NODES + 1], vrow[:, :], 1.0, 0.0, ALU.mult,
                                          ALU.add, pc))
                sync(1)
                op(v.tensor_scalar(hd, hd, TINY, guard, ALU.max, ALU.mult))
                sync()
                op(v.reciprocal(nc_, hd))
                dve.wait_ge(hh_av, k + 1)
                op(v.tensor_tensor_reduce(junk[:, :], vrow[:, :], eb(2)[:, 0:NODES], 1.0, 0.0, ALU.mult,
                                          ALU.add, t_))
                sync(1)
                op(v.tensor_tensor(nc2, nc_, nc_, ALU.mult))
                op(v.tensor_scalar(prow[:, :], eb(2)[:, 0:NODES], nc_, None, ALU.mult))
                op(v.tensor_scalar(wcol[:, :], pc, nc_, None, ALU.mult))
                sync(2)
                op(v.tensor_scalar(m_, t_, nc2, None, ALU.mult))
                sync(2)
                op(v.scalar_tensor_tensor(B[:, 0:NODES], prow[:, :], vcol[:, :], A[:, 1:NODES + 1], ALU.mult,
                                          ALU.add))
                sync(1)
                op(v.scalar_tensor_tensor(wcol[:, :], vcol[:, :], m_, wcol[:, :], ALU.mult, ALU.add))
                sync()
                v.scalar_tensor_tensor(B[:, 0:NODES], vrow[:, :], wcol[:, :], B[:, 0:NODES], ALU.mult, ALU.add)\
                    .then_inc(hh_S, 1)

            for k in range(REFLECTED[0]):
                reflection(k, True)

            def tail():
                dve.wait_ge(hh_S, REFLECTIONS + 1)
                step(v.tensor_copy(REC[:, REFLECTIONS:NODES], S[:, REFLECTIONS % 2, 0:2]))

                step(v.tensor_tensor(EV[:, 0, 0:NODES], REC[n64, :], ident[n64, n64], ALU.mult))
                step(v.tensor_tensor(EV[:, 1, 0:NODES], REC[n64, :], C("super")[n64, :], ALU.mult), "diagonals")
                dve.wait_ge(prep_pe, 5)
                d, e, ne2, ne, t4, t5 = (Trow[:, n, :] for n in range(6))
                step(v.tensor_copy(Trow[:, 0:2, :], eb(0)[:, 0:P].rearrange("p (a n) -> p a n", a=2)))
                step(v.tensor_scalar(ne, e, -1.0, None, ALU.mult))
                step(v.tensor_tensor(ne2, ne, e, ALU.mult))
                step(v.tensor_scalar(ne2, ne2, -TINY, None, ALU.min))
                step(v.tensor_tensor(t4, ne, e, ALU.max))
                step(v.tensor_scalar(t5, d, -1.0, None, ALU.mult))
                step(v.tensor_tensor(t5, t5, d, ALU.max))
                step(v.tensor_reduce(s1(20), t5, AX, ALU.max))
                step(v.tensor_tensor(t5, t5, t4, ALU.add))
                step(v.tensor_tensor(t5[:, 1:NODES], t5[:, 1:NODES], t4[:, 0:NODES - 1], ALU.add))
                step(v.tensor_reduce(s1(0), t5, AX, ALU.max))
                step(v.tensor_scalar(s1(1), s1(0), -1.0001, -TINY, ALU.mult, ALU.add))
                step(v.tensor_scalar(s1(2), s1(1), -2.0 / (2 * M + 1), None, ALU.mult), "bound")

                GOPS = 8 + 4 * (HALF - 1)
                with dve.Fori(0, ROUNDS) as r:
                    g = [0]

                    def gop(ins):
                        g[0] += 1
                        ins.then_inc(grid_ops, 1)

                    def gsync(back=0):
                        dve.wait_ge(grid_ops, r * GOPS + (g[0] - back))

                    gop(v.tensor_scalar(xg[:, :], C("grid"), s1(2), s1(1), ALU.mult, ALU.add))
                    gsync()
                    gop(v.tensor_tensor(Qh[:, :, :], d.unsqueeze(2).broadcast_to([P, NODES, M]),
                                        xg[:, :].unsqueeze(1).broadcast_to([P, NODES, M]), ALU.subtract))
                    gsync()
                    for i in range(HALF):
                        j = NODES - 1 - i
                        if i:
                            gsync(1)
                        gop(v.reciprocal(rq[:, 0, :], Qh[:, i, :]))
                        if i:
                            gsync(1)
                        if i < HALF - 1:
                            gop(v.reciprocal(rq[:, 1, :], Qh[:, j, :]))
                            gsync(1)
                        else:
                            gsync()
                        gop(v.scalar_tensor_tensor(Qh[:, i + 1, :], rq[:, 0, :], ne2[:, i:i + 1], Qh[:, i + 1, :],
                                                   ALU.mult, ALU.add))
                        if i < HALF - 1:
                            gsync(1)
                            gop(v.scalar_tensor_tensor(Qh[:, j - 1, :], rq[:, 1, :], ne2[:, j - 1:j], Qh[:, j - 1, :],
                                                       ALU.mult, ALU.add))
                    gsync()
                    gop(v.tensor_scalar(Qh[:, :, :], Qh[:, :, :], 0.0, None, ALU.is_lt))
                    gsync()
                    gop(v.tensor_reduce(cnt[:, :], Qh[:, :, :].rearrange("p i m -> p m i"), AX, ALU.add))
                    gsync()
                    v.tensor_scalar(xg[:, :], cnt[:, :], C("lane"), None, ALU.is_le, ALU.add, accum_out=s1(3))\
                        .then_inc(grid_cnt, 1)
                    dve.wait_ge(grid_sum, r + 1)
                    gop(v.scalar_tensor_tensor(s1(1), eb(2)[:, 0:1], s1(2), s1(1), ALU.mult, ALU.add))
                    gsync()
                    gop(v.tensor_scalar(s1(2), s1(2), 1.0 / (2 * M + 1), None, ALU.mult))
                    gsync()
                    alone(dve)
                    assert g[0] == GOPS, g[0]
                step(v.tensor_scalar(s1(2), s1(2), (2 * M + 1) / 2.0, None, ALU.mult))
                step(v.tensor_tensor(s1(1), s1(1), s1(2), ALU.add))

                top, bot, a, gam, hot, zt, zb, mul = (Fq[:, n, :] for n in range(8))
                step(v.tensor_scalar(a, d, s1(1), None, ALU.subtract))
                step(v.tensor_copy(top, a))
                step(v.tensor_copy(bot, a))
                for i in range(NODES - 1):
                    j = NODES - 1 - i
                    if i:
                        dve.wait_ge(twist_ops, 4 * i - 1)
                    v.reciprocal(s1(14), top[:, i:i + 1]).then_inc(twist_ops, 1)
                    if i:
                        dve.wait_ge(twist_ops, 4 * i)
                    v.reciprocal(s1(15), bot[:, j:j + 1]).then_inc(twist_ops, 1)
                    dve.wait_ge(twist_ops, 4 * i + 1)
                    v.scalar_tensor_tensor(top[:, i + 1:i + 2], s1(14), ne2[:, i:i + 1], top[:, i + 1:i + 2],
                                           ALU.mult, ALU.add).then_inc(twist_ops, 1)
                    dve.wait_ge(twist_ops, 4 * i + 2)
                    v.scalar_tensor_tensor(bot[:, j - 1:j], s1(15), ne2[:, j - 1:j], bot[:, j - 1:j],
                                           ALU.mult, ALU.add).then_inc(twist_ops, 1)
                dve.wait_ge(twist_ops, 4 * (NODES - 1))
                step(v.tensor_tensor(gam, top, bot, ALU.add))
                step(v.tensor_tensor(gam, gam, a, ALU.subtract))
                step(v.tensor_tensor(gam, gam, gam, ALU.mult))
                step(v.tensor_reduce(s1(14), gam, AX, ALU.min))
                step(v.tensor_scalar(hot, gam, s1(14), None, ALU.is_equal))
                step(v.reciprocal(mul, top))
                step(v.tensor_tensor(mul, mul, ne, ALU.mult))
                step(v.tensor_scalar(mul, mul, 1e18, -1e18, ALU.min, ALU.max))
                step(v.tensor_tensor_scan(zt[:, ::-1], mul[:, ::-1], hot[:, ::-1], 0.0, ALU.mult, ALU.add))
                step(v.reciprocal(mul, bot))
                step(v.tensor_tensor(mul[:, 1:NODES], mul[:, 1:NODES], ne[:, 0:NODES - 1], ALU.mult))
                step(v.tensor_scalar(mul, mul, 1e18, -1e18, ALU.min, ALU.max))
                step(v.tensor_tensor_scan(zb, mul, hot, 0.0, ALU.mult, ALU.add))
                step(v.tensor_tensor(zb, zb, zt, ALU.add))
                step(v.tensor_tensor(zb, zb, hot, ALU.subtract))
                step(v.tensor_tensor_reduce(junk[:, :], zb, zb, 1.0, 0.0, ALU.mult, ALU.add, s1(16)))
                step(v.tensor_tensor_reduce(junk[:, 0:HALF], zb[:, 0:HALF], zb[:, 0:HALF], 1.0, 0.0, ALU.mult, ALU.add,
                                            s1(17)))
                for n, cut in ((21, HALF), (22, HALF // 2), (23, HALF + HALF // 2)):
                    step(v.tensor_scalar(s1(24), e[:, cut - 1:cut], 0.0, 2.0, ALU.is_ge, ALU.mult))
                    step(v.tensor_scalar(s1(24), s1(24), -1.0, None, ALU.add))
                    step(v.scalar_tensor_tensor(s1(n), zb[:, cut:cut + 1], s1(24), zb[:, cut - 1:cut], ALU.mult, ALU.add))
                step(v.tensor_scalar(s1(18), s1(16), 0.5, None, ALU.mult))
                step(v.tensor_tensor(s1(18), s1(17), s1(18), ALU.is_gt))
                step(v.tensor_tensor(s1(25), s1(22), s1(23), ALU.subtract))
                step(v.scalar_tensor_tensor(s1(25), s1(25), s1(18), s1(23), ALU.mult, ALU.add))
                step(v.tensor_scalar(s1(26), s1(20), 8 * 2.0 ** -24 / 1.8, None, ALU.mult))
                step(v.tensor_scalar(s1(26), s1(26), s1(26), s1(16), ALU.mult, ALU.mult))
                step(v.tensor_scalar(s1(27), s1(21), e[:, HALF - 1:HALF], None, ALU.mult))
                step(v.tensor_tensor(s1(27), s1(27), s1(27), ALU.mult))
                step(v.tensor_tensor(s1(27), s1(27), s1(26), ALU.is_gt))
                step(v.tensor_tensor(s1(28), s1(21), s1(25), ALU.subtract))
                step(v.scalar_tensor_tensor(s1(28), s1(28), s1(27), s1(25), ALU.mult, ALU.add))
                step(v.tensor_scalar(s1(28), s1(28), 0.0, 2.0, ALU.is_le, ALU.mult))
                for c in inverse_root(s1(16), s1(29), step, lambda: None):
                    step(v.scalar_tensor_tensor(s1(30), s1(29), s1(29), s1(16), ALU.mult, ALU.mult))
                    step(v.scalar_tensor_tensor(s1(29), s1(30), -c, s1(29), ALU.add, ALU.mult))
                step(v.tensor_scalar(s1(29), s1(29), -1.0 / 8192, None, ALU.mult))
                step(v.scalar_tensor_tensor(s1(29), s1(28), -1.0, s1(29), ALU.add, ALU.mult))
                step(v.tensor_scalar(zb, zb, s1(29), None, ALU.mult), "V")

                def ev(n, m=NODES):
                    return EV[:, n, 0:m]

                def dup(n):
                    return EV[:, n, :].rearrange("p (b n) -> p b n", b=2)

                def twice(ap):
                    return ap.unsqueeze(1).broadcast_to([NODES, 2, NODES])

                dve.wait_ge(prep_pe, 6)
                step(v.tensor_copy(ev(2), eb(0)[n64, n64]))
                step(v.tensor_copy(dup(3), twice(eb(2)[n64, n64])), "VT")
                dve.wait_ge(prep_pe, 7)
                step(v.tensor_copy(ev(4), eb(0)[n64, n64]))
                step(v.tensor_copy(ev(5, P), eb(1)[n64, 0:P]), "U")
                dve.wait_ge(prep_pe, 8)
                step(v.tensor_copy(ev(6), eb(2)[n64, n64]), "AU")
                step(v.tensor_tensor_reduce(ev(9), eb(3)[n64, n64], ident[n64, n64], 1.0, 0.0, ALU.mult, ALU.add,
                                            sc[n64, 30:31]))
                step(v.tensor_tensor(ev(7), ident[n64, n64], eb(3)[n64, n64], ALU.subtract))
                dve.wait_ge(prep_pe, 9)
                step(v.tensor_copy(ev(8), eb(0)[n64, n64]))
                step(v.tensor_tensor_reduce(ev(9), ev(8), ident[n64, n64], 1.0, 0.0, ALU.mult, ALU.add, sc[n64, 31:32]))
                step(v.reciprocal(sc[n64, 30:31], sc[n64, 30:31]))
                step(v.tensor_tensor(sc[n64, 31:32], sc[n64, 31:32], sc[n64, 30:31], ALU.mult))
                step(v.tensor_scalar(ev(9), ident[n64, n64], sc[n64, 31:32], None, ALU.mult), "ritz")
                dve.wait_ge(prep_pe, 10)
                lam = eb(1)[n64, n64]
                step(v.tensor_tensor(ev(10), ev(7), lam, ALU.mult))
                step(v.tensor_tensor(ev(10), ev(10), ev(8), ALU.add))
                step(v.tensor_scalar(ev(11), lam, sc[n64, 31:32], None, ALU.subtract))
                step(v.tensor_tensor(ev(8), ev(11), ev(11), ALU.mult))
                step(v.tensor_scalar(ev(8), ev(8), 1e-9, None, ALU.is_gt))
                step(v.scalar_tensor_tensor(ev(11), ev(11), 1.0, ev(8), ALU.add, ALU.subtract))
                step(v.reciprocal(ev(11), ev(11)))
                step(v.tensor_tensor(ev(10), ev(10), ev(11), ALU.mult))
                step(v.tensor_scalar(ev(7), ev(7), 0.5, None, ALU.mult))
                step(v.tensor_tensor(ev(10), ev(10), ev(7), ALU.subtract))
                step(v.tensor_tensor(ev(10), ev(10), ev(8), ALU.mult))
                step(v.tensor_tensor(ev(10), ev(10), ev(7), ALU.add))
                step(v.tensor_tensor(dup(8), twice(ev(10)), twice(ident[n64, n64]), ALU.add), "I+E")
                step(v.memset(BDU[:, :], 0.0))
                step(v.memset(BDUT[:, :], 0.0))
                dve.wait_ge(prep_pe, 11)
                for b in range(2):
                    h = slice(b * NODES, (b + 1) * NODES)
                    step(v.tensor_copy(BDU[h, h], eb(2)[h, n64]))
                    step(v.tensor_copy(BDUT[h, h], eb(3)[h, n64]), "all" if b else None)

            ln = [0]

            def layer_norms(i):
                def do(ins):
                    ln[0] += 1
                    ins.then_inc(ln_ops, 1)

                def wait():
                    dve.wait_ge(ln_ops, ln[0])

                for k in range(NK):
                    dve.wait_ge(pe_done[k], C_PE.at(i, "turn"))
                    x = X[:, i * SG + k * CH:i * SG + (k + 1) * CH]
                    v.tensor_tensor(x, x, turn_bank(k), ALU.add).then_inc(dve_done[k], 1)
                for k in range(NK):
                    dve.wait_ge(dve_done[k], C_DVE.at(i, "add"))
                    for t in range(TPC):
                        a = i * SG + k * CH + t * P
                        do(v.bn_stats(stats[:, k, t, :], X[:, a:a + P]))
                wait()
                for k in range(NK):
                    for t in range(TPC):
                        do(v.bn_aggr(mv[:, k, t, :], stats[:, k, t, :]))
                wait()
                dve.wait_ge(act_done[NK - 1], B_ACT.end if i == 0 else C_ACT.at(i - 1, "norm"))
                x, y, a = lnv[:, 0, :], lnv[:, 1, :], lnv[:, 2, :]
                mean, var = (mv[:, :, :, n].rearrange("p k t -> p (k t)") for n in range(2))
                do(v.tensor_scalar(x, var, EPS, None, ALU.add))
                wait()
                for c in inverse_root(x, y, do, wait):
                    do(v.tensor_tensor(a, y, y, ALU.mult))
                    wait()
                    do(v.tensor_tensor(a, a, x, ALU.mult))
                    wait()
                    do(v.scalar_tensor_tensor(y, a, -c, y, ALU.add, ALU.mult))
                    wait()
                do(v.tensor_scalar(rstd[:, :, :].rearrange("p k t -> p (k t)"), y, -1.0 / 8192, None, ALU.mult))
                wait()
                v.scalar_tensor_tensor(shift[:, :, :].rearrange("p k t -> p (k t)"), mean, -1.0,
                                       rstd[:, :, :].rearrange("p k t -> p (k t)"), ALU.mult, ALU.mult)\
                    .then_inc(ln_ready, 1)

            def layer_norm(k, i, st, pst, sfx=""):
                alone(dve)
                for t in range(TPC):
                    j = v.bn_stats(stats[:, k, t, :], X[:, bass.ds(i * SG + k * CH + t * P, P)])
                j.then_inc(dve_done[k], 1)
                dve.wait_ge(dve_done[k], st.at(i, "stats" + sfx))
                alone(dve)
                for t in range(TPC):
                    j = v.bn_aggr(mv[:, k, t, :], stats[:, k, t, :])
                j.then_inc(dve_done[k], 1)
                dve.wait_ge(dve_done[k], st.at(i, "aggr" + sfx))
                dve.wait_ge(pool_done[k], pst.at(i, "rstd" + sfx))
                v.scalar_tensor_tensor(shift[:, k, :], mv[:, k, :, 0], -1.0, rstd[:, k, :], ALU.mult, ALU.mult)\
                    .then_inc(dve_done[k], 1)

            def chunk_no(i, k):
                return bass.ds(i * NK + k, 1)

            dve.wait_ge(ld_x, 16)
            with dve.Fori(0, ITER) as i:
                for k in range(NK):
                    dve.wait_ge(act_done[k], A_ACT.start(i))
                    layer_norm(k, i, A_DVE, A_POOL)
                for k in range(NK):
                    dve.wait_ge(pe_done[k], A_PE.at(i, "w1"))
                    v.tensor_scalar(Y1[:, 1, chunk_cols(i, k)], banks(k)[:, 1, :], W("b1")[:, 1:2], None, ALU.add)\
                        .then_inc(dve_done[k], 1)
                for k in range(NK):
                    dve.wait_ge(dve_done[k], A_DVE.at(i, "y_hi"))
                    dve.wait_ge(act_done[k], A_ACT.at(i, "y_lo"))
                    alone(dve)
                    for c in range(2):
                        j = v.bn_stats(ST1[:, c, chunk_no(i, k), :].squeeze(1), Y1[:, c, chunk_cols(i, k)])
                    j.then_inc(dve_done[k], 1)

            def b1(n, m=1):
                return bnv[:, n:n + m]

            nb = [0]

            def bstep(ins):
                nb[0] += 1
                ins.then_inc(bn_ops, 1)
                dve.wait_ge(bn_ops, nb[0])

            for k in range(NK):
                dve.wait_ge(dve_done[k], A_DVE.end)
            for c in range(2):
                bstep(v.bn_aggr(b1(2 * c, 2), ST1[:, c, :, :].rearrange("p n s -> p (n s)")))
                bstep(v.tensor_scalar(b1(4 + c), b1(2 * c + 1), EPS, None, ALU.add))
                v.sem_inc(bn_var, 1)
                dve.wait_ge(bn_root, 1 + c)
                bstep(v.tensor_tensor(b1(4 + c), b1(4 + c), W("g1")[:, c:c + 1], ALU.mult))
                bstep(v.tensor_tensor(b1(6 + c), b1(2 * c), b1(4 + c), ALU.mult))
                bstep(v.tensor_tensor(b1(6 + c), W("be1")[:, c:c + 1], b1(6 + c), ALU.subtract))
            v.sem_inc(bn1_ready, 1)
            with dve.Fori(0, ITER) as i:
                for k in range(NK):
                    dve.wait_ge(pe_done[k], B_PE.at(i, "w2"))
                    v.tensor_scalar(Y2[:, chunk_cols(i, k)], bank(k), W("b2"), None, ALU.add).then_inc(dve_done[k], 1)
                for k in range(NK):
                    dve.wait_ge(dve_done[k], B_DVE.at(i, "y"))
                    alone(dve)
                    v.bn_stats(ST2[:, chunk_no(i, k), :].squeeze(1), Y2[:, chunk_cols(i, k)]).then_inc(dve_done[k], 1)
            for k in range(NK):
                dve.wait_ge(dve_done[k], B_DVE.end)
            bstep(v.bn_aggr(b1(8, 2), ST2[:, :, :].rearrange("p n s -> p (n s)")))
            bstep(v.tensor_scalar(b1(12), b1(9), EPS, None, ALU.add))
            v.sem_inc(bn_var, 1)
            dve.wait_ge(bn_root, 3)
            bstep(v.tensor_tensor(b1(12), b1(12), W("g2"), ALU.mult))
            bstep(v.tensor_tensor(b1(13), b1(8), b1(12), ALU.mult))
            bstep(v.tensor_tensor(b1(13), W("be2"), b1(13), ALU.subtract))
            v.sem_inc(bn2_ready, 1)

            four = [P, TPC, P]

            def by_tile(ap):
                return ap.rearrange("p (t n) -> p t n", t=TPC)

            def add_to_state(k, i, before):
                dve.wait_ge(pe_done[k], before)
                v.tensor_tensor(X[:, chunk_cols(i, k)], X[:, chunk_cols(i, k)], bank(k), ALU.add)\
                    .then_inc(dve_done[k], 1)

            layer_norms(0)
            for i in range(ITER):
                for name, product, bias in (("bias0", "g0", RB0), ("bias1", "g1", RB1)):
                    for k in range(NK):
                        dve.wait_ge(pe_done[k], C_PE.at(i, product))
                        v.tensor_tensor(by_tile(T1[:, k, CH:2 * CH]), by_tile(bank(k)),
                                        bias[:, :].unsqueeze(1).broadcast_to(four), ALU.add).then_inc(dve_done[k], 1)
                if i + 1 < ITER:
                    layer_norms(i + 1)
                for k in range(REFLECTED[i], REFLECTED[i + 1]):
                    reflection(k, False)
                if i == ITER - 1:
                    tail()
                for k in range(NK):
                    dve.wait_ge(pe_done[k], C_PE.at(i, "turn_h"))
                    x = X[:, i * SG + k * CH:i * SG + (k + 1) * CH]
                    v.tensor_tensor(x, x, bank(k), ALU.add).then_inc(dve_done[k], 1)


            def add(i, k, src, before):
                dve.wait_ge(pe_done[k], before)
                x = X[:, i * SG + k * CH:i * SG + (k + 1) * CH]
                v.tensor_tensor(x, x, src, ALU.add).then_inc(dve_done[k], 1)

            def stats_of(i, k, sfx):
                for t in range(TPC):
                    a = i * SG + k * CH + t * P
                    j = v.bn_stats(stats[:, k, t, :], X[:, a:a + P])
                j.then_inc(dve_done[k], 1)
                dve.wait_ge(dve_done[k], D_DVE.at(i, "stats" + sfx))
                for t in range(TPC):
                    j = v.bn_aggr(mv[:, k, t, :], stats[:, k, t, :])
                j.then_inc(dve_done[k], 1)

            def shift_of(i, k, sfx):
                dve.wait_ge(pool_done[k], D_POOL.at(i, "rstd" + sfx))
                v.scalar_tensor_tensor(shift[:, k, :], mv[:, k, :, 0], -1.0, rstd[:, k, :], ALU.mult, ALU.mult)\
                    .then_inc(dve_done[k], 1)

            for k in range(NK):
                dve.wait_ge(dve_done[k], C_DVE.end)
                stats_of(0, k, "")
            for k in range(NK):
                shift_of(0, k, "")
            for i in range(ITER):
                for k in range(NK):
                    dve.wait_ge(pe_done[k], D_PE.at(i, "w2"))
                    v.tensor_tensor(by_tile(T1[:, k, 0:CH]), by_tile(bank(k)),
                                    W("l2b2row").unsqueeze(1).broadcast_to(four), ALU.add).then_inc(dve_done[k], 1)
                for k in range(NK):
                    add(i, k, bank(k), D_PE.at(i, "back"))
                    dve.wait_ge(dve_done[k], D_DVE.at(i, "add"))
                    stats_of(i, k, "3")
                    if k:
                        shift_of(i, k - 1, "3")
                shift_of(i, NK - 1, "3")
                if i:
                    for k in range(NK):
                        add(i - 1, k, banks(k)[:, 1, :], D_PE.at(i - 1, "mix3"))
                if i + 1 < ITER:
                    for k in range(NK):
                        dve.wait_ge(act_done[k], D_ACT.at(i, "norm3"))
                        stats_of(i + 1, k, "")
                    for k in range(NK):
                        shift_of(i + 1, k, "")
            for k in range(NK):
                add(ITER - 1, k, banks(k)[:, 1, :], D_PE.at(ITER - 1, "mix3"))


PREP = {"BDA": 1, "BDAT": 2, "hat_rows": 11, "lap_rows": 18, "S": 23, "diagonals": 29, "bound": 42, "V": 96,
        "VT": 98, "U": 100, "AU": 101, "ritz": 108, "I+E": 121, "all": 127}


def kernel(x, adj, **w):
    import concourse.bacc as bacc
    from concourse.bass_utils import run_bass_kernel_spmd

    f = {k: np.asarray(a) for k, a in w.items()}

    def cols(a):
        return np.ascontiguousarray(a.reshape(-1, P).T)

    def kchunks(a):
        return np.ascontiguousarray(a.reshape(-1, P, a.shape[1]).transpose(1, 0, 2).reshape(P, -1))

    def gate_major(a):
        return np.ascontiguousarray(a.transpose(2, 0, 1).reshape(P, -1))

    parts = {
        "w1T": f["L0_gnn_W1"].T, "w2T": kchunks(np.ascontiguousarray(f["L0_gnn_W2"].T)),
        "wg0": f["L1_gnn_Wg0"], "wg1": f["L1_gnn_Wg1"],
        "wihT": gate_major(f["L1_gnn_Wih"]), "whhT": gate_major(f["L1_gnn_Whh"]),
        "l2w1": f["L2_gnn_W1"], "l2w2": f["L2_gnn_W2"],
        "l3w1": f["L3_gnn_W1"], "l3w2": kchunks(f["L3_gnn_W2"]), "l3w3": kchunks(f["L3_gnn_W3"]),
        "b1": cols(f["L0_gnn_b1"]), "g1": cols(f["L0_gnn_g1"]), "be1": cols(f["L0_gnn_be1"]),
        "b2": cols(f["L0_gnn_b2"]), "g2": cols(f["L0_gnn_g2"]), "be2": cols(f["L0_gnn_be2"]),
        "bg1": cols(f["L1_gnn_bg1"]), "bih": cols(f["L1_gnn_bih"].reshape(-1)),
        "bhh": cols(f["L1_gnn_bhh"].reshape(-1)), "l2b1": cols(f["L2_gnn_b1"]),
        "bg0row": np.broadcast_to(f["L1_gnn_bg0"][None, :], (P, P)),
        "l2b2row": np.broadcast_to(f["L2_gnn_b2"][None, :], (P, P)),
    }
    arrays = {
        "x_in": np.ascontiguousarray(np.asarray(x).reshape(TILES, P, D).transpose(1, 0, 2).reshape(P, TILES * D)),
        "cst_in": np.ascontiguousarray(np.concatenate(list(constants().values()), axis=1)),
        "w_in": np.ascontiguousarray(np.concatenate([parts[k] for k in WEIGHT_W], axis=1)),
        "adj_in": np.ascontiguousarray(np.asarray(adj)),
    }
    nc = bacc.Bacc("TRN2", target_bir_lowering=False, num_devices=1)
    args = [nc.dram_tensor(n, a.shape, F32, kind="ExternalInput").ap() for n, a in arrays.items()]
    args.append(nc.dram_tensor("out", (P, TILES * D), F32, kind="ExternalOutput").ap())
    build(nc, *args)
    r = run_bass_kernel_spmd(nc, [arrays], core_ids=[0])
    got = r.results[0]["out"]
    return np.ascontiguousarray(got.reshape(P, TILES, D).transpose(1, 0, 2)).reshape(GRAPHS, NODES, D)
```

```python
from contextlib import ExitStack

import numpy as np

import concourse.bass as bass
from concourse import mybir

F32 = mybir.dt.float32
ALU = mybir.AluOpType
ACT = mybir.ActivationFunctionType
AX = mybir.AxisListType.X

P = 128
GRAPHS, NODES, D = 128, 64, 128
TOKENS = GRAPHS * NODES
TILES = TOKENS // P
CH = 512
TPC = CH // P
NK = 4
SG = NK * CH
ITER = TOKENS // SG
NCHUNK = TOKENS // CH
EPS = 1e-5
MAX_SKIP = 4
SET = SG // 2
SGR = SET // NODES
TINY = 1e-30
HALF = NODES // 2
M = 32
ROUNDS = 3
REFLECTIONS = NODES - 2


def constants():
    p = np.arange(P)[:, None]
    c = np.arange(P)[None, :]
    n = np.arange(NODES)[None, :]
    t = {}
    t["ident"] = (p == c)
    t["blocks"] = (p // NODES == c // NODES)
    t["fold"] = (p % NODES == c % NODES)
    t["ones"] = np.ones((P, P))
    t["below"] = (p > n) & (p < NODES)
    t["next"] = (p == n + 1)
    t["super"] = (n == p + 1)
    t["grid"] = np.arange(M)[None, :] + 1 + M * (p // NODES)
    t["lane"] = p % NODES
    t["minus_half"] = np.full((P, 4), -0.5)
    t["half"] = np.full((P, 1), 0.5)
    return {k: np.asarray(v, np.float32) for k, v in t.items()}


CONST_W = {k: v.shape[1] for k, v in constants().items()}
WEIGHT_W = {
    "w1T": 256, "w2T": 256, "wg0": 128, "wg1": 128, "wihT": 4 * 512, "whhT": 4 * 512, "l2w1": 128, "l2w2": 128,
    "l3w1": 256, "l3w2": 1024, "l3w3": 512,
    "b1": 2, "g1": 2, "be1": 2, "b2": 1, "g2": 1, "be2": 1, "bg1": 1, "bih": 16, "bhh": 16, "l2b1": 1,
    "bg0row": 128, "l2b2row": 128,
}


def offsets(widths):
    at, out = 0, {}
    for k, w in widths.items():
        out[k] = (at, at + w)
        at += w
    return out, at


class Steps:

    def __init__(self, before, names):
        self.before, self.names = before, names

    def at(self, i, name):
        return i * len(self.names) + (self.before + self.names.index(name) + 1)

    def start(self, i):
        return i * len(self.names) + self.before

    @property
    def end(self):
        return self.before + ITER * len(self.names)


BEGUN = 1

LN = ["stats", "aggr", "shift"]
LNP = ["var", "rstd"]
A_PE = Steps(BEGUN, ["agg", "w1"])
A_ACT = Steps(BEGUN, ["norm", "aggT", "y"])
A_DVE = Steps(BEGUN, LN)
B_PE = Steps(A_PE.end, ["w2"])
B_ACT = Steps(A_ACT.end, ["bn_relu", "y"])
B_DVE = Steps(A_DVE.end, ["bn_stats"])


class Order:

    def __init__(self, before, steps):
        self.before, self.steps = before, steps

    def at(self, i, name):
        return self.before + self.steps.index((i, name)) + 1

    @property
    def end(self):
        return self.before + len(self.steps)


def l1_order(before, first, inner, last):
    steps = [(0, n) for n in first]
    for i in range(ITER):
        steps += [(i, n) for n in inner] + [(i + 1, n) for n in first if i + 1 < ITER] + [(i, n) for n in last]
    return Order(before, steps)


C_PE = l1_order(B_PE.end, ["turn"], ["agg", "g0", "agg2", "g1"], ["turn_h"])
C_ACT = l1_order(B_ACT.end, ["bn", "norm"], ["aggT", "relu0", "aggT2", "h"], [])
C_DVE = l1_order(B_DVE.end, ["add"], ["bias0", "bias1"], ["add_h"])


def d_order(before, front, middle, rest, ahead=()):
    steps = [(0, n) for n in ahead]
    for i in range(ITER):
        steps += [(i, n) for n in front] + [(i - 1, n) for n in middle if i] + [(i, n) for n in rest]
        steps += [(i + 1, n) for n in ahead if i + 1 < ITER]
    return Order(before, steps + [(ITER - 1, n) for n in middle])


D_PE = d_order(C_PE.end, ["agg", "w1", "w2", "back"], ["s3", "mix3"], ["mix1", "s1", "mix2", "s2a", "s2b"])
D_ACT = d_order(C_ACT.end, ["aggT", "hid"], ["s3"], ["norm3", "mix1T", "relu1", "mix2T", "relu2a", "relu2b"],
                ["norm"])
D_DVE = d_order(C_DVE.end, ["o", "add"] + [s + "3" for s in LN], ["add3"], [], LN)
A_POOL = Steps(BEGUN, LNP)
D_POOL = d_order(A_POOL.end, [s + "3" for s in LNP], [], [], LNP)

LSTM = [(1, 0, 0), (1, 0, 1)] + [(p, s, 0) for p in range(2, MAX_SKIP + 1) for s in range(p)]
GATE = {"i": 0, "f": 1, "g": 2, "o": 3}


def gates(s):
    return "igo" if s == 0 else "igfo"


def lstm_steps():
    pe, act, pool = [], [], []
    for r, (p, s, _) in enumerate(LSTM):
        pe += [f"{g}{r}" for g in gates(s)]
        act += [f"{g}{r}" for g in gates(s)] + [f"tanh{r}"]
        pool += [f"ig{r}"] + ([f"fc{r}", f"c{r}"] if s else []) + [f"h{r}"]
    return Steps(BEGUN, pe), Steps(BEGUN, act), Steps(BEGUN, pool)


R_PE, R_ACT, R_POOL = lstm_steps()

LEAD = 1
L0_FIRST = NCHUNK + 4
L0_SECOND = NCHUNK // 2 + 2
REFLECTED = LEAD + L0_FIRST + L0_SECOND
PACE = 2.5
PACE_ROW = 1.8
PACE_AV = 4.9
PACE_GRID = 38.0
PACE_TWIST = 45.0
DVE_STEP = 0.24
LN_STEP = 0.5
GAP = 0.5
NORM_ROUND = 8


def build(nc, x_in, cst_in, w_in, adj_in, out):
    ctx = ExitStack()
    with ctx:
        def sb(name, shape):
            return ctx.enter_context(nc.sbuf_tensor(name, shape, F32))

        def sem(name):
            return ctx.enter_context(nc.semaphore(name))

        def sems(name, n):
            return [sem(f"{name}{k}") for k in range(n)]

        coff, cw = offsets(CONST_W)
        woff, ww = offsets(WEIGHT_W)
        cst = sb("cst", [P, cw])
        wts = sb("wts", [P, ww])

        def C(name):
            return cst[:, coff[name][0]:coff[name][1]]

        def W(name):
            return wts[:, woff[name][0]:woff[name][1]]

        X = sb("X", [P, TILES * D])
        BIG = sb("BIG", [P, 2 * TOKENS])
        Y1 = BIG[:, :].rearrange("p (c t) -> p c t", c=2)
        Y2 = Y1[:, 0, :]
        PS = ctx.enter_context(nc.psum_tensor("PS", [P, 8, 512], F32))

        def bank(k):
            return PS[:, 2 * k, :]

        def banks(k):
            return PS[:, 2 * k:2 * k + 2, :]

        AA = sb("AA", [P, NODES])
        BDA = sb("BDA", [P, P])
        BDAT = sb("BDAT", [P, P])
        BDHT = sb("BDHT", [P, P])
        BDST = sb("BDST", [P, P])
        BDU = sb("BDU", [P, P])
        BDUT = sb("BDUT", [P, P])
        RB0 = sb("RB0", [P, P])
        RB1 = sb("RB1", [P, P])
        lbias = sb("lbias", [P, 16])
        col = sb("col", [P, 16])
        tmp = sb("tmp", [P, P])
        tmp2 = sb("tmp2", [P, P])

        LS = sb("LS", [NODES, NODES])
        S = sb("S", [P, 2, NODES + 1])
        REC = sb("REC", [P, NODES])
        vcol = sb("vcol", [P, 1])
        wcol = sb("wcol", [P, 1])
        xrow = sb("xrow", [P, NODES])
        vrow = sb("vrow", [P, NODES])
        prow = sb("prow", [P, NODES])
        junk = sb("junk", [P, NODES])
        sc = sb("sc", [P, 40])
        Trow = sb("Trow", [P, 6, NODES])
        Qh = sb("Qh", [P, NODES, M])
        xg = sb("xg", [P, M])
        rq = sb("rq", [P, 2, M])
        cnt = sb("cnt", [P, M])
        Fq = sb("Fq", [P, 8, NODES])
        EV = sb("EV", [NODES, 12, P])

        lnv = sb("lnv", [P, 3, NK * TPC])
        stats = sb("stats", [P, NK, TPC, 6])
        mv = sb("mv", [P, NK, TPC, 2])
        rstd = sb("rstd", [P, NK, TPC])
        shift = sb("shift", [P, NK, TPC])
        T0 = sb("T0", [P, NK, CH])
        T1 = sb("T1", [P, NK, 2 * CH])
        ST1 = sb("ST1", [P, 2, NCHUNK, 6])
        ST2 = sb("ST2", [P, NCHUNK, 6])
        bnv = sb("bnv", [P, 16])
        LAT = BIG[:, TOKENS:2 * TOKENS]
        LB = LAT[:, 0:2 * 6 * 512].rearrange("p (s b n) -> p s b n", s=2, b=6)
        I_, G_, F_, O_, CELL, HP = range(6)
        H = LAT[:, 6144:6144 + SG]
        R1 = BIG[:, 0:4096].rearrange("p (k n) -> p k n", k=NK)
        A2 = BIG[:, 4096:8192].rearrange("p (k n) -> p k n", k=NK)
        R2 = BIG[:, 8192:16384].rearrange("p (k n) -> p k n", k=NK)

        ld_cst, ld_w, ld_adj, ld_x, st_out = sem("ld_cst"), sem("ld_w"), sem("ld_adj"), sem("ld_x"), sem("st_out")
        prep_dve, prep_pe = sem("prep_dve"), sem("prep_pe")
        hh_S, hh_row, hh_v, hh_av = sem("hh_S"), sem("hh_row"), sem("hh_v"), sem("hh_av")
        hh_upd = sem("hh_upd")
        hh_ops, grid_ops, twist_ops = sem("hh_ops"), sem("grid_ops"), sem("twist_ops")
        grid_cnt, grid_sum = sem("grid_cnt"), sem("grid_sum")
        bn1_ready, bn2_ready = sem("bn1_ready"), sem("bn2_ready")
        hidden_seen = sem("hidden_seen")
        bn_ops = sem("bn_ops")
        pe_done, act_done, dve_done = sems("pe_done", NK), sems("act_done", NK), sems("dve_done", NK)
        pool_done = sems("pool_done", NK)
        degree, degree_root, norm2, norm_root, hh_norm2, hh_norm, hh_rec = (
            sem(n) for n in ("degree", "degree_root", "norm2", "norm_root", "hh_norm2", "hh_norm", "hh_rec"))
        passed = sem("passed")
        bn_var, bn_root = sem("bn_var"), sem("bn_root")
        pe_set, act_set, pool_set = sems("pe_set", 2), sems("act_set", 2), sems("pool_set", 2)
        ln_ops, ln_ready = sem("ln_ops"), sem("ln_ready")

        sent, there = [], {}

        block = ctx.enter_context(nc.Block())

        def chunk_cols(i, k, n=CH):
            return bass.ds(i * (NK * n) + k * n, n)

        def wT(name, p, g):
            a = woff[name][0] + (p - 1) * 512 + GATE[g] * P
            return wts[:, a:a + P]

        def lstm_in(buf, q, p, s, part):
            if p == 1:
                return buf[:, q * SET + part * 512:q * SET + (part + 1) * 512], 512
            nw = NODES // p
            v = buf[:, q * SET:(q + 1) * SET].rearrange("p (b n) -> p b n", n=NODES)
            return v[:, :, s:s + p * (nw - 1) + 1:p], SGR * nw

        def is_chunk(c):
            return 0 <= c < NCHUNK

        def l0_banks(c):
            return PS[:, 2 * (c % 3):2 * (c % 3) + 2, :]

        def alone(eng):
            eng.sem_inc(passed, 1)

        def eb(n):
            return PS[:, 6, n * P:(n + 1) * P]

        def l1_bank(k):
            return PS[:, 3 * (k // 2) + k % 2, :]

        def turn_bank(i, k):
            return PS[:, 7, :] if i else l1_bank(k)

        def begin(eng, *groups):
            for group in groups:
                for one in group:
                    eng.sem_inc(one, BEGUN)

        @block.sync
        def _(sp):
            sp.dma_start(AA[0:NODES, :], adj_in).then_inc(ld_adj, 16)
            sp.dma_start(AA[NODES:P, :], adj_in).then_inc(ld_adj, 16)
            sp.dma_start(cst[:, :], cst_in).then_inc(ld_cst, 16)
            sp.dma_start(X[:, :], x_in).then_inc(ld_x, 16)
            sp.dma_start(wts[:, :], w_in).then_inc(ld_w, 16)
            for i in range(ITER):
                for k in range(NK):
                    sp.wait_ge(dve_done[k], D_DVE.at(i, "add3"))
                    a = i * SG + k * CH
                    sp.dma_start(out[:, a:a + CH], X[:, a:a + CH]).then_inc(st_out, 16)
            sp.wait_ge(st_out, 16 * NCHUNK)

        @block.tensor
        def _(pe):
            begin(pe, pe_done, pe_set)

            def mm(o, l, r, start=True, stop=True):
                return nc.tensor.matmul(o, l, r, start=start, stop=stop)

            ident = C("ident")
            ones = C("ones")
            n_prep = [0]

            def prep(ins):
                n_prep[0] += 1
                ins.then_inc(prep_pe, 1)

            pe.wait_ge(ld_cst, 16)
            pe.wait_ge(prep_dve, PREP["BDA"])
            prep(nc.tensor.transpose(PS[:, 0, 0:P], BDA[:, :], ident))
            pe.wait_ge(prep_dve, PREP["BDAT"])
            prep(mm(PS[:, 1, 0:P], ones, BDAT[:, :]))
            pe.wait_ge(prep_dve, PREP["hat_rows"])
            prep(nc.tensor.transpose(PS[:, 2, 0:P], tmp[:, :], ident))
            pe.wait_ge(prep_dve, PREP["lap_rows"])
            prep(nc.tensor.transpose(PS[0:NODES, 3, 0:NODES], tmp2[0:NODES, 0:NODES], ident[0:NODES, 0:NODES]))

            def row_product(k):
                pe.wait_ge(hh_S, k + 1)
                mm(eb(0)[:, 0:NODES + 1], S[0:NODES, k % 2, 0:1].broadcast_to((NODES, P)),
                   ident[0:NODES, k:k + NODES + 1] if k + NODES + 1 <= P else None).then_inc(hh_row, 1)

            def av_product(k):
                pe.wait_ge(hh_v, k + 1)
                mm(eb(2)[:, 0:NODES], vcol[0:NODES, 0:1].broadcast_to((NODES, P)), S[0:NODES, k % 2, 1:NODES + 1])\
                    .then_inc(hh_av, 1)

            def eigen_products(lo):
                for k in range(lo, REFLECTIONS):
                    yield PACE_ROW
                    row_product(k)
                    yield PACE_AV
                    av_product(k)
                yield PACE
                pe.wait_ge(prep_dve, PREP["diagonals"])
                mm(eb(0)[:, 0:NODES], ones[0:NODES, :], EV[:, 0, 0:NODES])
                prep(mm(eb(0)[:, NODES:P], ones[0:NODES, :], EV[:, 1, 1:NODES + 1]))
                for n in range(ROUNDS):
                    yield PACE_GRID
                    pe.wait_ge(grid_cnt, n + 1)
                    mm(eb(2)[:, 0:1], C("fold"), sc[:, 3:4]).then_inc(grid_sum, 1)
                yield PACE_TWIST
                pe.wait_ge(prep_dve, PREP["V"])
                prep(nc.tensor.transpose(eb(0)[0:NODES, 0:NODES], Fq[0:NODES, 6, :], ident[0:NODES, 0:NODES]))
                pe.wait_ge(prep_pe, 6)
                prep(nc.tensor.transpose(eb(2)[0:NODES, 0:NODES], REC[NODES:P, :], ident[NODES:P, NODES:P]))
                yield PACE
                pe.wait_ge(prep_dve, PREP["VT"])
                VT, QT = EV[:, 2, 0:NODES], EV[:, 3, 0:NODES]
                mm(eb(0)[0:NODES, 0:NODES], QT, VT)
                prep(mm(eb(1)[0:NODES, 0:P], VT, EV[:, 3, :]))
                yield PACE
                pe.wait_ge(prep_dve, PREP["U"])
                U = EV[:, 4, 0:NODES]
                mm(eb(2)[0:NODES, 0:NODES], LS[:, :], U)
                prep(mm(eb(3)[0:NODES, 0:NODES], U, U))
                yield PACE
                pe.wait_ge(prep_dve, PREP["AU"])
                prep(mm(eb(0)[0:NODES, 0:NODES], U, EV[:, 6, 0:NODES]))
                yield PACE
                pe.wait_ge(prep_dve, PREP["ritz"])
                prep(mm(eb(1)[0:NODES, 0:NODES], ones[0:NODES, 0:NODES], EV[:, 9, 0:NODES]))
                yield PACE
                pe.wait_ge(prep_dve, PREP["I+E"])
                mm(eb(2)[:, 0:NODES], EV[:, 5, :], EV[:, 8, 0:NODES])
                prep(mm(eb(3)[:, 0:NODES], EV[:, 8, :], EV[:, 5, 0:NODES]))

            pe.wait_ge(prep_dve, PREP["S"])

            def agg(c):
                i, k = divmod(c, NK)
                pe.wait_ge(act_done[k], A_ACT.at(i, "norm"))
                if c >= 3:
                    pe.wait_ge(act_done[(c - 3) % NK], A_ACT.at((c - 3) // NK, "y"))
                for t in range(TPC):
                    j = mm(l0_banks(c)[:, 0, t * P:(t + 1) * P], T0[:, k, t * P:(t + 1) * P], BDHT[:, :])
                j.then_inc(pe_done[k], 1)

            def w1(c):
                i, k = divmod(c, NK)
                pe.wait_ge(act_done[k], A_ACT.at(i, "aggT"))
                for h in range(2):
                    j = mm(l0_banks(c)[:, h, :], W("w1T")[:, h * P:(h + 1) * P], T1[:, k, 0:CH])
                j.then_inc(pe_done[k], 1)

            def w2(c):
                i, k = divmod(c, NK)
                pe.wait_ge(act_done[k], B_ACT.at(i, "bn_relu"))
                if c >= 6:
                    pe.wait_ge(act_done[(c - 6) % NK], B_ACT.at((c - 6) // NK, "y"))
                for h in range(2):
                    j = mm(PS[:, c % 6, :], W("w2T")[:, h * P:(h + 1) * P], T1[:, k, h * CH:(h + 1) * CH],
                           start=(h == 0), stop=(h == 1))
                j.then_inc(pe_done[k], 1)

            for r in range(REFLECTED):
                n = r - LEAD
                m = n - L0_FIRST
                if n == 3:
                    pe.wait_ge(ld_w, 16)
                row_product(r)
                if n < L0_FIRST and is_chunk(n - 3):
                    w1(n - 3)
                if m >= 0 and is_chunk(2 * m - 2):
                    w2(2 * m - 2)
                av_product(r)
                if n < L0_FIRST and is_chunk(n - 2):
                    agg(n - 2)
                if m >= 0 and is_chunk(2 * m - 1):
                    w2(2 * m - 1)

            def tiles(b, k, lhs, rhs):
                for t in range(TPC):
                    j = mm(b[:, t * P:(t + 1) * P], lhs[:, t * P:(t + 1) * P], rhs)
                j.then_inc(pe_done[k], 1)

            small = eigen_products(REFLECTED)
            clock, due = [0.0], [next(small)]

            def send():
                pace = next(small, None)
                sent.append(clock[0])
                due[0] = None if pace is None else max(due[0], clock[0] - 1.0) + pace

            def spend(us, i=None, k=None, name=None):
                clock[0] += us
                if name:
                    there[i, k, name] = clock[0]
                while due[0] is not None and due[0] <= clock[0]:
                    send()

            PRODUCT = CH * 4 / 2400

            def turn(i, k):
                pe.wait_ge(act_done[k], C_ACT.at(i, "bn"))
                if i and k:
                    pe.wait_ge(dve_done[k - 1], C_DVE.at(i, "add"))
                for t in range(TPC):
                    j = nc.tensor.transpose(turn_bank(i, k)[:, t * P:(t + 1) * P], T1[:, k, t * P:(t + 1) * P], ident)
                j.then_inc(pe_done[k], 1)
                spend(0.5, i, k, "turn")

            def lstm(i):
                rank = [[], []]
                turned = 0
                for r, (p, s, part) in enumerate(LSTM):
                    for q in range(2):
                        x, n = lstm_in(H, q, p, s, part)
                        if r == 0:
                            for k in (2 * q, 2 * q + 1):
                                pe.wait_ge(act_done[k], C_ACT.at(i, "h"))
                        elif p > 1:
                            pe.wait_ge(pool_set[q], R_POOL.at(i, f"h{r - 1}"))
                        for g in gates(s):
                            m = len(rank[q])
                            rank[q].append(f"{g}{r}")
                            if m >= 3:
                                pe.wait_ge(act_set[q], R_ACT.at(i, rank[q][m - 3]))
                            G = PS[:, 3 * q + m % 3, 0:n]
                            j = mm(G, wT("wihT", p, g), x, stop=(s == 0))
                            if s:
                                j = mm(G, wT("whhT", p, g), LB[:, q, HP, 0:n], start=False)
                            j.then_inc(pe_set[q], 1)
                            spend(n * 4 * (1 + (s > 0)) / 2400)
                        if r and turned < NK and i + 1 < ITER:
                            turn(i + 1, turned)
                            turned += 1

            for k in range(NK):
                turn(0, k)
            spend(8.0)
            for i in range(ITER):
                for k in range(NK):
                    pe.wait_ge(act_done[k], C_ACT.at(i, "norm"))
                    if i:
                        pe.wait_ge(dve_done[k], C_DVE.at(i - 1, "add_h"))
                    tiles(l1_bank(k), k, T0[:, k, :], BDAT[:, :])
                    spend(PRODUCT)
                for k in range(NK):
                    pe.wait_ge(act_done[k], C_ACT.at(i, "aggT"))
                    tiles(l1_bank(k), k, T1[:, k, :], W("wg0"))
                    spend(PRODUCT, i, k, "g0")
                spend(GAP)
                for k in range(NK):
                    pe.wait_ge(act_done[k], C_ACT.at(i, "relu0"))
                    tiles(l1_bank(k), k, T0[:, k, :], BDAT[:, :])
                    spend(PRODUCT)
                for k in range(NK):
                    pe.wait_ge(act_done[k], C_ACT.at(i, "aggT2"))
                    mm(l1_bank(k), W("wg1"), T1[:, k, 0:CH]).then_inc(pe_done[k], 1)
                    spend(PRODUCT, i, k, "g1")
                spend(GAP)
                lstm(i)
                spend(GAP)
                for k in range(NK):
                    pe.wait_ge(pool_set[k // 2], R_POOL.start(i + 1))
                    for t in range(TPC):
                        j = nc.tensor.transpose(l1_bank(k)[:, t * P:(t + 1) * P],
                                                H[:, k * CH + t * P:k * CH + (t + 1) * P], ident)
                    j.then_inc(pe_done[k], 1)
                    spend(0.5, i, k, "turn_h")
            while due[0] is not None:
                clock[0] = max(clock[0], due[0])
                send()

            pe.wait_ge(prep_dve, PREP["all"])

            def last_products(i):
                for k in range(NK):
                    pe.wait_ge(act_done[k], D_ACT.at(i, "relu2b"))
                    for t in range(TPC):
                        for c in range(4):
                            j = mm(banks(k)[:, 1, t * P:(t + 1) * P], R2[:, k, c * CH + t * P:c * CH + (t + 1) * P],
                                   W("l3w3")[:, c * P:(c + 1) * P], start=(c == 0), stop=(c == 3))
                    j.then_inc(pe_done[k], 1)
                for k in range(NK):
                    pe.wait_ge(act_done[k], D_ACT.at(i, "s3"))
                    mm(banks(k)[:, 1, :], BDST[:, :], T1[:, k, CH:2 * CH]).then_inc(pe_done[k], 1)

            for i in range(ITER):
                for k in range(NK):
                    pe.wait_ge(act_done[k], D_ACT.at(i, "norm"))
                    if i:
                        pe.wait_ge(act_done[k], D_ACT.at(i - 1, "relu2b"))
                    else:
                        for c in range(NK):
                            pe.wait_ge(dve_done[c], C_DVE.end)
                    tiles(bank(k), k, T0[:, k, :], BDU[:, :])
                for k in range(NK):
                    pe.wait_ge(act_done[k], D_ACT.at(i, "aggT"))
                    mm(bank(k), W("l2w1"), T1[:, k, 0:CH]).then_inc(pe_done[k], 1)
                for k in range(NK):
                    pe.wait_ge(act_done[k], D_ACT.at(i, "hid"))
                    tiles(bank(k), k, T0[:, k, :], W("l2w2"))
                for k in range(NK):
                    pe.wait_ge(dve_done[k], D_DVE.at(i, "o"))
                    mm(bank(k), BDUT[:, :], T1[:, k, 0:CH]).then_inc(pe_done[k], 1)
                if i:
                    last_products(i - 1)
                for k in range(NK):
                    pe.wait_ge(act_done[k], D_ACT.at(i, "norm3"))
                    tiles(bank(k), k, T0[:, k, :], BDST[:, :])
                for k in range(NK):
                    pe.wait_ge(act_done[k], D_ACT.at(i, "mix1T"))
                    if i:
                        pe.wait_ge(dve_done[k], D_DVE.at(i - 1, "add3"))
                    for t in range(TPC):
                        j = mm(banks(k)[:, t // 2, (t % 2) * 256:(t % 2 + 1) * 256],
                               T1[:, k, t * P:(t + 1) * P], W("l3w1"))
                    j.then_inc(pe_done[k], 1)
                for k in range(NK):
                    pe.wait_ge(act_done[k], D_ACT.at(i, "relu1"))
                    for t in range(TPC):
                        for c in range(2):
                            j = mm(banks(k)[:, c, t * P:(t + 1) * P],
                                   R1[:, k, t * 256 + c * P:t * 256 + (c + 1) * P], BDST[:, :])
                    j.then_inc(pe_done[k], 1)
                for half, before in ((0, "mix2T"), (1, "relu2a")):
                    for k in range(NK):
                        pe.wait_ge(act_done[k], D_ACT.at(i, before))
                        for o in range(2):
                            for c in range(2):
                                j = mm(banks(k)[:, o, :],
                                       W("l3w2")[:, c * 512 + (2 * half + o) * P:c * 512 + (2 * half + o + 1) * P],
                                       A2[:, k, c * CH:(c + 1) * CH], start=(c == 0), stop=(c == 1))
                        j.then_inc(pe_done[k], 1)
            last_products(ITER - 1)

        @block.scalar
        def _(act):
            begin(act, act_done, act_set)

            def copy(k, dst, src, before, fn=ACT.Copy, **kw):
                act.wait_ge(pe_done[k], before)
                nc.scalar.activation(dst, src, fn, **kw).then_inc(act_done[k], 1)

            def norm_tiles(i, k, name, before, free):
                act.wait_ge(dve_done[k], before)
                act.wait_ge(pe_done[k], free)
                for t in range(TPC):
                    a = i * SG + k * CH + t * P
                    j = nc.scalar.activation(T0[:, k, t * P:(t + 1) * P], X[:, a:a + P], ACT.Relu,
                                             bias=shift[:, k, t:t + 1], scale=rstd[:, k, t:t + 1])
                j.then_inc(act_done[k], 1)

            for n in range(L0_FIRST):
                if n == 3:
                    act.wait_ge(ld_w, 16)
                if is_chunk(n - 3):
                    i, k = divmod(n - 3, NK)
                    copy(k, T1[:, k, 0:CH], l0_banks(n - 3)[:, 0, :], A_PE.at(i, "agg"))
                if is_chunk(n - 1):
                    i, k = divmod(n - 1, NK)
                    norm_tiles(i, k, "norm", A_DVE.at(i, "shift"), A_PE.start(i))
                if is_chunk(n - 3):
                    i, k = divmod(n - 3, NK)
                    act.wait_ge(pe_done[k], A_PE.at(i, "w1"))
                    for h in range(2):
                        j = nc.scalar.activation(Y1[:, h, (n - 3) * CH:(n - 2) * CH], l0_banks(n - 3)[:, h, :],
                                                 ACT.Identity, bias=W("b1")[:, h:h + 1])
                    j.then_inc(act_done[k], 1)
            act.wait_ge(bn1_ready, 1)
            for m in range(L0_SECOND - 1):
                for c in (2 * m, 2 * m + 1):
                    if is_chunk(c):
                        i, k = divmod(c, NK)
                        act.wait_ge(pe_done[k], B_PE.start(i))
                        for h in range(2):
                            j = nc.scalar.activation(T1[:, k, h * CH:(h + 1) * CH], Y1[:, h, c * CH:(c + 1) * CH],
                                                     ACT.Relu, bias=bnv[:, 6 + h:7 + h], scale=bnv[:, 4 + h:5 + h])
                        j.then_inc(act_done[k], 1)
                for c in (2 * m - 2, 2 * m - 1):
                    if is_chunk(c):
                        i, k = divmod(c, NK)
                        copy(k, Y2[:, c * CH:(c + 1) * CH], PS[:, c % 6, :], B_PE.at(i, "w2"), ACT.Identity,
                             bias=W("b2"))
            act.wait_ge(bn2_ready, 1)

            def bn(i):
                for k in range(NK):
                    act.wait_ge(pe_done[k], B_PE.end if i == 0 else C_PE.at(i - 1, "g1"))
                    nc.scalar.activation(T1[:, k, 0:CH], Y2[:, i * SG + k * CH:i * SG + (k + 1) * CH], ACT.Identity,
                                         bias=bnv[:, 13:14], scale=bnv[:, 12:13]).then_inc(act_done[k], 1)

            def norm(i):
                act.wait_ge(ln_ready, i + 1)
                for k in range(NK):
                    if i:
                        act.wait_ge(pe_done[k], C_PE.at(i - 1, "agg2"))
                    for t in range(TPC):
                        a = i * SG + k * CH + t * P
                        j = nc.scalar.activation(T0[:, k, t * P:(t + 1) * P], X[:, a:a + P], ACT.Relu,
                                                 bias=shift[:, k, t:t + 1], scale=rstd[:, k, t:t + 1])
                    j.then_inc(act_done[k], 1)

            bn(0)
            norm(0)
            for i in range(ITER):
                for k in range(NK):
                    copy(k, T1[:, k, 0:CH], l1_bank(k), C_PE.at(i, "agg"))
                for k in range(NK):
                    act.wait_ge(dve_done[k], C_DVE.at(i, "bias0"))
                    nc.scalar.activation(T0[:, k, :], T1[:, k, CH:2 * CH], ACT.Relu).then_inc(act_done[k], 1)
                for k in range(NK):
                    copy(k, T1[:, k, 0:CH], l1_bank(k), C_PE.at(i, "agg2"))
                for k in range(NK):
                    act.wait_ge(dve_done[k], C_DVE.at(i, "bias1"))
                    nc.scalar.activation(H[:, k * CH:(k + 1) * CH], T1[:, k, CH:2 * CH], ACT.Relu)\
                        .then_inc(act_done[k], 1)
                if i + 1 < ITER:
                    bn(i + 1)
                rank = [0, 0]
                for r, (p, s, part) in enumerate(LSTM):
                    if r == NORM_ROUND and i + 1 < ITER:
                        norm(i + 1)
                    for q in range(2):
                        _, n = lstm_in(H, q, p, s, part)
                        act.wait_ge(pool_set[q], R_POOL.at(i, f"h{r - 1}") if r else R_POOL.start(i))
                        for g in gates(s):
                            act.wait_ge(pe_set[q], R_PE.at(i, f"{g}{r}"))
                            nc.scalar.activation(LB[:, q, {"i": I_, "g": G_, "f": F_, "o": O_}[g], 0:n],
                                                 PS[:, 3 * q + rank[q] % 3, 0:n],
                                                 ACT.Tanh if g == "g" else ACT.Sigmoid,
                                                 bias=lbias[:, (p - 1) * 4 + GATE[g]:(p - 1) * 4 + GATE[g] + 1])\
                                .then_inc(act_set[q], 1)
                            rank[q] += 1
                        act.wait_ge(pool_set[q], R_POOL.at(i, f"c{r}" if s else f"ig{r}"))
                        nc.scalar.activation(LB[:, q, I_, 0:n], LB[:, q, CELL, 0:n], ACT.Tanh).then_inc(act_set[q], 1)
            def both(k):
                return banks(k).rearrange("p b n -> p (b n)")

            for k in range(NK):
                norm_tiles(0, k, "norm", D_DVE.at(0, "shift"), C_PE.end)
            for i in range(ITER):
                for k in range(NK):
                    copy(k, T1[:, k, 0:CH], bank(k), D_PE.at(i, "agg"))
                for k in range(NK):
                    copy(k, T0[:, k, :], bank(k), D_PE.at(i, "w1"), ACT.Relu, bias=W("l2b1"))
                for k in range(NK):
                    if i:
                        copy(k, T1[:, k, CH:2 * CH], banks(k)[:, 1, :], D_PE.at(i - 1, "s3"))
                    norm_tiles(i, k, "norm3", D_DVE.at(i, "shift3"), D_PE.at(i, "w2"))
                for k in range(NK):
                    copy(k, T1[:, k, 0:CH], bank(k), D_PE.at(i, "mix1"))
                for k in range(NK):
                    copy(k, R1[:, k, :], both(k), D_PE.at(i, "s1"), ACT.Relu)
                for k in range(NK):
                    copy(k, A2[:, k, :], both(k), D_PE.at(i, "mix2"))
                for k in range(NK):
                    copy(k, R2[:, k, 0:1024], both(k), D_PE.at(i, "s2a"), ACT.Relu)
                for k in range(NK):
                    copy(k, R2[:, k, 1024:2048], both(k), D_PE.at(i, "s2b"), ACT.Relu)
                    if i + 1 < ITER:
                        norm_tiles(i + 1, k, "norm", D_DVE.at(i + 1, "shift"), D_PE.at(i, "mix1"))
            for k in range(NK):
                copy(k, T1[:, k, CH:2 * CH], banks(k)[:, 1, :], D_PE.at(ITER - 1, "s3"))

        @block.gpsimd
        def _(pool):
            begin(pool, pool_done, pool_set)
            mh = C("minus_half")

            def root(ap, out=None, e=None):
                o = ap if out is None else out
                return nc.gpsimd.tensor_tensor(o, ap, mh[:, 0:1] if e is None else e, ALU.pow)

            pool.wait_ge(ld_cst, 16)
            pool.wait_ge(degree, 1)
            nc.gpsimd.tensor_tensor(col[:, 4:6], col[:, 4:6], mh[:, 0:2], ALU.pow).then_inc(degree_root, 1)

            def layer_norm_roots(i, k, st, dst, sfx=""):
                pool.wait_ge(dve_done[k], dst.at(i, "aggr" + sfx))
                nc.gpsimd.tensor_scalar(rstd[:, k, :], mv[:, k, :, 1], EPS, None, ALU.add).then_inc(pool_done[k], 1)
                pool.wait_ge(pool_done[k], st.at(i, "var" + sfx))
                nc.gpsimd.tensor_tensor(rstd[:, k, :], rstd[:, k, :], mh[:, 0:TPC], ALU.pow).then_inc(pool_done[k], 1)

            for r in range(REFLECTED):
                pool.wait_ge(hh_norm2, r + 1)
                root(sc[:, 2:3], sc[:, 3:4], C("half")).then_inc(hh_norm, 1)
                if is_chunk(r - LEAD):
                    layer_norm_roots((r - LEAD) // NK, (r - LEAD) % NK, A_POOL, A_DVE)

            def product(q, name, out, a, b, op=ALU.mult):
                nc.gpsimd.tensor_tensor(out, a, b, op).then_inc(pool_set[q], 1)

            for i in range(ITER):
                for r, (p, s, part) in enumerate(LSTM):
                    for q in range(2):
                        place, n = lstm_in(H, q, p, s, part)
                        ig, gg, ff, oo, cell, hp = (LB[:, q, b, 0:n] for b in (I_, G_, F_, O_, CELL, HP))
                        pool.wait_ge(act_set[q], R_ACT.at(i, f"g{r}"))
                        product(q, "ig", gg if s else cell, ig, gg)
                        if s:
                            pool.wait_ge(act_set[q], R_ACT.at(i, f"f{r}"))
                            product(q, "fc", cell, cell, ff)
                            pool.wait_ge(pool_set[q], R_POOL.at(i, f"fc{r}"))
                            product(q, "c", cell, cell, gg, ALU.add)
                        pool.wait_ge(act_set[q], R_ACT.at(i, f"tanh{r}"))
                        if s < p - 1:
                            product(q, "h", hp, ig, oo)
                        elif p == 1:
                            product(q, "h", place, ig, oo)
                        else:
                            product(q, "h", place, ig.rearrange("p (b w) -> p b w", b=SGR),
                                    oo.rearrange("p (b w) -> p b w", b=SGR))
            for i in range(ITER + 1):
                for k in range(NK):
                    if i:
                        layer_norm_roots(i - 1, k, D_POOL, D_DVE, "3")
                for k in range(NK):
                    if i < ITER:
                        layer_norm_roots(i, k, D_POOL, D_DVE)

        @block.vector
        def _(dve):
            begin(dve, dve_done)
            v = nc.vector
            done = [0]
            l1, dclock, taken = [None], [0.0], [0]
            l1_next = [None]

            def before_next():
                return l1_next[0] is not None and (taken[0] >= len(sent) or l1_next[0] <= sent[taken[0]])

            def beside_l1():
                dclock[0] += DVE_STEP
                if before_next() and l1_next[0] <= dclock[0]:
                    l1_next[0] = next(l1[0], None)

            def small_product():
                if l1[0] is None:
                    return
                while before_next():
                    l1_next[0] = next(l1[0], None)
                dclock[0] = sent[taken[0]] + 0.3
                taken[0] += 1

            def step(ins, name=None):
                done[0] += 1
                ins.then_inc(prep_dve, 1)
                beside_l1()
                dve.wait_ge(prep_dve, done[0])
                if name:
                    assert PREP[name] == done[0], (name, done[0])

            def c1(n):
                return col[:, n:n + 1]

            def s1(n):
                return sc[:, n:n + 1]

            ident, blocks = C("ident"), C("blocks")
            pair = [P, 2, NODES]

            dve.wait_ge(ld_adj, 32)
            dve.wait_ge(ld_cst, 16)
            step(v.tensor_tensor(BDA[:, :].rearrange("p (b n) -> p b n", b=2),
                                 AA[:, :].unsqueeze(1).broadcast_to(pair),
                                 blocks.rearrange("p (b n) -> p b n", b=2), ALU.mult), "BDA")
            dve.wait_ge(prep_pe, 1)
            step(v.tensor_copy(BDAT[:, :], PS[:, 0, 0:P]), "BDAT")
            step(v.tensor_tensor(BDST[:, :], BDAT[:, :], BDAT[:, :], ALU.mult))
            step(v.tensor_reduce(c1(0), BDA[:, :], AX, ALU.add))
            step(v.tensor_reduce(c1(1), BDAT[:, :], AX, ALU.add))
            step(v.tensor_tensor_reduce(tmp[:, :], BDA[:, :], ident, 1.0, 0.0, ALU.mult, ALU.add, c1(2)))
            step(v.scalar_tensor_tensor(c1(3), c1(0), c1(1), c1(2), ALU.add, ALU.subtract))
            step(v.tensor_scalar(c1(4), c1(3), 1.0, None, ALU.add))
            step(v.tensor_scalar(c1(5), c1(3), TINY, None, ALU.max))
            v.sem_inc(degree, 1)
            dve.wait_ge(degree_root, 1)
            step(v.tensor_tensor(tmp[:, :], BDA[:, :], ident, ALU.add))
            step(v.tensor_scalar(tmp[:, :], tmp[:, :], c1(4), None, ALU.mult), "hat_rows")
            dve.wait_ge(prep_pe, 3)
            step(v.tensor_scalar(BDHT[:, :], PS[:, 2, 0:P], c1(4), None, ALU.mult))
            step(v.tensor_scalar(c1(6), c1(3), 0.0, None, ALU.is_gt))
            step(v.tensor_tensor(c1(5), c1(5), c1(6), ALU.mult))
            n64 = slice(0, NODES)
            step(v.tensor_scalar(tmp2[n64, 0:NODES], ident[n64, n64], col[n64, 3:4], 2.0, ALU.mult, ALU.mult))
            step(v.tensor_tensor(tmp2[n64, 0:NODES], tmp2[n64, 0:NODES], BDA[n64, n64], ALU.subtract))
            step(v.tensor_tensor(tmp2[n64, 0:NODES], tmp2[n64, 0:NODES], BDAT[n64, n64], ALU.subtract))
            step(v.tensor_scalar(tmp2[n64, 0:NODES], tmp2[n64, 0:NODES], col[n64, 5:6], None, ALU.mult), "lap_rows")
            dve.wait_ge(prep_pe, 4)
            step(v.tensor_scalar(LS[:, :], PS[n64, 3, n64], col[n64, 5:6], 0.5, ALU.mult, ALU.mult))
            step(v.memset(S[:, :, :], 0.0))
            step(v.memset(EV[:, 1, NODES:NODES + 1], 0.0))
            step(v.tensor_copy(S[n64, 0, 0:NODES], LS[:, :]))
            step(v.tensor_copy(S[NODES:P, 0, 0:NODES], ident[NODES:P, NODES:P]), "S")
            v.sem_inc(hh_S, 1)
            alpha, r2, n2, norm = xrow[:, 0:1], s1(1), s1(2), s1(3)
            sg, xm, esg, hd, nc_, guard, t_, m_, nc2, pc, y_ = (s1(n) for n in range(4, 15))
            hh = [0]

            def op(ins):
                hh[0] += 1
                ins.then_inc(hh_ops, 1)

            def sync_hh(back=0, beside=iter(())):
                next(beside, None)
                beside_l1()
                dve.wait_ge(hh_ops, hh[0] - back)

            I32 = mybir.dt.int32

            def inverse_root(x, y, do, wait):
                do(v.tensor_scalar(y.bitcast(I32), x.bitcast(I32), 1, None, ALU.logical_shift_right))
                wait()
                do(v.tensor_scalar(y.bitcast(I32), y.bitcast(I32), -1.0, float(0x5F3759DF), ALU.mult, ALU.add))
                wait()
                return (3.0, 12.0, 768.0)

            def reflection(k, by_pool, beside=iter(())):
                def sync(back=0):
                    sync_hh(back, beside)

                A, B = S[:, k % 2, :], S[:, 1 - k % 2, :]
                next(beside, None)
                next(beside, None)
                small_product()
                dve.wait_ge(hh_row, k + 1)
                op(v.tensor_copy(xrow[:, :], eb(0)[:, 1:NODES + 1]))
                op(v.tensor_tensor(xm, A[:, 0:1], C("below")[:, k:k + 1], ALU.mult))
                sync(1)
                op(v.tensor_tensor_reduce(junk[:, 1:NODES], xrow[:, 1:NODES], xrow[:, 1:NODES], 1.0, 0.0,
                                          ALU.mult, ALU.add, r2))
                op(v.tensor_scalar(sg, alpha, 0.0, 2.0, ALU.is_lt, ALU.mult))
                op(v.tensor_copy(REC[:, k:k + 1], A[:, 0:1]))
                sync(2)
                op(v.scalar_tensor_tensor(n2, alpha, alpha, r2, ALU.mult, ALU.add))
                if by_pool:
                    sync()
                    v.sem_inc(hh_norm2, 1)
                else:
                    sync(2)
                op(v.tensor_scalar(sg, sg, -1.0, None, ALU.add))
                op(v.tensor_scalar(vrow[:, 1:NODES], xrow[:, 1:NODES], -1.0, None, ALU.mult))
                op(v.tensor_scalar(guard, r2, 0.0, -1e30, ALU.is_le, ALU.mult))
                sync(2)
                op(v.tensor_scalar(esg, C("next")[:, k:k + 1], sg, None, ALU.mult))
                sync(1)
                op(v.tensor_scalar(guard, guard, -1.0, None, ALU.add))
                if by_pool:
                    dve.wait_ge(hh_norm, k + 1)
                else:
                    for c in inverse_root(n2, y_, op, sync):
                        op(v.scalar_tensor_tensor(m_, y_, y_, n2, ALU.mult, ALU.mult))
                        sync()
                        op(v.scalar_tensor_tensor(y_, m_, -c, y_, ALU.add, ALU.mult))
                        sync()
                    op(v.tensor_scalar(norm, y_, n2, -1.0 / 8192, ALU.mult, ALU.mult))
                sync()
                v.scalar_tensor_tensor(vcol[:, :], esg, norm, xm, ALU.mult, ALU.subtract).then_inc(hh_v, 1)
                op(v.scalar_tensor_tensor(vrow[:, 0:1], norm, sg, alpha, ALU.mult, ALU.subtract))
                sync()
                op(v.scalar_tensor_tensor(hd, norm, sg, vrow[:, 0:1], ALU.mult, ALU.mult))
                op(v.tensor_tensor_reduce(junk[:, :], A[:, 1:NODES + 1], vrow[:, :], 1.0, 0.0, ALU.mult,
                                          ALU.add, pc))
                sync(1)
                op(v.tensor_scalar(hd, hd, TINY, guard, ALU.max, ALU.mult))
                sync()
                op(v.reciprocal(nc_, hd))
                next(beside, None)
                small_product()
                dve.wait_ge(hh_av, k + 1)
                op(v.tensor_tensor_reduce(junk[:, :], vrow[:, :], eb(2)[:, 0:NODES], 1.0, 0.0, ALU.mult,
                                          ALU.add, t_))
                sync(1)
                op(v.tensor_tensor(nc2, nc_, nc_, ALU.mult))
                op(v.tensor_scalar(prow[:, :], eb(2)[:, 0:NODES], nc_, None, ALU.mult))
                op(v.tensor_scalar(wcol[:, :], pc, nc_, None, ALU.mult))
                sync(2)
                op(v.tensor_scalar(m_, t_, nc2, None, ALU.mult))
                sync(2)
                op(v.scalar_tensor_tensor(B[:, 0:NODES], prow[:, :], vcol[:, :], A[:, 1:NODES + 1], ALU.mult,
                                          ALU.add))
                sync(1)
                op(v.scalar_tensor_tensor(wcol[:, :], vcol[:, :], m_, wcol[:, :], ALU.mult, ALU.add))
                sync()
                v.scalar_tensor_tensor(B[:, 0:NODES], vrow[:, :], wcol[:, :], B[:, 0:NODES], ALU.mult, ALU.add)\
                    .then_inc(hh_S, 1)

            def tail():
                dve.wait_ge(hh_S, REFLECTIONS + 1)
                step(v.tensor_copy(REC[:, REFLECTIONS:NODES], S[:, REFLECTIONS % 2, 0:2]))

                step(v.tensor_tensor(EV[:, 0, 0:NODES], REC[n64, :], ident[n64, n64], ALU.mult))
                step(v.tensor_tensor(EV[:, 1, 0:NODES], REC[n64, :], C("super")[n64, :], ALU.mult), "diagonals")
                small_product()
                dve.wait_ge(prep_pe, 5)
                d, e, ne2, ne, t4, t5 = (Trow[:, n, :] for n in range(6))
                step(v.tensor_copy(Trow[:, 0:2, :], eb(0)[:, 0:P].rearrange("p (a n) -> p a n", a=2)))
                step(v.tensor_scalar(ne, e, -1.0, None, ALU.mult))
                step(v.tensor_tensor(ne2, ne, e, ALU.mult))
                step(v.tensor_scalar(ne2, ne2, -TINY, None, ALU.min))
                step(v.tensor_tensor(t4, ne, e, ALU.max))
                step(v.tensor_scalar(t5, d, -1.0, None, ALU.mult))
                step(v.tensor_tensor(t5, t5, d, ALU.max))
                step(v.tensor_reduce(s1(20), t5, AX, ALU.max))
                step(v.tensor_tensor(t5, t5, t4, ALU.add))
                step(v.tensor_tensor(t5[:, 1:NODES], t5[:, 1:NODES], t4[:, 0:NODES - 1], ALU.add))
                step(v.tensor_reduce(s1(0), t5, AX, ALU.max))
                step(v.tensor_scalar(s1(1), s1(0), -1.0001, -TINY, ALU.mult, ALU.add))
                step(v.tensor_scalar(s1(2), s1(1), -2.0 / (2 * M + 1), None, ALU.mult), "bound")

                GOPS = 8 + 4 * (HALF - 1)
                for r in range(ROUNDS):
                    g = [0]

                    def gop(ins):
                        g[0] += 1
                        ins.then_inc(grid_ops, 1)

                    def gsync(back=0):
                        beside_l1()
                        dve.wait_ge(grid_ops, r * GOPS + (g[0] - back))

                    gop(v.tensor_scalar(xg[:, :], C("grid"), s1(2), s1(1), ALU.mult, ALU.add))
                    gsync()
                    gop(v.tensor_tensor(Qh[:, :, :], d.unsqueeze(2).broadcast_to([P, NODES, M]),
                                        xg[:, :].unsqueeze(1).broadcast_to([P, NODES, M]), ALU.subtract))
                    gsync()
                    for i in range(HALF):
                        j = NODES - 1 - i
                        if i:
                            gsync(1)
                        gop(v.reciprocal(rq[:, 0, :], Qh[:, i, :]))
                        if i:
                            gsync(1)
                        if i < HALF - 1:
                            gop(v.reciprocal(rq[:, 1, :], Qh[:, j, :]))
                            gsync(1)
                        else:
                            gsync()
                        gop(v.scalar_tensor_tensor(Qh[:, i + 1, :], rq[:, 0, :], ne2[:, i:i + 1], Qh[:, i + 1, :],
                                                   ALU.mult, ALU.add))
                        if i < HALF - 1:
                            gsync(1)
                            gop(v.scalar_tensor_tensor(Qh[:, j - 1, :], rq[:, 1, :], ne2[:, j - 1:j], Qh[:, j - 1, :],
                                                       ALU.mult, ALU.add))
                    gsync()
                    gop(v.tensor_scalar(Qh[:, :, :], Qh[:, :, :], 0.0, None, ALU.is_lt))
                    gsync()
                    gop(v.tensor_reduce(cnt[:, :], Qh[:, :, :].rearrange("p i m -> p m i"), AX, ALU.add))
                    gsync()
                    v.tensor_scalar(xg[:, :], cnt[:, :], C("lane"), None, ALU.is_le, ALU.add, accum_out=s1(3))\
                        .then_inc(grid_cnt, 1)
                    small_product()
                    dve.wait_ge(grid_sum, r + 1)
                    gop(v.scalar_tensor_tensor(s1(1), eb(2)[:, 0:1], s1(2), s1(1), ALU.mult, ALU.add))
                    gsync()
                    gop(v.tensor_scalar(s1(2), s1(2), 1.0 / (2 * M + 1), None, ALU.mult))
                    gsync()
                    assert g[0] == GOPS, g[0]
                step(v.tensor_scalar(s1(2), s1(2), (2 * M + 1) / 2.0, None, ALU.mult))
                step(v.tensor_tensor(s1(1), s1(1), s1(2), ALU.add))

                top, bot, a, gam, hot, zt, zb, mul = (Fq[:, n, :] for n in range(8))
                step(v.tensor_scalar(a, d, s1(1), None, ALU.subtract))
                step(v.tensor_copy(top, a))
                step(v.tensor_copy(bot, a))
                for i in range(NODES - 1):
                    j = NODES - 1 - i
                    beside_l1()
                    if i:
                        dve.wait_ge(twist_ops, 4 * i - 1)
                    v.reciprocal(s1(14), top[:, i:i + 1]).then_inc(twist_ops, 1)
                    if i:
                        dve.wait_ge(twist_ops, 4 * i)
                    v.reciprocal(s1(15), bot[:, j:j + 1]).then_inc(twist_ops, 1)
                    beside_l1()
                    dve.wait_ge(twist_ops, 4 * i + 1)
                    v.scalar_tensor_tensor(top[:, i + 1:i + 2], s1(14), ne2[:, i:i + 1], top[:, i + 1:i + 2],
                                           ALU.mult, ALU.add).then_inc(twist_ops, 1)
                    dve.wait_ge(twist_ops, 4 * i + 2)
                    v.scalar_tensor_tensor(bot[:, j - 1:j], s1(15), ne2[:, j - 1:j], bot[:, j - 1:j],
                                           ALU.mult, ALU.add).then_inc(twist_ops, 1)
                dve.wait_ge(twist_ops, 4 * (NODES - 1))
                step(v.tensor_tensor(gam, top, bot, ALU.add))
                step(v.tensor_tensor(gam, gam, a, ALU.subtract))
                step(v.tensor_tensor(gam, gam, gam, ALU.mult))
                step(v.tensor_reduce(s1(14), gam, AX, ALU.min))
                step(v.tensor_scalar(hot, gam, s1(14), None, ALU.is_equal))
                step(v.reciprocal(mul, top))
                step(v.tensor_tensor(mul, mul, ne, ALU.mult))
                step(v.tensor_scalar(mul, mul, 1e18, -1e18, ALU.min, ALU.max))
                step(v.tensor_tensor_scan(zt[:, ::-1], mul[:, ::-1], hot[:, ::-1], 0.0, ALU.mult, ALU.add))
                step(v.reciprocal(mul, bot))
                step(v.tensor_tensor(mul[:, 1:NODES], mul[:, 1:NODES], ne[:, 0:NODES - 1], ALU.mult))
                step(v.tensor_scalar(mul, mul, 1e18, -1e18, ALU.min, ALU.max))
                step(v.tensor_tensor_scan(zb, mul, hot, 0.0, ALU.mult, ALU.add))
                step(v.tensor_tensor(zb, zb, zt, ALU.add))
                step(v.tensor_tensor(zb, zb, hot, ALU.subtract))
                step(v.tensor_tensor_reduce(junk[:, :], zb, zb, 1.0, 0.0, ALU.mult, ALU.add, s1(16)))
                step(v.tensor_tensor_reduce(junk[:, 0:HALF], zb[:, 0:HALF], zb[:, 0:HALF], 1.0, 0.0, ALU.mult, ALU.add,
                                            s1(17)))
                for n, cut in ((21, HALF), (22, HALF // 2), (23, HALF + HALF // 2)):
                    step(v.tensor_scalar(s1(24), e[:, cut - 1:cut], 0.0, 2.0, ALU.is_ge, ALU.mult))
                    step(v.tensor_scalar(s1(24), s1(24), -1.0, None, ALU.add))
                    step(v.scalar_tensor_tensor(s1(n), zb[:, cut:cut + 1], s1(24), zb[:, cut - 1:cut], ALU.mult, ALU.add))
                step(v.tensor_scalar(s1(18), s1(16), 0.5, None, ALU.mult))
                step(v.tensor_tensor(s1(18), s1(17), s1(18), ALU.is_gt))
                step(v.tensor_tensor(s1(25), s1(22), s1(23), ALU.subtract))
                step(v.scalar_tensor_tensor(s1(25), s1(25), s1(18), s1(23), ALU.mult, ALU.add))
                step(v.tensor_scalar(s1(26), s1(20), 8 * 2.0 ** -24 / 1.8, None, ALU.mult))
                step(v.tensor_scalar(s1(26), s1(26), s1(26), s1(16), ALU.mult, ALU.mult))
                step(v.tensor_scalar(s1(27), s1(21), e[:, HALF - 1:HALF], None, ALU.mult))
                step(v.tensor_tensor(s1(27), s1(27), s1(27), ALU.mult))
                step(v.tensor_tensor(s1(27), s1(27), s1(26), ALU.is_gt))
                step(v.tensor_tensor(s1(28), s1(21), s1(25), ALU.subtract))
                step(v.scalar_tensor_tensor(s1(28), s1(28), s1(27), s1(25), ALU.mult, ALU.add))
                step(v.tensor_scalar(s1(28), s1(28), 0.0, 2.0, ALU.is_le, ALU.mult))
                for c in inverse_root(s1(16), s1(29), step, lambda: None):
                    step(v.scalar_tensor_tensor(s1(30), s1(29), s1(29), s1(16), ALU.mult, ALU.mult))
                    step(v.scalar_tensor_tensor(s1(29), s1(30), -c, s1(29), ALU.add, ALU.mult))
                step(v.tensor_scalar(s1(29), s1(29), -1.0 / 8192, None, ALU.mult))
                step(v.scalar_tensor_tensor(s1(29), s1(28), -1.0, s1(29), ALU.add, ALU.mult))
                step(v.tensor_scalar(zb, zb, s1(29), None, ALU.mult), "V")

                def ev(n, m=NODES):
                    return EV[:, n, 0:m]

                def dup(n):
                    return EV[:, n, :].rearrange("p (b n) -> p b n", b=2)

                def twice(ap):
                    return ap.unsqueeze(1).broadcast_to([NODES, 2, NODES])

                small_product()
                dve.wait_ge(prep_pe, 7)
                step(v.tensor_copy(ev(2), eb(0)[n64, n64]))
                step(v.tensor_copy(dup(3), twice(eb(2)[n64, n64])), "VT")
                small_product()
                dve.wait_ge(prep_pe, 8)
                step(v.tensor_copy(ev(4), eb(0)[n64, n64]))
                step(v.tensor_copy(ev(5, P), eb(1)[n64, 0:P]), "U")
                small_product()
                dve.wait_ge(prep_pe, 9)
                step(v.tensor_copy(ev(6), eb(2)[n64, n64]))
                step(v.tensor_tensor_reduce(ev(9), eb(3)[n64, n64], ident[n64, n64], 1.0, 0.0, ALU.mult, ALU.add,
                                            sc[n64, 30:31]))
                step(v.tensor_tensor(ev(7), ident[n64, n64], eb(3)[n64, n64], ALU.subtract), "AU")
                small_product()
                dve.wait_ge(prep_pe, 10)
                step(v.tensor_copy(ev(8), eb(0)[n64, n64]))
                step(v.tensor_tensor_reduce(ev(9), ev(8), ident[n64, n64], 1.0, 0.0, ALU.mult, ALU.add, sc[n64, 31:32]))
                step(v.reciprocal(sc[n64, 30:31], sc[n64, 30:31]))
                step(v.tensor_tensor(sc[n64, 31:32], sc[n64, 31:32], sc[n64, 30:31], ALU.mult))
                step(v.tensor_scalar(ev(9), ident[n64, n64], sc[n64, 31:32], None, ALU.mult), "ritz")
                small_product()
                dve.wait_ge(prep_pe, 11)
                lam = eb(1)[n64, n64]
                step(v.tensor_tensor(ev(10), ev(7), lam, ALU.mult))
                step(v.tensor_tensor(ev(10), ev(10), ev(8), ALU.add))
                step(v.tensor_scalar(ev(11), lam, sc[n64, 31:32], None, ALU.subtract))
                step(v.tensor_tensor(ev(8), ev(11), ev(11), ALU.mult))
                step(v.tensor_scalar(ev(8), ev(8), 1e-9, None, ALU.is_gt))
                step(v.scalar_tensor_tensor(ev(11), ev(11), 1.0, ev(8), ALU.add, ALU.subtract))
                step(v.reciprocal(ev(11), ev(11)))
                step(v.tensor_tensor(ev(10), ev(10), ev(11), ALU.mult))
                step(v.tensor_scalar(ev(7), ev(7), 0.5, None, ALU.mult))
                step(v.tensor_tensor(ev(10), ev(10), ev(7), ALU.subtract))
                step(v.tensor_tensor(ev(10), ev(10), ev(8), ALU.mult))
                step(v.tensor_tensor(ev(10), ev(10), ev(7), ALU.add))
                step(v.tensor_tensor(dup(8), twice(ev(10)), twice(ident[n64, n64]), ALU.add), "I+E")
                step(v.memset(BDU[:, :], 0.0))
                step(v.memset(BDUT[:, :], 0.0))
                small_product()
                dve.wait_ge(prep_pe, 12)
                for b in range(2):
                    h = slice(b * NODES, (b + 1) * NODES)
                    step(v.tensor_copy(BDU[h, h], eb(2)[h, n64]))
                    step(v.tensor_copy(BDUT[h, h], eb(3)[h, n64]), "all" if b else None)

            ln = [0]

            def layer_norms(i, at):
                def do(ins):
                    ln[0] += 1
                    ins.then_inc(ln_ops, 1)

                def later():
                    at[0] += LN_STEP if i else 0.1
                    return at[0]

                def wait():
                    dve.wait_ge(ln_ops, ln[0])

                for k in range(NK):
                    dve.wait_ge(dve_done[k], C_DVE.at(i, "add"))
                    for t in range(TPC):
                        a = i * SG + k * CH + t * P
                        yield later()
                        do(v.bn_stats(stats[:, k, t, :], X[:, a:a + P]))
                yield later()
                wait()
                for k in range(NK):
                    for t in range(TPC):
                        yield later()
                        do(v.bn_aggr(mv[:, k, t, :], stats[:, k, t, :]))
                yield later()
                wait()
                dve.wait_ge(act_done[NK - 1], B_ACT.end if i == 0 else C_ACT.at(i - 1, "norm"))
                x, y, a = lnv[:, 0, :], lnv[:, 1, :], lnv[:, 2, :]
                mean, var = (mv[:, :, :, n].rearrange("p k t -> p (k t)") for n in range(2))
                do(v.tensor_scalar(x, var, EPS, None, ALU.add))
                yield later()
                wait()
                for c in inverse_root(x, y, do, wait):
                    do(v.tensor_tensor(a, y, y, ALU.mult))
                    yield later()
                    wait()
                    do(v.tensor_tensor(a, a, x, ALU.mult))
                    yield later()
                    wait()
                    do(v.scalar_tensor_tensor(y, a, -c, y, ALU.add, ALU.mult))
                    yield later()
                    wait()
                do(v.tensor_scalar(rstd[:, :, :].rearrange("p k t -> p (k t)"), y, -1.0 / 8192, None, ALU.mult))
                yield later()
                wait()
                v.scalar_tensor_tensor(shift[:, :, :].rearrange("p k t -> p (k t)"), mean, -1.0,
                                       rstd[:, :, :].rearrange("p k t -> p (k t)"), ALU.mult, ALU.mult)\
                    .then_inc(ln_ready, 1)

            def stats_of(i, k, st, sfx=""):
                for t in range(TPC):
                    a = i * SG + k * CH + t * P
                    j = v.bn_stats(stats[:, k, t, :], X[:, a:a + P])
                    if t < TPC - 1:
                        yield
                j.then_inc(dve_done[k], 1)
                yield
                dve.wait_ge(dve_done[k], st.at(i, "stats" + sfx))
                for t in range(TPC):
                    j = v.bn_aggr(mv[:, k, t, :], stats[:, k, t, :])
                    if t < TPC - 1:
                        yield
                j.then_inc(dve_done[k], 1)
                yield

            def shift_of(i, k, pst, sfx=""):
                dve.wait_ge(pool_done[k], pst.at(i, "rstd" + sfx))
                v.scalar_tensor_tensor(shift[:, k, :], mv[:, k, :, 0], -1.0, rstd[:, k, :], ALU.mult, ALU.mult)\
                    .then_inc(dve_done[k], 1)

            def l0_first(n):
                if is_chunk(n - 1):
                    shift_of((n - 1) // NK, (n - 1) % NK, A_POOL)
                    yield

                def hidden_stats(h):
                    c = n - 4
                    dve.wait_ge(act_done[c % NK], A_ACT.at(c // NK, "y"))
                    v.bn_stats(ST1[:, h, c, :], Y1[:, h, c * CH:(c + 1) * CH]).then_inc(hidden_seen, 1)

                if is_chunk(n - 4):
                    hidden_stats(0)
                    yield
                if is_chunk(n):
                    i, k = divmod(n, NK)
                    if i:
                        dve.wait_ge(act_done[k], A_ACT.at(i - 1, "norm"))
                    yield from stats_of(i, k, A_DVE)
                if is_chunk(n - 4):
                    hidden_stats(1)
                    yield

            def l0_second(m):
                for c in (2 * m - 4, 2 * m - 3):
                    if is_chunk(c):
                        i, k = divmod(c, NK)
                        dve.wait_ge(act_done[k], B_ACT.at(i, "y"))
                        v.bn_stats(ST2[:, c, :], Y2[:, c * CH:(c + 1) * CH]).then_inc(dve_done[k], 1)
                        yield

            def b1(n, m=1):
                return bnv[:, n:n + m]

            nb = [0]

            def bstep(ins):
                nb[0] += 1
                ins.then_inc(bn_ops, 1)
                dve.wait_ge(bn_ops, nb[0])

            def bn_scales(st, groups, g, be, at, ready):
                for c in range(groups):
                    bstep(v.bn_aggr(b1(at + 2 * c, 2), st(c)))
                means, var = bnv[:, at:at + 2 * groups:2], bnv[:, at + 1:at + 2 * groups:2]
                scale, shft = b1(at + 2 * groups, groups), b1(at + 3 * groups, groups)
                x, y, a = (lnv[:, q, 0:groups] for q in range(3))
                bstep(v.tensor_scalar(x, var, EPS, None, ALU.add))
                for f in inverse_root(x, y, bstep, lambda: None):
                    bstep(v.tensor_tensor(a, y, y, ALU.mult))
                    bstep(v.tensor_tensor(a, a, x, ALU.mult))
                    bstep(v.scalar_tensor_tensor(y, a, -f, y, ALU.add, ALU.mult))
                bstep(v.scalar_tensor_tensor(scale, y, -1.0 / 8192, g, ALU.mult, ALU.mult))
                bstep(v.tensor_tensor(shft, means, scale, ALU.mult))
                bstep(v.tensor_tensor(shft, be, shft, ALU.subtract))
                v.sem_inc(ready, 1)

            for r in range(REFLECTED):
                n = r - LEAD
                if n == 0:
                    dve.wait_ge(ld_x, 16)
                if n == 2:
                    dve.wait_ge(ld_w, 16)
                    step(v.tensor_scalar(RB0[:, :], W("bg0row"), c1(0), None, ALU.mult))
                    step(v.tensor_scalar(RB1[:, :], PS[:, 1, 0:P], W("bg1"), None, ALU.mult))
                    step(v.tensor_tensor(lbias[:, :], W("bih"), W("bhh"), ALU.add), "biases")
                if n == L0_FIRST:
                    dve.wait_ge(hidden_seen, 2 * NCHUNK)
                    bn_scales(lambda c: ST1[:, c, :, :].rearrange("p n s -> p (n s)"), 2, W("g1"), W("be1"), 0, bn1_ready)
                beside = iter(()) if n < 0 else l0_first(n) if n < L0_FIRST else l0_second(n - L0_FIRST)
                reflection(r, True, beside)
                for _ in beside:
                    pass
            bn_scales(lambda c: ST2[:, :, :].rearrange("p n s -> p (n s)"), 1, W("g2"), W("be2"), 10, bn2_ready)

            four = [P, TPC, P]

            def by_tile(ap):
                return ap.rearrange("p (t n) -> p t n", t=TPC)

            def add_to_state(k, i, before):
                dve.wait_ge(pe_done[k], before)
                v.tensor_tensor(X[:, chunk_cols(i, k)], X[:, chunk_cols(i, k)], bank(k), ALU.add)\
                    .then_inc(dve_done[k], 1)

            def l1_instructions():
                def add_turned(i, k, name, src):
                    add(i, k, src, C_PE.at(i, name))
                    dclock[0] += 0.6

                for i in range(ITER):
                    if i == 0:
                        for k in range(NK):
                            yield there[0, k, "turn"]
                            add_turned(0, k, "turn", turn_bank(0, k))
                        yield from layer_norms(0, [there[0, NK - 1, "turn"]])
                    for name, product, bias in (("bias0", "g0", RB0), ("bias1", "g1", RB1)):
                        for k in range(NK):
                            yield there[i, k, product]
                            dve.wait_ge(pe_done[k], C_PE.at(i, product))
                            v.tensor_tensor(by_tile(T1[:, k, CH:2 * CH]), by_tile(l1_bank(k)),
                                            bias[:, :].unsqueeze(1).broadcast_to(four), ALU.add).then_inc(dve_done[k], 1)
                            dclock[0] += 0.6
                    if i + 1 < ITER:
                        for k in range(NK):
                            yield there[i + 1, k, "turn"]
                            add_turned(i + 1, k, "turn", turn_bank(i + 1, k))
                        yield from layer_norms(i + 1, [there[i + 1, NK - 1, "turn"]])
                    for k in range(NK):
                        yield there[i, k, "turn_h"]
                        add_turned(i, k, "turn_h", l1_bank(k))

            def add(i, k, src, before):
                dve.wait_ge(pe_done[k], before)
                x = X[:, i * SG + k * CH:i * SG + (k + 1) * CH]
                v.tensor_tensor(x, x, src, ALU.add).then_inc(dve_done[k], 1)

            l1[0] = l1_instructions()
            l1_next[0] = next(l1[0])
            for k in range(REFLECTED, REFLECTIONS):
                reflection(k, False)
            tail()
            assert taken[0] == len(sent)
            for _ in l1[0]:
                pass

            for k in range(NK):
                dve.wait_ge(dve_done[k], C_DVE.end)
                for _ in stats_of(0, k, D_DVE, ""):
                    pass
            for k in range(NK):
                shift_of(0, k, D_POOL, "")
            for i in range(ITER):
                for k in range(NK):
                    dve.wait_ge(pe_done[k], D_PE.at(i, "w2"))
                    v.tensor_tensor(by_tile(T1[:, k, 0:CH]), by_tile(bank(k)),
                                    W("l2b2row").unsqueeze(1).broadcast_to(four), ALU.add).then_inc(dve_done[k], 1)
                for k in range(NK):
                    add(i, k, bank(k), D_PE.at(i, "back"))
                    dve.wait_ge(dve_done[k], D_DVE.at(i, "add"))
                    for _ in stats_of(i, k, D_DVE, "3"):
                        pass
                    if k:
                        shift_of(i, k - 1, D_POOL, "3")
                shift_of(i, NK - 1, D_POOL, "3")
                if i:
                    for k in range(NK):
                        add(i - 1, k, banks(k)[:, 1, :], D_PE.at(i - 1, "mix3"))
                if i + 1 < ITER:
                    for k in range(NK):
                        dve.wait_ge(act_done[k], D_ACT.at(i, "norm3"))
                        for _ in stats_of(i + 1, k, D_DVE, ""):
                            pass
                    for k in range(NK):
                        shift_of(i + 1, k, D_POOL, "")
            for k in range(NK):
                add(ITER - 1, k, banks(k)[:, 1, :], D_PE.at(ITER - 1, "mix3"))


PREP = {"BDA": 1, "BDAT": 2, "hat_rows": 11, "lap_rows": 18, "S": 23, "biases": 26, "diagonals": 29, "bound": 42,
        "V": 96, "VT": 98, "U": 100, "AU": 103, "ritz": 108, "I+E": 121, "all": 127}


def kernel(x, adj, **w):
    import concourse.bacc as bacc
    from concourse.bass_utils import run_bass_kernel_spmd

    f = {k: np.asarray(a) for k, a in w.items()}

    def cols(a):
        return np.ascontiguousarray(a.reshape(-1, P).T)

    def kchunks(a):
        return np.ascontiguousarray(a.reshape(-1, P, a.shape[1]).transpose(1, 0, 2).reshape(P, -1))

    def gate_major(a):
        return np.ascontiguousarray(a.transpose(2, 0, 1).reshape(P, -1))

    parts = {
        "w1T": f["L0_gnn_W1"].T, "w2T": kchunks(np.ascontiguousarray(f["L0_gnn_W2"].T)),
        "wg0": f["L1_gnn_Wg0"], "wg1": f["L1_gnn_Wg1"],
        "wihT": gate_major(f["L1_gnn_Wih"]), "whhT": gate_major(f["L1_gnn_Whh"]),
        "l2w1": f["L2_gnn_W1"], "l2w2": f["L2_gnn_W2"],
        "l3w1": f["L3_gnn_W1"], "l3w2": kchunks(f["L3_gnn_W2"]), "l3w3": kchunks(f["L3_gnn_W3"]),
        "b1": cols(f["L0_gnn_b1"]), "g1": cols(f["L0_gnn_g1"]), "be1": cols(f["L0_gnn_be1"]),
        "b2": cols(f["L0_gnn_b2"]), "g2": cols(f["L0_gnn_g2"]), "be2": cols(f["L0_gnn_be2"]),
        "bg1": cols(f["L1_gnn_bg1"]), "bih": cols(f["L1_gnn_bih"].reshape(-1)),
        "bhh": cols(f["L1_gnn_bhh"].reshape(-1)), "l2b1": cols(f["L2_gnn_b1"]),
        "bg0row": np.broadcast_to(f["L1_gnn_bg0"][None, :], (P, P)),
        "l2b2row": np.broadcast_to(f["L2_gnn_b2"][None, :], (P, P)),
    }
    arrays = {
        "x_in": np.ascontiguousarray(np.asarray(x).reshape(TILES, P, D).transpose(1, 0, 2).reshape(P, TILES * D)),
        "cst_in": np.ascontiguousarray(np.concatenate(list(constants().values()), axis=1)),
        "w_in": np.ascontiguousarray(np.concatenate([parts[k] for k in WEIGHT_W], axis=1)),
        "adj_in": np.ascontiguousarray(np.asarray(adj)),
    }
    nc = bacc.Bacc("TRN2", target_bir_lowering=False, num_devices=1)
    args = [nc.dram_tensor(n, a.shape, F32, kind="ExternalInput").ap() for n, a in arrays.items()]
    args.append(nc.dram_tensor("out", (P, TILES * D), F32, kind="ExternalOutput").ap())
    build(nc, *args)
    r = run_bass_kernel_spmd(nc, [arrays], core_ids=[0])
    got = r.results[0]["out"]
    return np.ascontiguousarray(got.reshape(P, TILES, D).transpose(1, 0, 2)).reshape(GRAPHS, NODES, D)
```
